# Optimizing a Trainium2 kernel written in Bass

```python
import numpy as np
import jax
import jax.numpy as jnp

def _softmax(x, axis=-1):
    return jax.nn.softmax(x, axis=axis)

def _gelu(x):
    return jax.nn.gelu(x, approximate=True)

def _silu(x):
    return jax.nn.silu(x)

def _sigmoid(x):
    return jax.nn.sigmoid(x)

def _layernorm(x, axis=-1, eps=1e-05):
    m = jnp.mean(x, axis=axis, keepdims=True)
    v = jnp.var(x, axis=axis, keepdims=True)
    return (x - m) / jnp.sqrt(v + eps)

def _scatter_add(tgt, idx, src, axis=0):
    return tgt.at[idx].add(src)

def _segment_sum(src, seg, n):
    return jax.ops.segment_sum(src, seg, n)
kernel_name = 'mk_xattn_ffn_d2_seqx_r8_04614a'

def setup_inputs(seed: int=0):
    np.random.seed(seed)
    _w = jnp.asarray

    def _rec_inputs():
        import jax
        import jax.numpy as jnp
        _rk = jax.random.key(seed)
        x = -0.0002928 + 1 * jax.random.normal(jax.random.fold_in(_rk, 1), (32, 56, 256), jnp.float32)
        _lenS = 56 - jax.random.randint(jax.random.fold_in(_rk, 7), (32,), 0, max(1, 56 // 4) + 1, jnp.int32)
        _lenS2 = 1500 - jax.random.randint(jax.random.fold_in(_rk, 8), (32,), 0, max(1, 1500 // 4) + 1, jnp.int32)
        _ctx_512P = jax.random.normal(jax.random.fold_in(_rk, 11), (32, 16, 64), jnp.float32)
        _ctx_512c = jax.random.dirichlet(jax.random.fold_in(_rk, 511), 0.3 * jnp.ones((16,), jnp.float32), (32, 1500))
        _ctx_512t = jnp.einsum('bsk,bkd->bsd', _ctx_512c, _ctx_512P)
        _ctx_512t = _ctx_512t * jax.lax.rsqrt(jnp.mean(jnp.square(_ctx_512t)) + 1e-12) * 0.953939
        ctx_512 = 0.000227908 + 0.99994 * (_ctx_512t + 0.3 * jax.random.normal(jax.random.fold_in(_rk, 611), (32, 1500, 64), jnp.float32))
        return (x, ctx_512)
    x, ctx_512 = _rec_inputs()

    def _L0_xattn_setup():
        import jax, jax.numpy as jnp
        import numpy as np
        B, S, L = (2, 128, 128)
        DIM_Q, H, K, D_C, D_CQ, R = (256, 16, 128, 64, 192, 64)

        def _rope_tables(length, dim):
            inv = 1.0 / 10000.0 ** (jnp.arange(0, dim, 2, dtype=jnp.float32) / dim)
            f = jnp.arange(length, dtype=jnp.float32)[:, None] * inv[None, :]
            sin = jnp.repeat(jnp.sin(f), 2, axis=-1)
            cos = jnp.repeat(jnp.cos(f), 2, axis=-1)
            return (sin, cos)

        def _rotate_half(x):
            half = x.shape[-1] // 2
            return jnp.concatenate([-x[..., half:], x[..., :half]], axis=-1)

        def _apply_rope(x, sin, cos):
            return x * cos + _rotate_half(x) * sin
        key = jax.random.key(seed)
        ks = jax.random.split(key, 8)
        return {'hidden_q': jax.random.normal(ks[0], (B, S, DIM_Q), jnp.float32), 'kv_c': jax.random.normal(ks[1], (B, L, D_C), jnp.float32), 'Wq': jax.random.normal(ks[2], (H * K, DIM_Q), jnp.float32) / np.sqrt(DIM_Q).astype(np.float32), 'w_kc_q': jax.random.normal(ks[3], (H, K, D_CQ), jnp.float32) / np.sqrt(K).astype(np.float32), 'w_kc_kv': jax.random.normal(ks[4], (H, K, D_C), jnp.float32) / np.sqrt(K).astype(np.float32), 'W_qr': jax.random.normal(ks[5], (H, D_CQ, R), jnp.float32) / np.float32(np.sqrt(D_CQ) * np.sqrt(R)), 'W_kr': jax.random.normal(ks[6], (H, D_C, R), jnp.float32) / np.sqrt(D_C).astype(np.float32), 'Wo': jax.random.normal(ks[7], (DIM_Q, H * K), jnp.float32) / np.sqrt(H * K).astype(np.float32)}
    _L0_xattn_all = _L0_xattn_setup()
    _L0_xattn_in = {k: v for k, v in _L0_xattn_all.items() if k in ('Wq', 'w_kc_q', 'w_kc_kv', 'W_qr', 'W_kr', 'Wo')}
    del _L0_xattn_all

    def _L0_ffn_setup():
        import jax, jax.numpy as jnp
        import numpy as np
        NUM_EXPERTS = 16
        TOP_K = 4
        N_GROUP = 4
        TOPK_GROUP = 2
        SCALING = 2.5

        def _route(x, gate_weight, expert_bias):
            logits = x @ gate_weight.T
            scores = jax.nn.sigmoid(logits)
            biased = scores + expert_bias[None, :]
            T = x.shape[0]
            gsz = NUM_EXPERTS // N_GROUP
            grp = biased.reshape(T, N_GROUP, gsz)
            top2, _ = jax.lax.top_k(grp, 2)
            group_scores = top2.sum(-1)
            _, gidx = jax.lax.top_k(group_scores, TOPK_GROUP)
            gmask = jax.nn.one_hot(gidx, N_GROUP, dtype=scores.dtype).sum(1)
            emask = jnp.repeat(gmask, gsz, axis=1)
            masked = jnp.where(emask > 0, biased, -jnp.inf)
            _, sel = jax.lax.top_k(masked, TOP_K)
            w = jnp.take_along_axis(scores, sel, axis=1)
            w = w / (w.sum(-1, keepdims=True) + 1e-20)
            return (w * SCALING, sel)

        def _moe(x, w, sel, gate_proj, up_proj, down_proj):
            cw = (jax.nn.one_hot(sel, NUM_EXPERTS, dtype=x.dtype) * w[..., None]).sum(1)

            def body(acc, inp):
                g, u, d, we = inp
                y = jax.nn.silu(x @ g.T) * (x @ u.T) @ d.T
                return (acc + we[:, None] * y, None)
            out, _ = jax.lax.scan(body, jnp.zeros_like(x), (gate_proj, up_proj, down_proj, cw.T))
            return out
        key = jax.random.key(seed)
        ks = jax.random.split(key, 9)
        B, S, H, I = (2, 128, 256, 128)
        w = lambda k, shape: jax.random.normal(k, shape, jnp.float32) * 0.02
        return {'hidden_states': jax.random.normal(ks[0], (B, S, H), jnp.float32), 'gate_weight': w(ks[1], (NUM_EXPERTS, H)), 'expert_bias': jnp.zeros((NUM_EXPERTS,), jnp.float32), 'gate_proj': w(ks[2], (NUM_EXPERTS, I, H)), 'up_proj': w(ks[3], (NUM_EXPERTS, I, H)), 'down_proj': w(ks[4], (NUM_EXPERTS, H, I)), 'shared_gate': w(ks[5], (I, H)), 'shared_up': w(ks[6], (I, H)), 'shared_down': w(ks[7], (H, I))}
    _L0_ffn_all = _L0_ffn_setup()
    _L0_ffn_in = {k: v for k, v in _L0_ffn_all.items() if k in ('gate_weight', 'expert_bias', 'gate_proj', 'up_proj', 'down_proj', 'shared_gate', 'shared_up', 'shared_down')}
    del _L0_ffn_all

    def _L1_xattn_setup():
        import jax, jax.numpy as jnp
        import numpy as np
        B, S, L = (2, 128, 128)
        DIM_Q, H, K, D_C, D_CQ, R = (256, 16, 128, 64, 192, 64)

        def _rope_tables(seq_len, dim, dtype):
            inv_freq = 1.0 / 10000.0 ** (jnp.arange(0, dim, 2, dtype=dtype) / dim)
            t = jnp.arange(seq_len, dtype=dtype)
            freqs = t[:, None] * inv_freq[None, :]
            sin = jnp.repeat(jnp.sin(freqs), 2, axis=-1)
            cos = jnp.repeat(jnp.cos(freqs), 2, axis=-1)
            return (sin, cos)

        def _rotate_half(x):
            h = x.shape[-1] // 2
            return jnp.concatenate([-x[..., h:], x[..., :h]], axis=-1)
        key = jax.random.key(seed)
        ks = jax.random.split(key, 8)
        s_in = 1.0 / np.sqrt(DIM_Q)
        s_k = 1.0 / np.sqrt(K)
        s_cq = 1.0 / np.sqrt(D_CQ)
        s_c = 1.0 / np.sqrt(D_C)
        return {'hidden_q': jax.random.normal(ks[0], (B, S, DIM_Q), jnp.float32), 'kv_c': jax.random.normal(ks[1], (B, L, D_C), jnp.float32), 'Wq': jax.random.normal(ks[2], (H * K, DIM_Q), jnp.float32) * s_in, 'w_kc_q': jax.random.normal(ks[3], (H, K, D_CQ), jnp.float32) * s_k, 'w_kc_kv': jax.random.normal(ks[4], (H, K, D_C), jnp.float32) * s_k, 'W_qr': jax.random.normal(ks[5], (H, D_CQ, R), jnp.float32) * s_cq / np.sqrt(R), 'W_kr': jax.random.normal(ks[6], (H, D_C, R), jnp.float32) * s_c, 'Wo': jax.random.normal(ks[7], (DIM_Q, H * K), jnp.float32) * s_k}
    _L1_xattn_all = _L1_xattn_setup()
    _L1_xattn_in = {k: v for k, v in _L1_xattn_all.items() if k in ('Wq', 'w_kc_q', 'w_kc_kv', 'W_qr', 'W_kr', 'Wo')}
    del _L1_xattn_all

    def _L1_ffn_setup():
        import jax, jax.numpy as jnp
        import numpy as np
        NUM_EXPERTS = 8
        TOP_K = 2
        LORA_ALPHA = 2.0
        LORA_RANK = 16
        D_MODEL = 256
        D_HIDDEN = 704
        key = jax.random.key(seed)
        ks = jax.random.split(key, 11)
        B, S, D, H, E, R = (2, 128, D_MODEL, D_HIDDEN, NUM_EXPERTS, LORA_RANK)
        sd = 1.0 / np.sqrt(D)
        sh = 1.0 / np.sqrt(H)
        x = jax.random.normal(ks[0], (B, S, D), jnp.float32)
        gate_w = jax.random.normal(ks[1], (E, D), jnp.float32) * sd
        w_up = jax.random.normal(ks[2], (H, D), jnp.float32) * sd
        w_gate = jax.random.normal(ks[3], (H, D), jnp.float32) * sd
        w_down = jax.random.normal(ks[4], (D, H), jnp.float32) * sh
        up_A = jax.random.normal(ks[5], (E, R, D), jnp.float32) * sd
        up_B = jax.random.normal(ks[6], (E, H, R), jnp.float32) * 0.02
        gate_A = jax.random.normal(ks[7], (E, R, D), jnp.float32) * sd
        gate_B = jax.random.normal(ks[8], (E, H, R), jnp.float32) * 0.02
        down_A = jax.random.normal(ks[9], (E, R, H), jnp.float32) * sh
        down_B = jax.random.normal(ks[10], (E, D, R), jnp.float32) * 0.02
        return {'x': x, 'gate_w': gate_w, 'w_up': w_up, 'w_gate': w_gate, 'w_down': w_down, 'up_A': up_A, 'up_B': up_B, 'gate_A': gate_A, 'gate_B': gate_B, 'down_A': down_A, 'down_B': down_B}
    _L1_ffn_all = _L1_ffn_setup()
    _L1_ffn_in = {k: v for k, v in _L1_ffn_all.items() if k in ('gate_w', 'w_up', 'w_gate', 'w_down', 'up_A', 'up_B', 'gate_A', 'gate_B', 'down_A', 'down_B')}
    del _L1_ffn_all
    return {'x': x, 'ctx_512': ctx_512, 'L0_xattn_Wq': _L0_xattn_in['Wq'], 'L0_xattn_w_kc_q': _L0_xattn_in['w_kc_q'], 'L0_xattn_w_kc_kv': _L0_xattn_in['w_kc_kv'], 'L0_xattn_W_qr': _L0_xattn_in['W_qr'], 'L0_xattn_W_kr': _L0_xattn_in['W_kr'], 'L0_xattn_Wo': _L0_xattn_in['Wo'], 'L0_ffn_gate_weight': _L0_ffn_in['gate_weight'], 'L0_ffn_expert_bias': _L0_ffn_in['expert_bias'], 'L0_ffn_gate_proj': _L0_ffn_in['gate_proj'], 'L0_ffn_up_proj': _L0_ffn_in['up_proj'], 'L0_ffn_down_proj': _L0_ffn_in['down_proj'], 'L0_ffn_shared_gate': _L0_ffn_in['shared_gate'], 'L0_ffn_shared_up': _L0_ffn_in['shared_up'], 'L0_ffn_shared_down': _L0_ffn_in['shared_down'], 'L1_xattn_Wq': _L1_xattn_in['Wq'], 'L1_xattn_w_kc_q': _L1_xattn_in['w_kc_q'], 'L1_xattn_w_kc_kv': _L1_xattn_in['w_kc_kv'], 'L1_xattn_W_qr': _L1_xattn_in['W_qr'], 'L1_xattn_W_kr': _L1_xattn_in['W_kr'], 'L1_xattn_Wo': _L1_xattn_in['Wo'], 'L1_ffn_gate_w': _L1_ffn_in['gate_w'], 'L1_ffn_w_up': _L1_ffn_in['w_up'], 'L1_ffn_w_gate': _L1_ffn_in['w_gate'], 'L1_ffn_w_down': _L1_ffn_in['w_down'], 'L1_ffn_up_A': _L1_ffn_in['up_A'], 'L1_ffn_up_B': _L1_ffn_in['up_B'], 'L1_ffn_gate_A': _L1_ffn_in['gate_A'], 'L1_ffn_gate_B': _L1_ffn_in['gate_B'], 'L1_ffn_down_A': _L1_ffn_in['down_A'], 'L1_ffn_down_B': _L1_ffn_in['down_B']}

def reference(x, ctx_512, L0_xattn_Wq, L0_xattn_w_kc_q, L0_xattn_w_kc_kv, L0_xattn_W_qr, L0_xattn_W_kr, L0_xattn_Wo, L0_ffn_gate_weight, L0_ffn_expert_bias, L0_ffn_gate_proj, L0_ffn_up_proj, L0_ffn_down_proj, L0_ffn_shared_gate, L0_ffn_shared_up, L0_ffn_shared_down, L1_xattn_Wq, L1_xattn_w_kc_q, L1_xattn_w_kc_kv, L1_xattn_W_qr, L1_xattn_W_kr, L1_xattn_Wo, L1_ffn_gate_w, L1_ffn_w_up, L1_ffn_w_gate, L1_ffn_w_down, L1_ffn_up_A, L1_ffn_up_B, L1_ffn_gate_A, L1_ffn_gate_B, L1_ffn_down_A, L1_ffn_down_B):
    import jax
    import jax.numpy as jnp

    def _L0_xattn_ref(hidden_q, kv_c, Wq, w_kc_q, w_kc_kv, W_qr, W_kr, Wo):
        import jax, jax.numpy as jnp
        import numpy as np
        B, S, L = (2, 128, 128)
        DIM_Q, H, K, D_C, D_CQ, R = (256, 16, 128, 64, 192, 64)

        def _rope_tables(length, dim):
            inv = 1.0 / 10000.0 ** (jnp.arange(0, dim, 2, dtype=jnp.float32) / dim)
            f = jnp.arange(length, dtype=jnp.float32)[:, None] * inv[None, :]
            sin = jnp.repeat(jnp.sin(f), 2, axis=-1)
            cos = jnp.repeat(jnp.cos(f), 2, axis=-1)
            return (sin, cos)

        def _rotate_half(x):
            half = x.shape[-1] // 2
            return jnp.concatenate([-x[..., half:], x[..., :half]], axis=-1)

        def _apply_rope(x, sin, cos):
            return x * cos + _rotate_half(x) * sin
        Bv, Sv, _ = hidden_q.shape
        _, Lv, _ = kv_c.shape
        q_hk = (hidden_q @ Wq.T).reshape(Bv, Sv, H, K)
        q_big = jnp.einsum('bshk,hkq->bshq', q_hk, w_kc_q)
        sin_q, cos_q = _rope_tables(Sv, D_CQ)
        q_big = _apply_rope(q_big, sin_q[None, :, None, :], cos_q[None, :, None, :])
        sin_k, cos_k = _rope_tables(Lv, D_C)
        kv_r = _apply_rope(kv_c, sin_k[None], cos_k[None])
        q_r = jnp.einsum('bshq,hqr->bhsr', q_big, W_qr)
        k_r = jnp.einsum('bld,hdr->bhlr', kv_r, W_kr)
        scores = jnp.einsum('bhsr,bhlr->bhsl', q_r, k_r)
        attn = jax.nn.softmax(scores, axis=-1)
        ctx_c = jnp.einsum('bhsl,bld->bhsd', attn, kv_r)
        ctx_lat = jnp.einsum('bhsd,hkd->bhsk', ctx_c, w_kc_kv)
        ctx = ctx_lat.transpose(0, 2, 1, 3).reshape(Bv, Sv, H * K)
        return ctx @ Wo.T

    def _L0_ffn_ref(hidden_states, gate_weight, expert_bias, gate_proj, up_proj, down_proj, shared_gate, shared_up, shared_down):
        import jax, jax.numpy as jnp
        import numpy as np
        NUM_EXPERTS = 16
        TOP_K = 4
        N_GROUP = 4
        TOPK_GROUP = 2
        SCALING = 2.5

        def _route(x, gate_weight, expert_bias):
            logits = x @ gate_weight.T
            scores = jax.nn.sigmoid(logits)
            biased = scores + expert_bias[None, :]
            T = x.shape[0]
            gsz = NUM_EXPERTS // N_GROUP
            grp = biased.reshape(T, N_GROUP, gsz)
            top2, _ = jax.lax.top_k(grp, 2)
            group_scores = top2.sum(-1)
            _, gidx = jax.lax.top_k(group_scores, TOPK_GROUP)
            gmask = jax.nn.one_hot(gidx, N_GROUP, dtype=scores.dtype).sum(1)
            emask = jnp.repeat(gmask, gsz, axis=1)
            masked = jnp.where(emask > 0, biased, -jnp.inf)
            _, sel = jax.lax.top_k(masked, TOP_K)
            w = jnp.take_along_axis(scores, sel, axis=1)
            w = w / (w.sum(-1, keepdims=True) + 1e-20)
            return (w * SCALING, sel)

        def _moe(x, w, sel, gate_proj, up_proj, down_proj):
            cw = (jax.nn.one_hot(sel, NUM_EXPERTS, dtype=x.dtype) * w[..., None]).sum(1)

            def body(acc, inp):
                g, u, d, we = inp
                y = jax.nn.silu(x @ g.T) * (x @ u.T) @ d.T
                return (acc + we[:, None] * y, None)
            out, _ = jax.lax.scan(body, jnp.zeros_like(x), (gate_proj, up_proj, down_proj, cw.T))
            return out
        B, S, H = hidden_states.shape
        x = hidden_states.reshape(-1, H)
        w, sel = _route(x, gate_weight, expert_bias)
        out = _moe(x, w, sel, gate_proj, up_proj, down_proj)
        shared = jax.nn.silu(x @ shared_gate.T) * (x @ shared_up.T) @ shared_down.T
        return (out + shared).reshape(B, S, H)

    def _L1_xattn_ref(hidden_q, kv_c, Wq, w_kc_q, w_kc_kv, W_qr, W_kr, Wo):
        import jax, jax.numpy as jnp
        import numpy as np
        B, S, L = (2, 128, 128)
        DIM_Q, H, K, D_C, D_CQ, R = (256, 16, 128, 64, 192, 64)

        def _rope_tables(seq_len, dim, dtype):
            inv_freq = 1.0 / 10000.0 ** (jnp.arange(0, dim, 2, dtype=dtype) / dim)
            t = jnp.arange(seq_len, dtype=dtype)
            freqs = t[:, None] * inv_freq[None, :]
            sin = jnp.repeat(jnp.sin(freqs), 2, axis=-1)
            cos = jnp.repeat(jnp.cos(freqs), 2, axis=-1)
            return (sin, cos)

        def _rotate_half(x):
            h = x.shape[-1] // 2
            return jnp.concatenate([-x[..., h:], x[..., :h]], axis=-1)
        b, s, _ = hidden_q.shape
        l = kv_c.shape[1]
        q_hk = (hidden_q @ Wq.T).reshape(b, s, H, K)
        q_big = jnp.einsum('bshk,hkq->bshq', q_hk, w_kc_q)
        sin, cos = _rope_tables(l, D_C, kv_c.dtype)
        kv_rope = kv_c * cos[None] + _rotate_half(kv_c) * sin[None]
        q_r = jnp.einsum('bshq,hqr->bhsr', q_big, W_qr)
        k_r = jnp.einsum('bld,hdr->bhlr', kv_rope, W_kr)
        scores = jnp.einsum('bhsr,bhlr->bhsl', q_r, k_r)
        attn = jax.nn.softmax(scores, axis=-1)
        ctx_c = jnp.einsum('bhsl,bld->bhsd', attn, kv_rope)
        ctx_lat = jnp.einsum('bhsd,hkd->bshk', ctx_c, w_kc_kv)
        out = ctx_lat.reshape(b, s, H * K) @ Wo.T
        return out

    def _L1_ffn_ref(x, gate_w, w_up, w_gate, w_down, up_A, up_B, gate_A, gate_B, down_A, down_B):
        import jax, jax.numpy as jnp
        import numpy as np
        NUM_EXPERTS = 8
        TOP_K = 2
        LORA_ALPHA = 2.0
        LORA_RANK = 16
        D_MODEL = 256
        D_HIDDEN = 704
        B, S, D = x.shape
        H = w_up.shape[0]
        gate_logits = jnp.einsum('bsd,ed->bse', x, gate_w)
        topw, sel = jax.lax.top_k(gate_logits, TOP_K)
        topw = jax.nn.softmax(topw.astype(jnp.float32), axis=1).astype(x.dtype)
        xt = x.reshape(-1, D)
        wf = topw.reshape(-1, TOP_K)
        sf = sel.reshape(-1, TOP_K)
        base_up = xt @ w_up.T
        base_gate = xt @ w_gate.T
        mixed_h = jnp.zeros((xt.shape[0], H), x.dtype)
        lora_down = jnp.zeros_like(xt)
        for e in range(NUM_EXPERTS):
            c = jnp.sum(jnp.where(sf == e, wf, 0.0), axis=1)
            lo_up = LORA_ALPHA * (xt @ up_A[e].T @ up_B[e].T)
            lo_gate = LORA_ALPHA * (xt @ gate_A[e].T @ gate_B[e].T)
            h_e = jax.nn.silu(base_up + lo_up) * (base_gate + lo_gate)
            ch = c[:, None] * h_e
            mixed_h = mixed_h + ch
            lora_down = lora_down + LORA_ALPHA * (ch @ down_A[e].T @ down_B[e].T)
        out = mixed_h @ w_down.T + lora_down
        return out.reshape(B, S, D)
    x = x + _L0_xattn_ref(_layernorm(x, axis=-1), ctx_512, L0_xattn_Wq, L0_xattn_w_kc_q, L0_xattn_w_kc_kv, L0_xattn_W_qr, L0_xattn_W_kr, L0_xattn_Wo)
    x = x + _L0_ffn_ref(_layernorm(x, axis=-1), L0_ffn_gate_weight, L0_ffn_expert_bias, L0_ffn_gate_proj, L0_ffn_up_proj, L0_ffn_down_proj, L0_ffn_shared_gate, L0_ffn_shared_up, L0_ffn_shared_down)
    x = x + _L1_xattn_ref(_layernorm(x, axis=-1), ctx_512, L1_xattn_Wq, L1_xattn_w_kc_q, L1_xattn_w_kc_kv, L1_xattn_W_qr, L1_xattn_W_kr, L1_xattn_Wo)
    x = x + _L1_ffn_ref(_layernorm(x, axis=-1), L1_ffn_gate_w, L1_ffn_w_up, L1_ffn_w_gate, L1_ffn_w_down, L1_ffn_up_A, L1_ffn_up_B, L1_ffn_gate_A, L1_ffn_gate_B, L1_ffn_down_A, L1_ffn_down_B)
    return x

_drawn_inputs = setup_inputs


def setup_inputs(seed=0):
    import zlib

    import numpy as np

    out = dict(_drawn_inputs(seed))
    spreads = {'L0_ffn_expert_bias': (0.0, 0.697)}
    factors = {'L0_ffn_gate_weight': 7.529,
     'L0_ffn_gate_proj': 5.053,
     'L0_ffn_up_proj': 5.001,
     'L0_ffn_down_proj': 4.992,
     'L0_ffn_shared_gate': 6.44,
     'L0_ffn_shared_up': 6.327,
     'L0_ffn_shared_down': 6.304,
     'L1_ffn_gate_w': 6.953,
     'L1_ffn_w_up': 3.674,
     'L1_ffn_w_gate': 3.401,
     'L1_ffn_w_down': 3.418,
     'L1_ffn_up_A': 8.0,
     'L1_ffn_up_B': 8.0,
     'L1_ffn_gate_A': 8.0,
     'L1_ffn_gate_B': 8.0,
     'L1_ffn_down_A': 8.0,
     'L1_ffn_down_B': 8.0}
    for name, (base, spread) in spreads.items():
        noise = np.random.default_rng([zlib.crc32(name.encode()), seed]).standard_normal(out[name].shape)
        drawn = base * np.exp(spread * noise) if base else spread * noise
        out[name] = jnp.asarray(drawn.astype(out[name].dtype))
    for name, factor in factors.items():
        out[name] = (out[name] * factor).astype(out[name].dtype)
    return out
```

```python
from contextlib import ExitStack

import concourse.bass as bass
import numpy as np
from concourse import mybir

ALU = mybir.AluOpType
ACT = mybir.ActivationFunctionType
AX = mybir.AxisListType
F32 = mybir.dt.float32
F32R = mybir.dt.float32r

B, S, L, D = 32, 56, 1500, 256
H, HK, DC, DCQ, DR = 16, 128, 64, 192, 64
BG = 4
G = B // BG
NT = BG * S
NQ = H * S
HQ = NQ // 2
LT, LP = 12, 125
LB = L // 3
KT = D // 128
HALF = DCQ // 2
NMAX = NQ // 128
NPROB = 4
POOL_TILES = 8
KSP = L // LP
E0, TOP0, GRP0 = 16, 4, 4
E1, RANK = 8, 16
I0 = 128
HID = 704
MT = -(-HID // 128)
TR = NT // 2
NEG = -3.0e38
EPS = 1e-5
WSLOT = 4


def head_rows(t):
    return (128 * t + 127) // S


def schedule(layer):
    steps = []
    spin = [0]

    def add(kind, *key, region=None):
        steps.append((kind, key, region))

    def turn():
        spin[0] += 1
        return 3 + (spin[0] - 1) % 3

    def keys(j):
        for c in range(3):
            add("keyT", j, c, region=turn())

    def maxima(j, tiles):
        for t in tiles:
            for c in range(3):
                add("smax", j, t, c, region=turn())

    add("rope", 0)
    add("mean", 0, region=2)
    add("var", 0, region=5)
    add("rope", 1)
    spin[0] = 0
    keys(0)
    done = 0
    ahead = 2
    for h in range(H + ahead):
        if layer == 0:
            if h < H:
                add("qwide", h, region=h % 2)
            if 1 <= h <= H:
                add("query", h - 1, region=2)
        elif h < H:
            add("query", h, region=h % 3)
        while done < NMAX and head_rows(done) <= h - ahead:
            maxima(0, [done])
            done += 1
    maxima(0, range(done, NMAX))
    add("maxT", 0, region=turn())
    last = None
    for j in range(BG):
        for t in range(LT):
            add("score", j, t, region=t % 2)
            if last is not None:
                add("mix", *last)
                if last[1] == LT - 1:
                    add("context", last[0])
            last = (j, t)
            if j + 1 < BG:
                if t == 0:
                    keys(j + 1)
                if 1 <= t <= NMAX:
                    maxima(j + 1, [t - 1])
                if t == NMAX + 1:
                    add("maxT", j + 1, region=turn())
            if t == 3 and j:
                add("norm", j - 1, region=turn())
            if t == 9 and j + 2 < BG:
                add("rope", j + 2)
    add("mix", *last)
    add("context", BG - 1)
    add("norm", BG - 1, region=turn())
    add("attn", region=0)
    add("mean", 1, region=2)
    add("var", 1, region=5)
    add("route", region=1)
    if layer == 0:
        order = list(range(E0 + 1))
        for i in order:
            add("gateup", i, region=i % 2)
            if i:
                add("down", i - 1)
            if i:
                add("weight", i, region=3 + i % 2)
        add("down", E0)
    else:
        add("lora", region=5)
        add("tokw", region=3)
        add("mask", region=4)
        for m in range(MT):
            add("gateup", m, region=m % 2)
            if m:
                add("down", m - 1)
        add("down", MT - 1)
        add("loradown")
    add("out")
    return steps


class Regions:

    def __init__(self, steps, filled, drained):
        self.full, self.empty, self.at, self.before = filled, drained, {}, {}
        used = [0] * len(filled)
        for kind, key, region in steps:
            if region is not None:
                self.before[kind, key] = (region, used[region])
                used[region] += 1
                self.at[kind, key] = (region, used[region])
        self.used = used

    def room(self, eng, kind, *key):
        r, n = self.before[kind, key]
        if n:
            eng.wait_ge(self.empty[r], n)

    def filled(self, kind, *key):
        r, n = self.at[kind, key]
        return self.full[r], n

    def drained(self, kind, *key):
        r, n = self.at[kind, key]
        return self.empty[r], n

    def signal_filled(self, kind, *key):
        return self.full[self.at[kind, key][0]], 1

    def signal_drained(self, kind, *key):
        return self.empty[self.at[kind, key][0]], 1


def rope_tables():
    def table(n, dim):
        inv = (1.0 / 10000.0 ** (np.arange(0, dim, 2, dtype=np.float32) / np.float32(dim))).astype(np.float32)
        f = np.arange(n, dtype=np.float32)[:, None] * inv[None, :]
        return np.repeat(np.sin(f), 2, axis=-1), np.repeat(np.cos(f), 2, axis=-1)
    sk, ck = table(L, DC)
    sk = np.concatenate([-sk[:, :DC // 2], sk[:, DC // 2:]], axis=1)
    sq, cq = table(S, DCQ)
    lay = lambda a: np.tile(a.T, (1, BG))
    cosq = np.stack([lay(cq[:, :HALF]), lay(cq[:, HALF:])], axis=1)
    sinq = np.stack([lay(sq[:, HALF:]), -lay(sq[:, :HALF])], axis=1)
    return (ck.reshape(LP, LT * DC).astype(np.float32), sk.reshape(LP, LT * DC).astype(np.float32),
            np.ascontiguousarray(cosq, np.float32), np.ascontiguousarray(sinq, np.float32))


def before_masks(n):
    return np.tril(np.ones((n, n), np.float32), -1).reshape(1, n * n)


def build_program(nc, a, out, x_mid):
    top = ExitStack()
    with top:
        def sb(name, shape, dt=F32, stack=top):
            return stack.enter_context(nc.sbuf_tensor(name, shape, dt))

        wide = [top.enter_context(nc.psum_tensor(f"wide{i}", [128, 2, 512], F32)) for i in range(2)]
        single = [top.enter_context(nc.psum_tensor(f"single{i}", [128, 512], F32)) for i in range(4)]
        region = wide + single
        mix_acc = region[2]

        ident = sb("ident", [128, 128])
        ones = sb("ones", [128, DC])
        mean_w = sb("mean_w", [128, 128])
        eps = sb("eps", [128, 1])
        cosk = sb("cosk", [LP, LT, DC])
        sink = sb("sink", [LP, LT, DC])
        cosq = sb("cosq", [HALF, 2, NT])
        sinq = sb("sinq", [HALF, 2, NT])
        tie4 = sb("tie4", [TR, 16])
        tie8 = sb("tie8", [TR, 64])
        tie16 = sb("tie16", [TR, 256])
        bias0 = sb("bias0", [TR, E0])

        s_names = ["load", "setup_full", "setup_const"] + [f"setup_copied_{i}" for i in range(2)]
        setup_sems = {n: top.enter_context(nc.semaphore(n)) for n in s_names}
        group_names = (
            [f"filled_{i}" for i in range(6)] + [f"drained_{i}" for i in range(6)]
            + [f"ctx_loaded_{j}" for j in range(1, BG)] + [f"weights_loaded_{i}" for i in range(WSLOT)] + ["next_loaded", "stored", "rope_cos", "rope_sin", "rope_done", "keyh", "keyone",
               "centred", "squared", "std", "rstd", "normed", "qcos", "qrot", "qhigh", "mixed", "pool_sum", "dve_sum",
               "maxneg", "shift_loaded", "recip", "ctx_ready", "route_step", "routed", "gate_act",
               "hid_ready", "down_done", "acc_done", "lora_in", "tok_step",
               "tok_exp", "mask_ready", "lora_acc", "lora_z", "out_ready", "premix"])
        first = None
        sems = {n: top.enter_context(nc.semaphore(n)) for n in group_names}
        nums = [s.num for s in sems.values()]
        group_range = range(min(nums), max(nums) + 1)
        setup_nums = [s.num for s in setup_sems.values()]
        setup_range = range(min(setup_nums), max(setup_nums) + 1)
        assert len(group_range) == len(nums) and len(setup_range) == len(setup_nums)

        with nc.Block() as block:
            load = setup_sems["load"]

            @block.sync
            def _(sp):
                for dst, name in ((cosk[:], "cosk"), (sink[:], "sink"), (cosq[:], "cosq"), (sinq[:], "sinq"),
                                  (ident[:], "ident")):
                    sp.dma_start(dst.rearrange("p a b -> p (a b)") if name != "ident" else dst,
                                 a[name].rearrange("p a b -> p (a b)") if name.endswith("q") else a[name]).then_inc(load, 16)
                for dst, name in ((tie4, "tie4"), (tie8, "tie8"), (tie16, "tie16"), (bias0, "bias")):
                    src = a[name]
                    sp.dma_start(dst[:], src.broadcast_to([TR, src.shape[1]])).then_inc(load, 16)
                sp.wait_ge(load, 9 * 16)

            @block.vector
            def _(dve):
                nc.vector.memset(ones[:], 1.0)
                nc.vector.memset(mean_w[:], 1.0 / D)
                nc.vector.memset(eps[:], EPS)
        nc.all_engine_barrier(sems_to_clear=setup_range)

        for layer in range(2):
            with ExitStack() as weights:
                w = layer_weights(nc, layer, sb, weights)
                with ExitStack() as staging:
                    merge_weights(nc, layer, a, w, region, setup_sems, sb, staging)
                nc.all_engine_barrier(sems_to_clear=setup_range)
                with ExitStack() as work:
                    run_layer(nc, layer, a, w, x_mid, out, sems, group_range, setup_sems, setup_range, sb, work,
                              region, mix_acc,
                              dict(ident=ident, ones=ones, mean_w=mean_w, eps=eps, cosk=cosk, sink=sink, cosq=cosq,
                                   sinq=sinq, tie4=tie4, tie8=tie8, tie16=tie16, bias0=bias0))


def layer_weights(nc, layer, sb, stack):
    w = {"wvo": sb(f"wvo{layer}", [128, H // 2, D], stack=stack)}
    if layer == 0:
        w["w1"] = sb("w1", [128, KT, H, DCQ], stack=stack)
        w["w2"] = sb("w2", [HALF, 2, H, 2 * DC], stack=stack)
        w["router"] = sb("router0", [128, KT, E0], stack=stack)
    else:
        w["wabs"] = sb("wabs", [128, KT, H, 2 * DC], stack=stack)
        w["router"] = sb("router1", [128, KT, E1], stack=stack)
        w["up"] = sb("w_up", [128, KT, HID], stack=stack)
        w["gate"] = sb("w_gate", [128, KT, HID], stack=stack)
        w["down"] = sb("w_down", [128, MT, D], stack=stack)
        w["upA"] = sb("upA", [128, KT, 128], stack=stack)
        w["gateA"] = sb("gateA", [128, KT, 128], stack=stack)
        w["upB"] = sb("upB", [128, HID], stack=stack)
        w["gateB"] = sb("gateB", [128, HID], stack=stack)
        w["downA"] = sb("downA", [128, MT, 128], stack=stack)
        w["downB"] = sb("downB", [128, D], stack=stack)
    return w


def merge_weights(nc, layer, a, w, region, sems, sb, stack):
    n = str(layer)
    wq = sb("st_wq" + n, [128, H, D], stack=stack)
    kcq = sb("st_kcq" + n, [128, H, DCQ], stack=stack)
    kckv = sb("st_kckv" + n, [128, H, DC], stack=stack)
    wo = sb("st_wo" + n, [128, H, D], stack=stack)
    wqr = sb("st_wqr" + n, [DR, H, DCQ], stack=stack)
    wkr = sb("st_wkr" + n, [DR, H, DC], stack=stack)
    if layer == 1:
        w1t = sb("st_w1t", [HALF, 2, H, D], stack=stack)
        w2 = sb("st_w2", [HALF, 2, H, 2 * DC], stack=stack)
    else:
        w2 = w["w2"]
    load, full, copied = sems["load"], sems["setup_full"], [sems["setup_copied_0"], sems["setup_copied_1"]]
    loads = [(wq[:], a[f"wq{n}"].rearrange("(h k) f -> k h f", k=HK)),
             (kcq[:], a[f"kcq{n}"].rearrange("h k q -> k h q")),
             (wqr[:], a[f"wqr{n}"]), (wkr[:], a[f"wkr{n}"]),
             (kckv[:], a[f"kckv{n}"].rearrange("h k d -> k h d")),
             (wo[:], a[f"wo{n}"].rearrange("(h k) f -> k h f", k=HK)),
             (w["router"][:], a[f"router{n}"].rearrange("(k p) e -> p k e", p=128))]
    if layer == 1:
        for name in ("up", "gate", "upA", "gateA"):
            loads.append((w[name][:], a["f_" + name].rearrange("(k p) e -> p k e", p=128)))
        for name in ("upB", "gateB", "downB"):
            loads.append((w[name][:], a["f_" + name]))
        whole = HID // 128
        for name in ("down", "downA"):
            src = a["f_" + name]
            loads.append((w[name][:, 0:whole, :], src[0:whole * 128, :].rearrange("(m p) e -> p m e", p=128)))
            loads.append((w[name][0:HID - whole * 128, whole, :], src[whole * 128:HID, :]))

    items = []
    for h in range(H):
        for c in range(2):
            items.append(("w2", h, c))
        for c in range(2):
            items.append(("w1" if layer == 0 else "w1t", h, c))
        items.append(("wvo", h, 0))
    if layer == 1:
        for h in range(H):
            for c in range(2):
                items.append(("wabs", h, c))
    banks = [region[0][:, 0, :], region[0][:, 1, :], region[1][:, 0, :], region[1][:, 1, :]] + [region[i][:, :] for i in range(2, 6)]

    def place(item):
        kind, h, c = item
        if kind == "w2":
            return w2[:, c, h, :], (0, HALF), 2 * DC
        if kind == "w1":
            return w["w1"][:, c, h, :], (0, 128), DCQ
        if kind == "w1t":
            return w1t[:, c, h, :], (0, HALF), D
        if kind == "wvo":
            p = 64 * (h // (H // 2))
            return w["wvo"][p:p + DC, h % (H // 2), :], (p, p + DC), D
        return w["wabs"][:, c, h, :], (0, 128), 2 * DC

    with nc.Block() as block:
        @block.sync
        def _(sp):
            for dst, src in loads:
                sp.dma_start(dst, src).then_inc(load, 16)
            sp.wait_ge(load, 16 * len(loads))

        @block.tensor
        def _(pe):
            pe.wait_ge(load, 16 * len(loads))
            for i, (kind, h, c) in enumerate(items):
                bank = banks[i % 8]
                if i >= 8:
                    pe.wait_ge(copied[i % 2], (i - 8) // 2 + 1)
                if kind == "wabs" and h == 0 and c == 0:
                    for k in range(2):
                        pe.wait_ge(copied[k], (i + 1 - k) // 2)
                if kind == "w2":
                    mm = pe.matmul(bank[0:HALF, 0:2 * DC], wqr[:, h, c * HALF:(c + 1) * HALF],
                                   wkr[:, h, :].unsqueeze(1).broadcast_to([DR, 2, DC]), start=True, stop=True)
                elif kind == "w1":
                    mm = pe.matmul(bank[:, 0:DCQ], wq[:, h, c * 128:(c + 1) * 128], kcq[:, h, :], start=True, stop=True)
                elif kind == "w1t":
                    mm = pe.matmul(bank[0:HALF, 0:D], kcq[:, h, c * HALF:(c + 1) * HALF], wq[:, h, :], start=True, stop=True)
                elif kind == "wvo":
                    p = 64 * (h // (H // 2))
                    mm = pe.matmul(bank[p:p + DC, 0:D], kckv[:, h, :], wo[:, h, :], start=True, stop=True)
                else:
                    for k in range(2):
                        mm = pe.matmul(bank[:, 0:2 * DC], w1t[:, k, h, c * 128:(c + 1) * 128], w2[:, k, h, :],
                                       start=(k == 0), stop=(k == 1))
                mm.then_inc(full, 1)

        def copies(eng, k, copy):
            for i, item in enumerate(items):
                if i % 2 == k:
                    dst, (p, q), width = place(item)
                    eng.wait_ge(full, i + 1)
                    copy(dst, banks[i % 8][p:q, 0:width]).then_inc(copied[k], 1)

        @block.scalar
        def _(act):
            copies(act, 0, lambda dst, src: nc.scalar.activation(dst, src, ACT.Copy))

        @block.vector
        def _(dve):
            copies(dve, 1, nc.vector.tensor_copy)


def run_layer(nc, layer, a, w, x_mid, out, sems, group_range, setup_sems, setup_range, sb, stack, region, mix_acc, c):
    n = str(layer)

    def buf(name, shape, dt=F32):
        return sb(name + n, shape, dt, stack=stack)

    raw = buf("raw", [LP, 2, LT, DC])
    rope_c = buf("rope_c", [LP, LT, DC])
    rope_s = buf("rope_s", [LP, LT, DC])
    kv = buf("kv", [LP, 3, LT, DC])
    kparts = buf("kparts", [128, 2, L], F32R)
    kones = buf("kones", [DC + 1, 2, L], F32R)
    qhigh = buf("qhigh", [128, BG, NQ], F32R)
    qlow = buf("qlow", [DC + 1, BG, NQ], F32R)
    prob = buf("prob", [LP, NPROB, NQ])
    sum_pool = buf("sum_pool", [LP, 2, NQ])
    sum_dve = buf("sum_dve", [LP, 2, NQ])
    ctx_raw = buf("ctx_raw", [128, 2, HQ])
    recip = buf("recip", [128, 2, HQ])
    ctx_n = buf("ctx_n", [128, BG, HQ])
    maxpart = buf("maxpart", [128, 2, NMAX, 3])
    maxneg = buf("maxneg", [128, 2, NMAX])
    maxrow = buf("maxrow", [NMAX, 2, 128], F32R)
    x_in = buf("x_in", [128, KT, NT])
    x_cen = buf("x_cen", [128, KT, NT])
    x_sq = buf("x_sq", [128, KT, NT])
    x_std = buf("x_std", [128, NT])
    x_rstd = buf("x_rstd", [128, NT])
    x_n = buf("x_n", [128, KT, NT])
    x_res = buf("x_res", [128, KT, NT])
    if layer == 0:
        qa, qb, qr = (prob[0:HALF, i, :].rearrange("p (h a b) -> p h a b", h=2, a=2) for i in range(3))
        gact = buf("gact", [128, 2, NT])
        hid = buf("hid", [128, 2, NT])
        wexp = buf("wexp", [128, WSLOT, 3 * D])
        NE = E0
    else:
        NE = E1
        lora_in = ctx_raw[:, :, :].rearrange("p h (a b) -> p h a b", a=2)
        tok, tokc, maskT, lora_z = (ctx_n[:, i, :].rearrange("p (a b) -> p a b", a=2) for i in range(4))
        tokmax = buf("tokmax", [128, 2 * BG])
        mask_rows = sum_pool[0:TR, 0, 0:4 * 128].rearrange("p (a b c) -> p a b c", a=2, b=2)
        sact = buf("sact", [128, 2, 2 * NT])
        hid = buf("hid", [128, 2, 2 * NT])
        hsum = buf("hsum", [128, 2, NT])
        tokw = buf("tokw", [TR, 2, 2])
        mask = buf("mask", [TR, 2, 2, E1])
        tokm = buf("tokm", [TR, 2, 2, E1])
    score = buf("score", [TR, 2, NE])
    rt1 = buf("rt1", [TR, 2, NE])
    rt2 = buf("rt2", [TR, 2, NE])
    rt3 = buf("rt3", [TR, 2, NE])
    rt4 = buf("rt4", [TR, 2, NE])
    rg1 = buf("rg1", [TR, 2, GRP0])
    rg2 = buf("rg2", [TR, 2, GRP0])
    rs1 = buf("rs1", [TR, 2])
    rs2 = buf("rs2", [TR, 2])
    cmp1 = buf("cmp1", [TR, 2 * NE * NE])
    cmp2 = buf("cmp2", [TR, 2 * NE * NE])
    cw = buf("cw", [TR, 2, NE])

    x_src = a["x"] if layer == 0 else x_mid
    x_dst = x_mid if layer == 0 else out
    steps = schedule(layer)
    R = Regions(steps, [sems[f"filled_{i}"] for i in range(6)], [sems[f"drained_{i}"] for i in range(6)])
    s = sems

    def kdst(j):
        return j % 2

    with nc.Block() as block:
        @block.sync
        def _(sp):
            sp.dma_start(x_in[:], x_src[0]).then_inc(setup_sems["load"], 16)
            sp.dma_start(raw[:, 0, :, :].rearrange("p t d -> p (t d)"), a["ctx"][0]).then_inc(setup_sems["load"], 16)
            sp.wait_ge(setup_sems["load"], 32)
            if layer == 0:
                sp.dma_start(x_mid[G], x_in[:]).then_inc(setup_sems["load"], 16)
                sp.wait_ge(setup_sems["load"], 48)

        @block.vector
        def _(dve):
            nc.vector.memset(kones[DC:DC + 1, :, :].bitcast(F32), 1.0)
    nc.all_engine_barrier(sems_to_clear=setup_range)

    with nc.Fori(0, G) as g:
        with nc.Block() as block:
            @block.sync
            def _(sp):
                def weights_of(i):
                    if i >= WSLOT:
                        sp.wait_ge(s["down_done"], i - WSLOT + 1)
                    sp.dma_start(wexp[:, i % WSLOT, :], a["experts"][i]).then_inc(s[f"weights_loaded_{i % WSLOT}"], 16)

                sp.dma_start(raw[:, 1, :, :].rearrange("p t d -> p (t d)"), a["ctx"][BG * g + 1]).then_inc(s["ctx_loaded_1"], 16)
                if layer == 0:
                    for i in range(WSLOT):
                        weights_of(i)
                for kind, key, _ in steps:
                    if kind == "rope" and key[0] + 2 <= BG:
                        j = key[0] + 2
                        sp.wait_ge(s["rope_done"], key[0] + 1)
                        sem = s[f"ctx_loaded_{j}"] if j < BG else s["next_loaded"]
                        sp.dma_start(raw[:, j % 2, :, :].rearrange("p t d -> p (t d)"), a["ctx"][BG * g + j]).then_inc(sem, 16)
                    if kind == "maxT":
                        j, = key
                        sp.wait_ge(*R.drained("maxT", j))
                        sp.dma_start(qlow[DC:DC + 1, j, :].bitcast(F32), maxrow[:, j % 2, :].bitcast(F32)).then_inc(s["shift_loaded"], 16)
                    if kind == "attn":
                        sp.wait_ge(*R.drained("attn"))
                        sp.dma_start(x_in[:], x_src[g + 1]).then_inc(s["next_loaded"], 16)
                if layer == 0:
                    for i in range(WSLOT, E0 + 1):
                        weights_of(i)
                sp.wait_ge(s["out_ready"], 2)
                sp.dma_start(x_dst[g], x_cen[:]).then_inc(s["stored"], 16)
                sp.wait_ge(s["next_loaded"], 32)
                sp.wait_ge(s["stored"], 16)

            @block.tensor
            def _(pe):
                for kind, key, reg in steps:
                    if reg is not None:
                        R.room(pe, kind, *key)
                        acc = region[reg]
                    if kind == "mean":
                        src = x_in if key[0] == 0 else x_res
                        if key[0]:
                            pe.wait_ge(*R.drained("attn"))
                        for k in range(KT):
                            mm = pe.matmul(acc[:, 0:NT], c["mean_w"][:], src[:, k, :], start=(k == 0), stop=(k == KT - 1))
                        mm.then_inc(*R.signal_filled(kind, *key))
                    elif kind == "var":
                        pe.wait_ge(s["squared"], key[0] + 1)
                        for k in range(KT):
                            mm = pe.matmul(acc[:, 0:NT], c["mean_w"][:], x_sq[:, k, :], start=(k == 0), stop=(k == KT - 1))
                        mm.then_inc(*R.signal_filled(kind, *key))
                    elif kind == "keyT":
                        j, b = key
                        pe.wait_ge(s["rope_done"], j + 1)
                        for i in range(4):
                            mm = pe.transpose(acc[0:DC, i * LP:(i + 1) * LP], kv[:, j % 3, 4 * b + i, :], c["ident"][0:LP, 0:LP])
                        mm.then_inc(*R.signal_filled(kind, *key))
                    elif kind == "qwide":
                        h, = key
                        if h == 0:
                            pe.wait_ge(s["normed"], 1)
                        for half in range(2):
                            for k in range(KT):
                                mm = pe.matmul(acc[0:HALF, 0, half * NT:(half + 1) * NT], w["w1"][:, k, h, half * HALF:(half + 1) * HALF],
                                               x_n[:, k, :], start=(k == 0), stop=(k == KT - 1))
                        mm.then_inc(*R.signal_filled(kind, *key))
                    elif kind == "query":
                        h, = key
                        dst = acc[:, 0, 0:NT] if reg < 2 else acc[:, 0:NT]
                        if layer == 0:
                            pe.wait_ge(s["qrot"], 2 * (h + 1))
                            for half in range(2):
                                mm = pe.matmul(dst, w["w2"][:, half, h, :], qr[:, h % 2, half, :], start=(half == 0), stop=(half == 1))
                        else:
                            if h == 0:
                                pe.wait_ge(s["normed"], 1)
                            for k in range(KT):
                                mm = pe.matmul(dst, w["wabs"][:, k, h, :], x_n[:, k, :], start=(k == 0), stop=(k == KT - 1))
                        mm.then_inc(*R.signal_filled(kind, *key))
                    elif kind == "smax":
                        j, t, b = key
                        if b == 0:
                            pe.wait_ge(*R.drained("query", head_rows(t)))
                            if t == 0:
                                for i in range(3):
                                    pe.wait_ge(*R.drained("keyT", j, i))
                        pe.matmul(acc[:, 0:LB], qhigh[:, j, t * 128:(t + 1) * 128], kparts[:, kdst(j), b * LB:(b + 1) * LB],
                                  start=True, stop=True).then_inc(*R.signal_filled(kind, *key))
                    elif kind == "maxT":
                        j, = key
                        pe.wait_ge(s["maxneg"], j + 1)
                        pe.matmul(acc[0:NMAX, 0:128], maxneg[:, j % 2, :], c["ident"][:], start=True, stop=True)\
                            .then_inc(*R.signal_filled(kind, *key))
                    elif kind == "score":
                        j, t = key
                        if t == 0:
                            pe.wait_ge(s["shift_loaded"], 16 * (j + 1))
                            pe.wait_ge(*R.drained("query", H - 1))
                            pe.wait_ge(s["keyone"], 3 * (j + 1))
                        cols = slice(t * LP, (t + 1) * LP)
                        for half in range(2):
                            q = slice(half * HQ, (half + 1) * HQ)
                            pe.matmul(acc[0:LP, half, 0:HQ], kparts[:, kdst(j), cols], qhigh[:, j, q], start=True, stop=False)
                        for half in range(2):
                            q = slice(half * HQ, (half + 1) * HQ)
                            mm = pe.matmul(acc[0:LP, half, 0:HQ], kones[:, kdst(j), cols], qlow[:, j, q], start=False, stop=True)
                        mm.then_inc(*R.signal_filled(kind, *key))
                    elif kind == "mix":
                        j, t = key
                        if t == 0 and j:
                            pe.wait_ge(s["mixed"], j)
                        if t == 0 and not j:
                            last = H - 1 if layer == 0 else max(h for h in range(H) if h % 3 == 2)
                            pe.wait_ge(*R.drained("query", last))
                        pe.wait_ge(*R.drained("score", j, t))
                        for half in range(2):
                            mm = pe.matmul(mix_acc[64 * half:64 * half + DC, 0:HQ], kv[:, j % 3, t, :],
                                           prob[:, (j * LT + t) % NPROB, half * HQ:(half + 1) * HQ], start=(t == 0), stop=(t == LT - 1))
                        mm.then_inc(s["premix"], 1)
                    elif kind == "norm":
                        j, = key
                        pe.wait_ge(s["pool_sum"], (POOL_TILES - 1) * (j + 1))
                        pe.wait_ge(s["dve_sum"], (LT - POOL_TILES - 1) * (j + 1))
                        for i, part in enumerate((sum_pool, sum_dve)):
                            for half in range(2):
                                mm = pe.matmul(acc[64 * half:64 * half + DC, 0:HQ], c["ones"][0:LP, :],
                                               part[:, j % 2, half * HQ:(half + 1) * HQ], start=(i == 0), stop=(i == 1))
                        mm.then_inc(*R.signal_filled(kind, *key))
                    elif kind == "attn":
                        pe.wait_ge(s["ctx_ready"], BG)
                        for m in range(KT):
                            for i in range(H // 2):
                                mm = pe.matmul(acc[:, m, 0:NT].rearrange("p (j s) -> p j s", j=BG), w["wvo"][:, i, m * 128:(m + 1) * 128],
                                               ctx_n[:, :, i * S:(i + 1) * S], start=(i == 0), stop=(i == H // 2 - 1))
                        mm.then_inc(*R.signal_filled(kind, *key))
                    elif kind == "route":
                        pe.wait_ge(s["normed"], 2)
                        for i in range(2):
                            for k in range(KT):
                                mm = pe.matmul(acc[0:TR, 0, i * NE:(i + 1) * NE], x_n[:, k, i * TR:(i + 1) * TR], w["router"][:, k, :],
                                               start=(k == 0), stop=(k == KT - 1))
                        mm.then_inc(*R.signal_filled(kind, *key))
                    elif kind == "gateup" and layer == 0:
                        i, = key
                        pe.wait_ge(s[f"weights_loaded_{i % WSLOT}"], 16 * (i // WSLOT + 1))
                        for half in range(2):
                            for k in range(KT):
                                at = (half * KT + k) * I0
                                mm = pe.matmul(acc[:, half, 0:NT], wexp[:, i % WSLOT, at:at + I0], x_n[:, k, :],
                                               start=(k == 0), stop=(k == KT - 1))
                        mm.then_inc(*R.signal_filled(kind, *key))
                    elif kind == "weight":
                        i, = key
                        if i == 1:
                            pe.wait_ge(s["routed"], 1)
                        for r in range(2):
                            mm = pe.matmul(acc[:, r * TR:(r + 1) * TR], cw[:, r, i - 1:i].broadcast_to([TR, 128]), c["ident"][0:TR, 0:TR],
                                           start=True, stop=True)
                        mm.then_inc(*R.signal_filled(kind, *key))
                    elif kind == "down" and layer == 0:
                        i, = key
                        if i == 0:
                            pe.wait_ge(s["normed"], 2)
                        pe.wait_ge(*R.drained("gateup", i))
                        for m in range(KT):
                            mm = pe.matmul(region[(2, 5)[m]][:, 0:NT], wexp[:, i % WSLOT, 2 * D + m * 128:2 * D + (m + 1) * 128],
                                           hid[:, i % 2, :], start=(i == 0), stop=(i == E0))
                        mm.then_inc(s["down_done"], 1)
                    elif kind == "lora":
                        for half, name in enumerate(("upA", "gateA")):
                            for k in range(KT):
                                mm = pe.matmul(acc[:, half * NT:(half + 1) * NT], w[name][:, k, :], x_n[:, k, :], start=(k == 0), stop=(k == KT - 1))
                        mm.then_inc(*R.signal_filled(kind, *key))
                    elif kind == "tokw":
                        pe.wait_ge(s["routed"], 1)
                        for slot in range(2):
                            for r in range(2):
                                at = slot * NT + r * TR
                                mm = pe.matmul(acc[:, at:at + TR], tokw[:, slot, r:r + 1].broadcast_to([TR, 128]), c["ident"][0:TR, 0:TR],
                                               start=True, stop=True)
                        mm.then_inc(*R.signal_filled(kind, *key))
                    elif kind == "mask":
                        for slot in range(2):
                            for r in range(2):
                                at = slot * NT + r * TR
                                mm = pe.matmul(acc[:, at:at + TR], mask_rows[:, slot, r, :],
                                               c["ident"][0:TR, 0:TR], start=True, stop=True)
                        mm.then_inc(*R.signal_filled(kind, *key))
                    elif kind == "gateup":
                        m, = key
                        M = min(128, HID - m * 128)
                        cols = slice(m * 128, m * 128 + M)
                        if m == 0:
                            pe.wait_ge(s["lora_in"], 2)
                        for half, (base, low) in enumerate((("up", "upB"), ("gate", "gateB"))):
                            for k in range(KT):
                                pe.matmul(acc[0:M, half, 0:2 * NT].rearrange("p (a b) -> p a b", a=2), w[base][:, k, cols],
                                          x_n[:, k, :].unsqueeze(1).broadcast_to([128, 2, NT]), start=(k == 0), stop=False)
                            mm = pe.matmul(acc[0:M, half, 0:2 * NT], w[low][:, cols], lora_in[:, half, :, :].rearrange("p a b -> p (a b)"),
                                           start=False, stop=True)
                        mm.then_inc(*R.signal_filled(kind, *key))
                    elif kind == "down":
                        m, = key
                        M = min(128, HID - m * 128)
                        if m == 0:
                            pe.wait_ge(*R.drained("tokw"))
                            pe.wait_ge(*R.drained("mask"))
                        pe.wait_ge(s["hid_ready"], m + 1)
                        pe.matmul(region[3][:, 0:2 * NT], w["downA"][0:M, m, :], hid[0:M, m % 2, :], start=(m == 0), stop=(m == MT - 1))
                        pe.wait_ge(s["acc_done"], m + 1)
                        for q in range(KT):
                            mm = pe.matmul(region[(2, 4)[q]][:, 0:NT], w["down"][0:M, m, q * 128:(q + 1) * 128], hsum[0:M, m % 2, :],
                                           start=(m == 0), stop=False)
                        mm.then_inc(s["down_done"], 1)
                    elif kind == "loradown":
                        pe.wait_ge(s["lora_z"], 1)
                        for q in range(KT):
                            for slot in range(2):
                                mm = pe.matmul(region[(2, 4)[q]][:, 0:NT], w["downB"][:, q * 128:(q + 1) * 128], lora_z[:, slot, :],
                                               start=False, stop=(slot == 1))
                        mm.then_inc(s["down_done"], 1)

            @block.scalar
            def _(act):
                for kind, key, reg in steps:
                    if reg is not None:
                        acc = region[reg]
                    if kind == "var":
                        act.wait_ge(*R.filled(kind, *key))
                        if key[0]:
                            act.wait_ge(s["rstd"], 1)
                        nc.scalar.activation(x_std[:], acc[:, 0:NT], ACT.Sqrt, bias=c["eps"][:, 0:1]).then_inc(*R.signal_drained(kind, *key))
                    elif kind == "keyT":
                        j, b = key
                        cols = slice(b * LB, (b + 1) * LB)
                        act.wait_ge(*R.filled(kind, *key))
                        nc.scalar.activation(kparts[0:DC, kdst(j), cols], acc[0:DC, 0:LB], ACT.Copy).then_inc(s["keyh"], 1)
                        nc.scalar.activation(kones[0:DC, kdst(j), cols], acc[0:DC, 0:LB], ACT.Copy).then_inc(s["keyone"], 1)
                    elif kind == "query":
                        h, = key
                        src = acc[:, 0, 0:NT] if reg < 2 else acc[:, 0:NT]
                        act.wait_ge(*R.filled(kind, *key))
                        nc.scalar.activation(qhigh[:, :, h * S:(h + 1) * S], src.rearrange("p (j s) -> p j s", j=BG), ACT.Copy)\
                            .then_inc(s["qhigh"], 1)
                    elif kind == "maxT":
                        j, = key
                        act.wait_ge(*R.filled(kind, *key))
                        if j >= 2:
                            act.wait_ge(s["shift_loaded"], 16 * (j - 1))
                        nc.scalar.activation(maxrow[:, j % 2, :], acc[0:NMAX, 0:128], ACT.Copy).then_inc(*R.signal_drained(kind, *key))
                    elif kind == "score":
                        j, t = key
                        n_ = j * LT + t
                        act.wait_ge(*R.filled(kind, *key))
                        if n_ >= NPROB:
                            act.wait_ge(s["premix"], n_ - NPROB + 1)
                            jo, to = divmod(n_ - NPROB, LT)
                            if to < POOL_TILES:
                                act.wait_ge(s["pool_sum"], (POOL_TILES - 1) * jo + max(1, to))
                            else:
                                act.wait_ge(s["dve_sum"], (LT - POOL_TILES - 1) * jo + max(1, to - POOL_TILES))
                        nc.scalar.activation(prob[:, n_ % NPROB, :].rearrange("p (a b) -> p a b", a=2), acc[0:LP, :, 0:HQ], ACT.Exp)\
                            .then_inc(*R.signal_drained(kind, *key))
                    elif kind == "context":
                        j, = key
                        act.wait_ge(s["premix"], LT * (j + 1))
                        if j >= 2:
                            act.wait_ge(s["ctx_ready"], j - 1)
                        nc.scalar.activation(ctx_raw[:, j % 2, :], mix_acc[:, 0:HQ], ACT.Copy).then_inc(s["mixed"], 1)
                    elif kind == "route" and layer == 0:
                        act.wait_ge(*R.filled(kind))
                        nc.scalar.activation(rt1[:], acc[0:TR, 0, 0:2 * NE].rearrange("p (a e) -> p a e", a=2), ACT.Exp, scale=-1.0)\
                            .then_inc(*R.signal_drained(kind))
                    elif kind == "tokw":
                        act.wait_ge(s["tok_step"], 2)
                        nc.scalar.activation(tok, tok, ACT.Exp).then_inc(s["tok_exp"], 1)
                    elif kind == "gateup" and layer == 0:
                        i, = key
                        act.wait_ge(*R.filled(kind, *key))
                        if i >= 2:
                            act.wait_ge(*R.drained(kind, i - 2))
                        nc.scalar.activation(gact[:, i % 2, :], acc[:, 0, 0:NT], ACT.Silu).then_inc(s["gate_act"], 1)
                    elif kind == "gateup":
                        m, = key
                        M = min(128, HID - m * 128)
                        act.wait_ge(*R.filled(kind, *key))
                        if m >= 2:
                            act.wait_ge(s["hid_ready"], m - 1)
                        nc.scalar.activation(sact[0:M, m % 2, :], acc[0:M, 0, 0:2 * NT], ACT.Silu).then_inc(s["gate_act"], 1)

            @block.gpsimd
            def _(pool):
                for kind, key, reg in steps:
                    if kind == "rope":
                        j, = key
                        if j:
                            pool.wait_ge(s["rope_done"], j)
                        if 1 <= j:
                            pool.wait_ge(s[f"ctx_loaded_{j}"], 16)
                        r = raw[:, j % 2, :, :]
                        hd = DC // 2
                        nc.gpsimd.tensor_tensor(rope_s[:, :, 0:hd], r[:, :, hd:DC], c["sink"][:, :, 0:hd], ALU.mult).then_inc(s["rope_sin"], 1)
                        nc.gpsimd.tensor_tensor(rope_s[:, :, hd:DC], r[:, :, 0:hd], c["sink"][:, :, hd:DC], ALU.mult).then_inc(s["rope_sin"], 1)
                    elif kind == "qwide":
                        h, = key
                        pool.wait_ge(s["qcos"], h + 1)
                        pool.wait_ge(*R.drained("qwide", h))
                        if h >= 2:
                            pool.wait_ge(*R.filled("query", h - 2))
                        for half in range(2):
                            nc.gpsimd.tensor_tensor(qr[:, h % 2, half, :], qa[:, h % 2, half, :], qb[:, h % 2, 1 - half, :], ALU.add)\
                                .then_inc(s["qrot"], 1)
                    elif kind == "mix":
                        j, t = key
                        if 1 <= t < POOL_TILES:
                            pool.wait_ge(*R.drained("score", j, t))
                            n_ = j * LT + t
                            dst = sum_pool[:, j % 2, :]
                            if t == 1:
                                if j >= 2:
                                    pool.wait_ge(*R.filled("norm", j - 2))
                                first_in = prob[:, (n_ - 1) % NPROB, :]
                            else:
                                pool.wait_ge(s["pool_sum"], (POOL_TILES - 1) * j + t - 1)
                                first_in = dst
                            nc.gpsimd.tensor_tensor(dst, first_in, prob[:, n_ % NPROB, :], ALU.add).then_inc(s["pool_sum"], 1)
                    elif kind == "gateup" and layer == 1:
                        m, = key
                        M = min(128, HID - m * 128)
                        pool.wait_ge(s["hid_ready"], m + 1)
                        if m >= 2:
                            pool.wait_ge(s["down_done"], m - 1)
                        nc.gpsimd.tensor_tensor(hsum[0:M, m % 2, :], hid[0:M, m % 2, 0:NT], hid[0:M, m % 2, NT:2 * NT], ALU.add)\
                            .then_inc(s["acc_done"], 1)

            @block.vector
            def _(dve):
                V = nc.vector
                forks = [0]

                def then(ins):
                    forks[0] += 1
                    ins.then_inc(s["route_step"], 1)
                    dve.wait_ge(s["route_step"], forks[0])

                def ranks(v, groups, width, tie, dst):
                    shape = [TR, groups, width, width]
                    gt = cmp1[:, 0:groups * width * width].rearrange("p (g a b) -> p g a b", g=groups, a=width)
                    eq = cmp2[:, 0:groups * width * width].rearrange("p (g a b) -> p g a b", g=groups, a=width)
                    other = v.unsqueeze(2).broadcast_to(shape)
                    own = v.unsqueeze(3).broadcast_to(shape)
                    V.tensor_tensor(gt, other, own, ALU.is_gt)
                    then(V.tensor_tensor(eq, other, own, ALU.is_equal))
                    flat_eq = cmp2[:, 0:groups * width * width].rearrange("p (g x) -> p g x", g=groups)
                    then(V.tensor_tensor(flat_eq, flat_eq, tie[:].unsqueeze(1).broadcast_to([TR, groups, width * width]), ALU.mult))
                    then(V.tensor_tensor(gt, gt, eq, ALU.add))
                    then(V.tensor_reduce(dst, gt, AX.X, ALU.add))

                for kind, key, reg in steps:
                    if reg is not None:
                        acc = region[reg]
                    if kind == "rope":
                        j, = key
                        r = raw[:, j % 2, :, :]
                        if j:
                            dve.wait_ge(s[f"ctx_loaded_{j}"], 16)
                            dve.wait_ge(s["rope_done"], j)
                        V.tensor_tensor(rope_c[:], r, c["cosk"][:], ALU.mult).then_inc(s["rope_cos"], 1)
                        dve.wait_ge(s["rope_cos"], j + 1)
                        dve.wait_ge(s["rope_sin"], 2 * (j + 1))
                        if j >= 3:
                            dve.wait_ge(s["premix"], LT * (j - 2))
                        V.tensor_tensor(kv[:, j % 3, :, :], rope_c[:], rope_s[:], ALU.add).then_inc(s["rope_done"], 1)
                    elif kind == "mean":
                        src = x_in if key[0] == 0 else x_res
                        dve.wait_ge(*R.filled(kind, *key))
                        V.tensor_tensor(x_cen[:], src[:], acc[:, 0:NT].unsqueeze(1).broadcast_to([128, KT, NT]), ALU.subtract)\
                            .then_inc(*R.signal_drained(kind, *key))
                        dve.wait_ge(*R.drained(kind, *key))
                        V.tensor_tensor(x_sq[:], x_cen[:], x_cen[:], ALU.mult).then_inc(s["squared"], 1)
                    elif kind == "var":
                        dve.wait_ge(*R.drained(kind, *key))
                        V.reciprocal(x_rstd[:], x_std[:]).then_inc(s["rstd"], 1)
                        dve.wait_ge(s["rstd"], key[0] + 1)
                        if key[0]:
                            dve.wait_ge(*R.filled("query", H - 1))
                        V.tensor_tensor(x_n[:], x_cen[:], x_rstd[:].unsqueeze(1).broadcast_to([128, KT, NT]), ALU.mult).then_inc(s["normed"], 1)
                    elif kind == "keyT":
                        j, b = key
                        cols = slice(b * LB, (b + 1) * LB)
                        dve.wait_ge(s["keyone"], 3 * j + b + 1)
                        V.tensor_tensor(kparts[DC:2 * DC, kdst(j), cols], acc[0:DC, 0:LB], kparts[0:DC, kdst(j), cols].bitcast(F32), ALU.subtract)\
                            .then_inc(*R.signal_drained(kind, *key))
                    elif kind == "qwide":
                        h, = key
                        src = acc[0:HALF, 0, 0:2 * NT].rearrange("p (a b) -> p a b", a=2)
                        dve.wait_ge(*R.filled(kind, *key))
                        if h >= 2:
                            dve.wait_ge(s["qrot"], 2 * (h - 1))
                        V.tensor_tensor(qa[:, h % 2, :, :], src, c["cosq"][:], ALU.mult).then_inc(s["qcos"], 1)
                        V.tensor_tensor(qb[:, h % 2, :, :], src, c["sinq"][:], ALU.mult).then_inc(*R.signal_drained(kind, *key))
                    elif kind == "query":
                        h, = key
                        cols = slice(h * S, (h + 1) * S)
                        src = acc[0:DC, 0, 0:NT] if reg < 2 else acc[0:DC, 0:NT]
                        dve.wait_ge(s["qhigh"], h + 1)
                        V.tensor_tensor(qlow[0:DC, :, cols], src.rearrange("p (j s) -> p j s", j=BG), qhigh[0:DC, :, cols].bitcast(F32), ALU.subtract)\
                            .then_inc(*R.signal_drained(kind, *key))
                    elif kind == "smax":
                        j, t, b = key
                        dve.wait_ge(*R.filled(kind, *key))
                        V.tensor_reduce(maxpart[:, j % 2, t, b:b + 1], acc[:, 0:LB], AX.X, ALU.max).then_inc(*R.signal_drained(kind, *key))
                    elif kind == "maxT":
                        j, = key
                        for b in range(3):
                            dve.wait_ge(*R.drained("smax", j, NMAX - 1, b))
                        V.tensor_reduce(maxneg[:, j % 2, :], maxpart[:, j % 2, :, :], AX.X, ALU.max, negate=True).then_inc(s["maxneg"], 1)
                    elif kind == "mix":
                        j, t = key
                        if t > POOL_TILES:
                            n_ = j * LT + t
                            dve.wait_ge(*R.drained("score", j, t))
                            dst = sum_dve[:, j % 2, :]
                            if t == POOL_TILES + 1:
                                if j >= 2:
                                    dve.wait_ge(*R.filled("norm", j - 2))
                                first_in = prob[:, (n_ - 1) % NPROB, :]
                            else:
                                dve.wait_ge(s["dve_sum"], (LT - POOL_TILES - 1) * j + t - POOL_TILES - 1)
                                first_in = dst
                            V.tensor_tensor(dst, first_in, prob[:, n_ % NPROB, :], ALU.add).then_inc(s["dve_sum"], 1)
                    elif kind == "norm":
                        j, = key
                        dve.wait_ge(*R.filled(kind, *key))
                        V.reciprocal(recip[:, j % 2, :], acc[:, 0:HQ]).then_inc(*R.signal_drained(kind, *key))
                        dve.wait_ge(*R.drained(kind, *key))
                        dve.wait_ge(s["mixed"], j + 1)
                        V.tensor_tensor(ctx_n[:, j, :], ctx_raw[:, j % 2, :], recip[:, j % 2, :], ALU.mult).then_inc(s["ctx_ready"], 1)
                    elif kind == "attn":
                        dve.wait_ge(*R.filled(kind, *key))
                        V.tensor_tensor(x_res[:], acc[:, :, 0:NT], x_in[:], ALU.add).then_inc(*R.signal_drained(kind, *key))
                    elif kind == "route" and layer == 0:
                        dve.wait_ge(*R.drained(kind))
                        then(V.tensor_scalar(rt2[:], rt1[:], 1.0, None, ALU.add))
                        then(V.reciprocal(score[:], rt2[:]))
                        then(V.tensor_tensor(rt1[:], score[:], c["bias0"][:].unsqueeze(1).broadcast_to([TR, 2, NE]), ALU.add))
                        quads = rt1[:].rearrange("p a (g b) -> p (a g) b", g=GRP0)
                        quad2 = rt2[:].rearrange("p a (g b) -> p (a g) b", g=GRP0)
                        quad3 = rt3[:].rearrange("p a (g b) -> p (a g) b", g=GRP0)
                        ranks(quads, 2 * GRP0, E0 // GRP0, c["tie4"], quad2)
                        then(V.tensor_scalar(rt2[:], rt2[:], 2.0, None, ALU.is_lt))
                        then(V.tensor_tensor(rt2[:], rt2[:], rt1[:], ALU.mult))
                        then(V.tensor_reduce(rg1[:].rearrange("p a g -> p (a g)"), quad2, AX.X, ALU.add))
                        ranks(rg1[:], 2, GRP0, c["tie4"], rg2[:])
                        then(V.tensor_scalar(rg2[:], rg2[:], 2.0, None, ALU.is_lt))
                        pick = rg2[:].rearrange("p a g -> p (a g)").unsqueeze(2).broadcast_to([TR, 2 * GRP0, E0 // GRP0])
                        then(V.tensor_tensor(quad3, quads, pick, ALU.mult))
                        then(V.tensor_scalar(rg2[:], rg2[:], 1.0, -NEG, ALU.subtract, ALU.mult))
                        then(V.tensor_tensor(quad3, quad3, pick, ALU.add))
                        ranks(rt3[:], 2, E0, c["tie16"], rt4[:])
                        then(V.tensor_scalar(rt4[:], rt4[:], float(TOP0), None, ALU.is_lt))
                        then(V.tensor_tensor(rt4[:], rt4[:], score[:], ALU.mult))
                        then(V.tensor_reduce(rs1[:], rt4[:], AX.X, ALU.add))
                        then(V.tensor_scalar(rs1[:], rs1[:], 1e-20, None, ALU.add))
                        then(V.reciprocal(rs2[:], rs1[:]))
                        then(V.tensor_tensor(rt4[:], rt4[:], rs2[:].unsqueeze(2).broadcast_to([TR, 2, NE]), ALU.mult))
                        V.tensor_scalar(cw[:], rt4[:], 2.5, None, ALU.mult).then_inc(s["routed"], 1)
                    elif kind == "route":
                        dve.wait_ge(*R.filled(kind))
                        V.tensor_copy(score[:], acc[0:TR, 0, 0:2 * NE].rearrange("p (a e) -> p a e", a=2)).then_inc(*R.signal_drained(kind))
                        dve.wait_ge(*R.drained(kind))
                        ranks(score[:], 2, NE, c["tie8"], rt1[:])
                        for slot in range(2):
                            then(V.tensor_scalar(mask[:, slot, :, :], rt1[:], float(slot), None, ALU.is_equal))
                            then(V.tensor_tensor(tokm[:, slot, :, :], mask[:, slot, :, :], score[:], ALU.mult))
                        then(V.tensor_copy(mask_rows.rearrange("p a b (e r) -> p (a b e) r", r=RANK),
                                           mask[:].rearrange("p a b e -> p (a b e)").unsqueeze(2).broadcast_to([TR, 4 * E1, RANK])))
                        V.tensor_reduce(tokw[:], tokm[:], AX.X, ALU.add).then_inc(s["routed"], 1)
                    elif kind == "tokw":
                        dve.wait_ge(*R.filled(kind))
                        v = acc[:, 0:2 * NT].rearrange("p (a s) -> p a s", s=S)
                        t3 = tok.rearrange("p a (j s) -> p (a j) s", s=S)
                        V.tensor_reduce(tokmax[:], v, AX.X, ALU.max).then_inc(s["tok_step"], 1)
                        dve.wait_ge(s["tok_step"], 1)
                        V.tensor_tensor(t3, v, tokmax[:].unsqueeze(2).broadcast_to([128, 2 * BG, S]), ALU.subtract).then_inc(s["tok_step"], 1)
                        dve.wait_ge(s["tok_exp"], 1)
                        then(V.tensor_reduce(tokmax[:], t3, AX.X, ALU.add))
                        then(V.reciprocal(tokmax[:], tokmax[:]))
                        V.tensor_tensor(tokc.rearrange("p a (j s) -> p (a j) s", s=S), t3,
                                        tokmax[:].unsqueeze(2).broadcast_to([128, 2 * BG, S]), ALU.mult).then_inc(*R.signal_drained(kind))
                    elif kind == "mask":
                        dve.wait_ge(*R.filled(kind))
                        V.tensor_copy(maskT, acc[:, 0:2 * NT].rearrange("p (a b) -> p a b", a=2)).then_inc(*R.signal_drained(kind))
                        dve.wait_ge(*R.drained(kind))
                        dve.wait_ge(*R.filled("lora"))
                        for half in range(2):
                            src = region[5][:, half * NT:(half + 1) * NT].unsqueeze(1).broadcast_to([128, 2, NT])
                            V.scalar_tensor_tensor(out=lora_in[:, half, :, :], in0=src, scalar=2.0, in1=maskT, op0=ALU.mult, op1=ALU.mult)\
                                .then_inc(s["lora_in"], 1)
                    elif kind == "gateup" and layer == 0:
                        i, = key
                        dve.wait_ge(s["gate_act"], i + 1)
                        if i == 0:
                            V.tensor_tensor(hid[:, 0, :], gact[:, 0, :], acc[:, 1, 0:NT], ALU.mult).then_inc(*R.signal_drained(kind, *key))
                    elif kind == "weight":
                        i, = key
                        up = region[i % 2][:, 1, 0:NT]
                        dve.wait_ge(*R.filled(kind, *key))
                        V.tensor_tensor(gact[:, i % 2, :], gact[:, i % 2, :], acc[:, 0:NT], ALU.mult).then_inc(*R.signal_drained(kind, *key))
                        dve.wait_ge(*R.drained(kind, *key))
                        if i >= 2:
                            dve.wait_ge(s["down_done"], i - 1)
                        V.tensor_tensor(hid[:, i % 2, :], gact[:, i % 2, :], up, ALU.mult).then_inc(*R.signal_drained("gateup", i))
                    elif kind == "gateup":
                        m, = key
                        M = min(128, HID - m * 128)
                        dve.wait_ge(s["gate_act"], m + 1)
                        V.tensor_tensor(sact[0:M, m % 2, :], sact[0:M, m % 2, :], acc[0:M, 1, 0:2 * NT], ALU.mult)\
                            .then_inc(*R.signal_drained(kind, *key))
                        dve.wait_ge(*R.drained(kind, *key))
                        if m >= 2:
                            dve.wait_ge(s["down_done"], m - 1)
                            dve.wait_ge(s["acc_done"], m - 1)
                        V.tensor_tensor(hid[0:M, m % 2, :], sact[0:M, m % 2, :], tokc.rearrange("p a b -> p (a b)")[0:M, :], ALU.mult)\
                            .then_inc(s["hid_ready"], 1)
                    elif kind == "loradown":
                        dve.wait_ge(s["down_done"], MT)
                        V.scalar_tensor_tensor(out=lora_z, in0=region[3][:, 0:2 * NT].rearrange("p (a b) -> p a b", a=2), scalar=2.0,
                                               in1=maskT, op0=ALU.mult, op1=ALU.mult).then_inc(s["lora_z"], 1)
                    elif kind == "out":
                        dve.wait_ge(s["down_done"], E0 + 1 if layer == 0 else MT + 1)
                        for q in range(KT):
                            V.tensor_tensor(x_cen[:, q, :], region[(2, (5, 4)[layer])[q]][:, 0:NT], x_res[:, q, :], ALU.add)\
                                .then_inc(s["out_ready"], 1)
        nc.all_engine_barrier(sems_to_clear=group_range)


def kernel(**inputs):
    import concourse.bacc as bacc
    from concourse.bass_utils import run_bass_kernel_spmd

    def arr(x):
        return np.ascontiguousarray(np.asarray(x))

    x = arr(inputs["x"]).reshape(G, NT, KT, 128).transpose(0, 3, 2, 1)
    d = {"x": np.concatenate([x, np.zeros_like(x[:1])])}
    ctx = arr(inputs["ctx_512"]).reshape(B, LP, LT * DC)
    d["ctx"] = np.concatenate([ctx, np.zeros_like(ctx[:1])])
    d["cosk"], d["sink"], d["cosq"], d["sinq"] = rope_tables()
    d["ident"] = np.eye(128, dtype=np.float32)
    d["tie4"], d["tie8"], d["tie16"] = before_masks(4), before_masks(8), before_masks(16)
    d["bias"] = arr(inputs["L0_ffn_expert_bias"]).reshape(1, E0)
    for n in range(2):
        p = f"L{n}_xattn_"
        d[f"wq{n}"] = arr(inputs[p + "Wq"])
        d[f"kcq{n}"] = arr(inputs[p + "w_kc_q"])
        d[f"kckv{n}"] = arr(inputs[p + "w_kc_kv"])
        d[f"wo{n}"] = arr(inputs[p + "Wo"]).T
        d[f"wqr{n}"] = arr(inputs[p + "W_qr"]).transpose(2, 0, 1)
        d[f"wkr{n}"] = arr(inputs[p + "W_kr"]).transpose(2, 0, 1)
    d["router0"] = arr(inputs["L0_ffn_gate_weight"]).T
    d["router1"] = arr(inputs["L1_ffn_gate_w"]).T

    def expert(gate, up, down):
        parts = [m.T.reshape(KT, 128, I0).transpose(1, 0, 2).reshape(128, KT * I0) for m in (gate, up)]
        return np.concatenate(parts + [down.T], axis=1)

    q = "L0_ffn_"
    gate, up, down = (arr(inputs[q + f"{m}_proj"]) for m in ("gate", "up", "down"))
    shared = expert(*(arr(inputs[q + f"shared_{m}"]) for m in ("gate", "up", "down")))
    d["experts"] = np.stack([shared] + [expert(gate[e], up[e], down[e]) for e in range(E0)])
    q = "L1_ffn_"
    d["f_up"], d["f_gate"] = arr(inputs[q + "w_up"]).T, arr(inputs[q + "w_gate"]).T
    d["f_down"] = arr(inputs[q + "w_down"]).T
    d["f_upA"], d["f_gateA"] = (arr(inputs[q + m]).reshape(E1 * RANK, D).T for m in ("up_A", "gate_A"))
    d["f_upB"], d["f_gateB"] = (arr(inputs[q + m]).transpose(0, 2, 1).reshape(E1 * RANK, HID) for m in ("up_B", "gate_B"))
    d["f_downA"] = arr(inputs[q + "down_A"]).reshape(E1 * RANK, HID).T
    d["f_downB"] = arr(inputs[q + "down_B"]).transpose(0, 2, 1).reshape(E1 * RANK, D)

    nc = bacc.Bacc("TRN2", target_bir_lowering=False, num_devices=1)
    arrays, aps = {}, {}
    for name, v in d.items():
        arrays["in_" + name] = np.ascontiguousarray(v)
        aps[name] = nc.dram_tensor("in_" + name, v.shape, mybir.dt.from_np(v.dtype), kind="ExternalInput").ap()
    out = nc.dram_tensor("out_x", [G, 128, KT, NT], F32, kind="ExternalOutput").ap()
    x_mid = nc.dram_tensor("x_mid", [G + 1, 128, KT, NT], F32).ap()
    build_program(nc, aps, out, x_mid)
    r = run_bass_kernel_spmd(nc, [arrays], core_ids=[0])
    y = r.results[0]["out_x"]
    return np.ascontiguousarray(y.transpose(0, 3, 2, 1)).reshape(B, S, D)
```

```python
from contextlib import ExitStack

import concourse.bass as bass
import numpy as np
from concourse import mybir

ALU = mybir.AluOpType
ACT = mybir.ActivationFunctionType
AX = mybir.AxisListType
F32 = mybir.dt.float32
F32R = mybir.dt.float32r

B, S, L, D = 32, 56, 1500, 256
H, HK, DC, DCQ, DR = 16, 128, 64, 192, 64
BG = 8
G = B // BG
NT = BG * S
NQ = H * S
HQ = NQ // 2
LT, LP = 12, 125
LB = L // 3
KT = D // 128
HALF = DCQ // 2
NMAX = NQ // 128
NPROB = 4
POOL_TILES, POOL_LAST = 10, 5
E0, TOP0, GRP0 = 16, 4, 4
E1, RANK = 8, 16
I0 = 128
HID = 704
MT = -(-HID // 128)
SMAX_PACE = (0, 0, 2, 2, 3, 3, 3, 3, 3, 2, 0, 0)
RT = NT // 112
TR = NT // RT
NEG = -3.0e38
EPS = 1e-5
WSLOT = 4
HSLOTS = (4, 6)
SPLIT_AHEAD = 2


def head_rows(t):
    return (128 * t + 127) // S


def pool_tiles(j):
    return POOL_TILES if j < BG - 1 else POOL_LAST


def pool_sums(j):
    return j * (POOL_TILES - 1)


def vector_sums(j):
    return sum(LT - pool_tiles(i) for i in range(j))


def schedule(layer):
    steps = []
    spin = [0]

    def add(kind, *key, region=None):
        steps.append((kind, key, region))

    def turn():
        spin[0] += 1
        return 3 + (spin[0] - 1) % 3

    def keys(j):
        for c in range(3):
            add("keyT", j, c, region=turn())

    def maxima(j, tiles):
        for t in tiles:
            for c in range(3):
                add("smax", j, t, c, region=turn())

    for h in range(SPLIT_AHEAD):
        add("wsplit", h)
    add("rotate", 0)
    add("mean", 0, region=2)
    add("rope", 0)
    add("var", 0, region=5)
    add("xsplit", 0)
    add("rotate", 1)
    add("rope", 1)
    spin[0] = 0
    keys(0)
    done = 0
    ahead = 3 if layer == 0 else 2
    for h in range(H + ahead):
        if h + SPLIT_AHEAD < H:
            add("wsplit", h + SPLIT_AHEAD)
        if layer == 0:
            if h < H:
                add("qwide", h, region=h % 2)
            if 2 <= h < H + 2:
                add("query", h - 2, region=2)
        elif h < H:
            add("query", h, region=h % 3)
        while done < NMAX and head_rows(done) <= h - ahead:
            maxima(0, [done])
            done += 1
    maxima(0, range(done, NMAX))
    add("maxneg", 0)
    add("maxT", 0, region=turn())
    last = None
    for c in range(3):
        add("kone", 0, c)
    for j in range(BG):
        ahead = [(row, c) for row in range(NMAX) for c in range(3)] if j + 1 < BG else []
        for t in range(LT):
            if t == 0 and j + 2 < BG:
                add("rotate", j + 2)
            if t == 1 and j:
                add("kone", j, 2)
            if t in (5, 9) and j + 1 < BG:
                add("kone", j + 1, t // 4 - 1)
            add("score", j, t, region=t % 2)
            if last is not None:
                add("mix", *last)
                if last[1] == LT - 1:
                    add("context", last[0])
            last = (j, t)
            if j + 1 < BG and t == 0:
                keys(j + 1)
            if t == 1 and j:
                add("norm", j - 1, region=turn())
            if t in (1, 2, 3) and j:
                add("share", j - 1, t - 1)
            for _ in range(SMAX_PACE[t]):
                if ahead:
                    row, c = ahead.pop(0)
                    add("smax", j + 1, row, c, region=turn())
            if j + 1 < BG:
                if t == 9:
                    add("maxneg", j + 1)
                if t == 10:
                    add("maxT", j + 1, region=turn())
            if t == 10 and j + 2 < BG:
                add("rope", j + 2)
        assert not ahead
    add("mix", *last)
    add("context", BG - 1)
    add("norm", BG - 1, region=turn())
    for part in range(3):
        add("share", BG - 1, part)
    add("attn", region=0)
    add("mean", 1, region=2)
    add("var", 1, region=5)
    add("xsplit", 1)
    add("route", region=1)
    if layer == 0:
        for i in range(2):
            add("esplit", i)
        add("gateup", 0, region=0)
        add("cwT", region=3)
        for i in range(E0 + 1):
            if i:
                add("gateup", i, region=i % 2)
                add("weight", i, region=3 + i % 2)
                add("down", i - 1)
            if i + 2 <= E0:
                add("esplit", i + 2)
            add("hidden", i)
        add("down", E0)
    else:
        add("lora", region=0)
        add("mask", region=1)
        add("tokw", region=1)
        for m in range(MT):
            for slot in range(2):
                add("gateup", m, slot, region=slot)
            if m:
                add("down", m - 1)
        add("down", MT - 1)
        add("loradown")
    add("out")
    return steps


class Regions:

    def __init__(self, steps, filled, drained):
        self.full, self.empty, self.at, self.before = filled, drained, {}, {}
        used = [0] * len(filled)
        for kind, key, region in steps:
            if region is not None:
                self.before[kind, key] = (region, used[region])
                used[region] += 1
                self.at[kind, key] = (region, used[region])
        self.used = used

    def room(self, eng, kind, *key):
        r, n = self.before[kind, key]
        if n:
            eng.wait_ge(self.empty[r], n)

    def filled(self, kind, *key):
        r, n = self.at[kind, key]
        return self.full[r], n

    def drained(self, kind, *key):
        r, n = self.at[kind, key]
        return self.empty[r], n

    def signal_filled(self, kind, *key):
        return self.full[self.at[kind, key][0]], 1

    def signal_drained(self, kind, *key):
        return self.empty[self.at[kind, key][0]], 1


def rope_tables():
    def table(n, dim):
        inv = (1.0 / 10000.0 ** (np.arange(0, dim, 2, dtype=np.float32) / np.float32(dim))).astype(np.float32)
        f = np.arange(n, dtype=np.float32)[:, None] * inv[None, :]
        return np.repeat(np.sin(f), 2, axis=-1), np.repeat(np.cos(f), 2, axis=-1)
    sk, ck = table(L, DC)
    sk = np.concatenate([-sk[:, :DC // 2], sk[:, DC // 2:]], axis=1)
    sq, cq = table(S, DCQ)
    lay = lambda a: np.tile(a.T, (1, BG))
    cosq = np.stack([lay(cq[:, :HALF]), lay(cq[:, HALF:])], axis=1)
    sinq = np.stack([lay(sq[:, HALF:]), -lay(sq[:, :HALF])], axis=1)
    return (ck.reshape(LP, LT * DC).astype(np.float32), sk.reshape(LP, LT * DC).astype(np.float32),
            np.ascontiguousarray(cosq, np.float32), np.ascontiguousarray(sinq, np.float32))


def before_masks(n):
    return np.tril(np.ones((n, n), np.float32), -1).reshape(1, n * n)


def build_program(nc, a, scratch, out, x_mid):
    top = ExitStack()
    with top:
        def sb(name, shape, dt=F32, stack=top):
            return stack.enter_context(nc.sbuf_tensor(name, shape, dt))

        wide = [top.enter_context(nc.psum_tensor(f"wide{i}", [128, 2, 512], F32)) for i in range(2)]
        single = [top.enter_context(nc.psum_tensor(f"single{i}", [128, 512], F32)) for i in range(4)]
        region = wide + single
        mix_acc = region[2]

        ident = sb("ident", [128, 128])
        ones = sb("ones", [128, DC])
        mean_w = sb("mean_w", [128, 128])
        eps = sb("eps", [128, 1])
        cosk = sb("cosk", [LP, LT, DC])
        sink = sb("sink", [LP, LT, DC])
        tie4 = sb("tie4", [TR, 16])
        tie8 = sb("tie8", [TR, 64])
        tie16 = sb("tie16", [TR, 256])
        bias0 = sb("bias0", [TR, E0])
        pick = sb("pick", [32 + E0, E0], F32R)

        s_names = ["load", "setup_full", "setup_const"] + [f"setup_copied_{i}" for i in range(2)]
        setup_sems = {n: top.enter_context(nc.semaphore(n)) for n in s_names}
        group_names = (
            [f"filled_{i}" for i in range(6)] + [f"drained_{i}" for i in range(6)]
            + [f"ctx_loaded_{j}" for j in range(1, BG)] + [f"weights_loaded_{i}" for i in range(WSLOT)] + [f"head_loaded_{i}" for i in range(max(HSLOTS))] + [f"second_loaded_{i}" for i in range(HSLOTS[0])] + ["ffn_loaded", "next_loaded", "stored", "rope_cos", "rope_sin", "rope_done", "keyh", "keyone",
               "centred", "squared", "std", "rstd", "normed", "qcos", "qrot", "qhigh", "mixed", "pool_sum", "dve_sum",
               "maxneg", "shift_loaded", "w_high", "w_low", "x_high", "x_low", "e_high", "e_low", "cw_high", "hid_high", "hid_low", "lora_high", "lora_low",
               "ffn_high", "ffn_low", "gate_up", "recip", "ctx_ready", "route_step", "routed", "gate_act",
               "hid_ready", "down_done", "acc_done", "lora_in", "tok_step",
               "tok_exp", "mask_ready", "lora_acc", "lora_z", "out_ready", "premix"])
        sems = {n: top.enter_context(nc.semaphore(n)) for n in group_names}
        nums = [s.num for s in sems.values()]
        group_range = range(min(nums), max(nums) + 1)
        setup_nums = [s.num for s in setup_sems.values()]
        setup_range = range(min(setup_nums), max(setup_nums) + 1)
        assert len(group_range) == len(nums) and len(setup_range) == len(setup_nums)

        with nc.Block() as block:
            load = setup_sems["load"]

            @block.sync
            def _(sp):
                for dst, name in ((cosk, "cosk"), (sink, "sink")):
                    sp.dma_start(dst[:].rearrange("p a b -> p (a b)"), a[name]).then_inc(load, 16)
                sp.dma_start(ident[:], a["ident"]).then_inc(load, 16)
                for dst, name in ((tie4, "tie4"), (tie8, "tie8"), (tie16, "tie16"), (bias0, "bias")):
                    src = a[name]
                    sp.dma_start(dst[:], src.broadcast_to([TR, src.shape[1]])).then_inc(load, 16)
                sp.wait_ge(load, 7 * 16)

            @block.vector
            def _(dve):
                nc.vector.memset(ones[:], 1.0)
                nc.vector.memset(mean_w[:], 1.0 / D)
                nc.vector.memset(eps[:], EPS)
                nc.vector.memset(pick[:].bitcast(F32), 0.0).then_inc(setup_sems["setup_const"], 1)
                dve.wait_ge(setup_sems["setup_const"], 1)
                dve.wait_ge(load, 7 * 16)
                for r in (0, 32):
                    nc.vector.tensor_copy(pick[r:r + E0, :], ident[r:r + E0, r:r + E0])
        nc.all_engine_barrier(sems_to_clear=setup_range)

        merge_weights(nc, a, scratch, region, setup_sems, setup_range, sb)
        for layer in range(2):
            with ExitStack() as work:
                run_layer(nc, layer, a, scratch, x_mid, out, sems, group_range, setup_sems, setup_range, sb, work,
                          region, mix_acc,
                          dict(ident=ident, ones=ones, mean_w=mean_w, eps=eps, cosk=cosk, sink=sink, tie4=tie4,
                               tie8=tie8, tie16=tie16, bias0=bias0, pick=pick))


def merge_weights(nc, a, scratch, region, sems, sems_range, sb):
    load, full, copied = sems["load"], sems["setup_full"], [sems["setup_copied_0"], sems["setup_copied_1"]]
    banks = [region[0][:, 0, :], region[0][:, 1, :], region[1][:, 0, :], region[1][:, 1, :]] + [region[i][:, :] for i in range(2, 6)]

    def raw_weights(n, stack):
        buf = lambda name, shape: sb(f"{name}_raw{n}", shape, stack=stack)
        r = dict(wq=buf("wq", [128, H, D]), kcq=buf("kcq", [128, H, DCQ]), kckv=buf("kckv", [128, H, DC]),
                 wo=buf("wo", [128, H, D]), wqr=buf("wqr", [DR, H, DCQ]), wkr=buf("wkr", [DR, H, DC]))
        loads = [(r["wqr"][:], a[f"wqr{n}"]), (r["wkr"][:], a[f"wkr{n}"]),
                 (r["wq"][:], a[f"wq{n}"].rearrange("(h k) f -> k h f", k=HK)),
                 (r["kcq"][:], a[f"kcq{n}"].rearrange("h k q -> k h q")),
                 (r["kckv"][:], a[f"kckv{n}"].rearrange("h k d -> k h d")),
                 (r["wo"][:], a[f"wo{n}"].rearrange("(h k) f -> k h f", k=HK))]
        return r, loads

    def multiply(layer, r, m, loads, later, stores):
        items = []
        for h in range(H):
            items += [("w2", h, c) for c in range(2)]
            items += [("w1" if layer == 0 else "w1t", h, c) for c in range(2)]
            items.append(("wvo", h, 0))
        if layer == 1:
            items += [("wabs", h, c) for h in range(H) for c in range(2)]

        def place(item):
            kind, h, c = item
            if kind == "wvo":
                p = 64 * (h // (H // 2))
                return m["wvo"][p:p + DC, h % (H // 2), :], (p, p + DC), D
            rows, width = {"w2": (HALF, 2 * DC), "w1": (128, DCQ), "w1t": (HALF, D), "wabs": (128, 2 * DC)}[kind]
            return m[kind][:, c, h, :], (0, rows), width

        with nc.Block() as block:
            @block.sync
            def _(sp):
                for dst, src in loads + later:
                    sp.dma_start(dst, src).then_inc(load, 16)
                for k in range(2):
                    sp.wait_ge(copied[k], (len(items) + 1 - k) // 2)
                for dst, src in stores:
                    sp.dma_start(dst, src).then_inc(load, 16)
                sp.wait_ge(load, 16 * (len(loads) + len(later) + len(stores)))

            @block.tensor
            def _(pe):
                pe.wait_ge(load, 16 * len(loads + later))
                for i, (kind, h, c) in enumerate(items):
                    bank = banks[i % 8]
                    if i >= 8:
                        pe.wait_ge(copied[i % 2], (i - 8) // 2 + 1)
                    if kind == "wabs" and h == 0 and c == 0:
                        for k in range(2):
                            pe.wait_ge(copied[k], (i + 1 - k) // 2)
                    if kind == "w2":
                        mm = pe.matmul(bank[0:HALF, 0:2 * DC], r["wqr"][:, h, c * HALF:(c + 1) * HALF],
                                       r["wkr"][:, h, :].unsqueeze(1).broadcast_to([DR, 2, DC]), start=True, stop=True)
                    elif kind == "w1":
                        mm = pe.matmul(bank[:, 0:DCQ], r["wq"][:, h, c * 128:(c + 1) * 128], r["kcq"][:, h, :], start=True, stop=True)
                    elif kind == "w1t":
                        mm = pe.matmul(bank[0:HALF, 0:D], r["kcq"][:, h, c * HALF:(c + 1) * HALF], r["wq"][:, h, :], start=True, stop=True)
                    elif kind == "wvo":
                        p = 64 * (h // (H // 2))
                        mm = pe.matmul(bank[p:p + DC, 0:D], r["kckv"][:, h, :], r["wo"][:, h, :], start=True, stop=True)
                    else:
                        for k in range(2):
                            mm = pe.matmul(bank[:, 0:2 * DC], m["w1t"][:, k, h, c * 128:(c + 1) * 128], m["w2"][:, k, h, :],
                                           start=(k == 0), stop=(k == 1))
                    mm.then_inc(full, 1)

            def copies(eng, k, copy):
                for i, item in enumerate(items):
                    if i % 2 == k:
                        dst, (p, q), width = place(item)
                        eng.wait_ge(full, i + 1)
                        copy(dst, banks[i % 8][p:q, 0:width]).then_inc(copied[k], 1)

            @block.scalar
            def _(act):
                copies(act, 0, lambda dst, src: nc.scalar.activation(dst, src, ACT.Copy))

            @block.vector
            def _(dve):
                copies(dve, 1, nc.vector.tensor_copy)
        nc.all_engine_barrier(sems_to_clear=sems_range)

    with ExitStack() as stack1:
        raw1, loads1 = raw_weights(1, stack1)
        with ExitStack() as stack0:
            raw0, loads0 = raw_weights(0, stack0)
            m = {"w1": sb("w1", [128, KT, H, DCQ], stack=stack0), "w2": sb("w2_0", [HALF, 2, H, 2 * DC], stack=stack0),
                 "wvo": sb("wvo_0", [128, H // 2, D], stack=stack0)}
            multiply(0, raw0, m, loads0, loads1,
                     [(scratch["w1"].rearrange("h p (k q) -> p k h q", k=KT), m["w1"][:]),
                      (scratch["w2"].rearrange("h p (k q) -> p k h q", k=2), m["w2"][:]),
                      (scratch["wvo"][0], m["wvo"][:].rearrange("p h f -> p (h f)"))])
        with ExitStack() as stack0:
            m = {"w1t": sb("w1t", [HALF, 2, H, D], stack=stack0), "w2": sb("w2_1", [HALF, 2, H, 2 * DC], stack=stack0),
                 "wabs": sb("wabs", [128, KT, H, 2 * DC], stack=stack0), "wvo": sb("wvo_1", [128, H // 2, D], stack=stack0)}
            multiply(1, raw1, m, [], [],
                     [(scratch["wabs"].rearrange("h p (k q) -> p k h q", k=KT), m["wabs"][:]),
                      (scratch["wvo"][1], m["wvo"][:].rearrange("p h f -> p (h f)"))])


def run_layer(nc, layer, a, scratch, x_mid, out, sems, group_range, setup_sems, setup_range, sb, stack, region, mix_acc, c):
    n = str(layer)

    def buf(name, shape, dt=F32):
        return sb(name + n, shape, dt, stack=stack)

    def split_in_place(name, shape, where=stack):
        with ExitStack() as first_use:
            values = sb(name + "_values" + n, shape, stack=first_use)
        return values, sb(name + n, shape, F32R, stack=where)

    NE = E0 if layer == 0 else E1
    HSLOT = HSLOTS[layer]
    w = {"wvo": buf("wvo", [128, H // 2, D]), "router": buf("router", [128, KT, NE])}
    raw = buf("raw", [LP, 2, LT, DC])
    rope_c = buf("rope_c", [LP, LT, DC])
    rope_s = buf("rope_s", [LP, LT, DC])
    kv = buf("kv", [LP, 3, LT, DC])
    kparts = buf("kparts", [128, 2, L], F32R)
    kones = buf("kones", [DC + 1, L], F32R)
    ctx_raw = buf("ctx_raw", [128, 2, HQ])
    recip = buf("recip", [128, HQ])
    total = buf("total", [128, HQ])
    ctx_n = buf("ctx_n", [128, BG, HQ])
    maxpart = buf("maxpart", [128, 2, NMAX, 3])
    maxneg = buf("maxneg", [128, 2, NMAX])
    maxrow = buf("maxrow", [NMAX, 2, 128], F32R)
    x_in = buf("x_in", [128, KT, NT])
    x_cen = buf("x_cen", [128, KT, NT])
    x_std = buf("x_std", [128, NT])
    x_rstd = buf("x_rstd", [128, NT])
    x_n = buf("x_n", [128, KT, NT])
    x_sq = x_n
    x_res = buf("x_res", [128, KT, NT])
    x_high = buf("x_high", [128, KT, NT], F32R)
    x_low = buf("x_low", [128, KT, NT], F32R)
    if layer == 0:
        cosq = buf("cosq", [HALF, 2, NT])
        sinq = buf("sinq", [HALF, 2, NT])
        w_in, w_low = split_in_place("w_low", [128, HSLOT, KT, DCQ])
        w_high = buf("w_high", [128, HSLOT, KT, DCQ], F32R)
        w2 = buf("w2", [HALF, HSLOT, 2, 2 * DC])
    else:
        with ExitStack() as making_queries:
            w_in, w_low = split_in_place("w_low", [128, HSLOT, KT, 2 * DC], making_queries)
            w_high = sb("w_high" + n, [128, HSLOT, KT, 2 * DC], F32R, stack=making_queries)
    with ExitStack() as attention:
        prob = sb("prob" + n, [LP, NPROB, NQ], stack=attention)
        sum_pool = sb("sum_pool" + n, [LP, 2, NQ], stack=attention)
        sum_dve = sb("sum_dve" + n, [LP, NQ], stack=attention)
        qhigh = sb("qhigh" + n, [128, BG, NQ], F32R, stack=attention)
        qlow = sb("qlow" + n, [DC + 1, BG, NQ], F32R, stack=attention)
    if layer == 0:
        qa = prob[0:HALF, 0:2, :].rearrange("p h (a b) -> p h a b", a=2)
        qb = prob[0:HALF, 2:4, :].rearrange("p h (a b) -> p h a b", a=2)
        qr = sum_pool[0:HALF, :, :].rearrange("p h (a b) -> p h a b", a=2)
        gact = buf("gact", [128, 2, NT])
        hid = buf("hid", [128, 2, NT])
        hid_high = buf("hid_high", [128, 2, NT], F32R)
        hid_low = buf("hid_low", [128, 2, NT], F32R)
        cwT = buf("cwT", [32 + E0, NT], F32R)
    else:
        sact = buf("sact", [128, 2, NT])
        hid = buf("hid", [128, 2, 2, NT])
        gate_up = buf("gate_up", [128, 2, NT])
        hsum = buf("hsum", [128, 2, NT])
        mask_rows = buf("mask_rows", [TR, 2, RT, 128])
        tokmax = buf("tokmax", [128, 2 * BG])
        tokw = buf("tokw", [TR, 2, RT])
        mask = buf("mask", [TR, 2, RT, E1])
        tokm = buf("tokm", [TR, 2, RT, E1])
    score = buf("score", [TR, RT, NE])
    rt1 = buf("rt1", [TR, RT, NE])
    rt2 = buf("rt2", [TR, RT, NE])
    rt3 = buf("rt3", [TR, RT, NE])
    rt4 = buf("rt4", [TR, RT, NE])
    rg1 = buf("rg1", [TR, RT, GRP0])
    rg2 = buf("rg2", [TR, RT, GRP0])
    rs1 = buf("rs1", [TR, RT])
    rs2 = buf("rs2", [TR, RT])
    cw = buf("cw", [TR, RT, NE])
    cmp1 = buf("cmp1", [TR, RT * NE * NE])
    cmp2 = buf("cmp2", [TR, RT * NE * NE])
    ffn_loads = []
    if layer == 0:
        wexp_in, wexp_low = split_in_place("wexp_low", [128, WSLOT, 3 * D])
        wexp_high = buf("wexp_high", [128, WSLOT, 3 * D], F32R)
    else:
        lora_high = buf("lora_high", [128, 2, 2, NT], F32R)
        lora_in, lora_low = split_in_place("lora_low", [128, 2, 2, NT])
        tok = buf("tok", [128, 2, NT])
        tokc = buf("tokc", [128, 2, NT])
        maskT = buf("maskT", [128, 2, NT])
        mask_diff = buf("mask_diff", [128, NT])
        lora_z = tok
        for name, shape in (("upA", [128, KT, 128]), ("gateA", [128, KT, 128]), ("up", [128, KT, HID]), ("gate", [128, KT, HID])):
            w[name + "_in"], w[name] = split_in_place("w_" + name, shape)
            w[name + "_high"] = buf(f"w_{name}_high", shape, F32R)
            ffn_loads.append((w[name + "_in"][:], a["f_" + name].rearrange("(k p) e -> p k e", p=128)))
        for name in ("upB", "gateB"):
            w[name + "_in"], w[name] = split_in_place("w_" + name, [128, HID])
            w[name + "_high"] = buf(f"w_{name}_high", [128, HID], F32R)
            ffn_loads.append((w[name + "_in"][:], a["f_" + name]))
        w["downB"] = buf("w_downB", [128, D])
        ffn_loads.append((w["downB"][:], a["f_downB"]))
        whole = HID // 128
        for name, width in (("down", D), ("downA", 128)):
            w[name] = buf("w_" + name, [128, MT, width])
            src = a["f_" + name]
            ffn_loads.append((w[name][:, 0:whole, :], src[0:whole * 128, :].rearrange("(m p) e -> p m e", p=128)))
            ffn_loads.append((w[name][0:HID - whole * 128, whole, :], src[whole * 128:HID, :]))
        split_names = ("upA", "gateA", "up", "gate", "upB", "gateB")

    x_src = a["x"] if layer == 0 else x_mid
    x_dst = x_mid if layer == 0 else out
    steps = schedule(layer)
    R = Regions(steps, [sems[f"filled_{i}"] for i in range(6)], [sems[f"drained_{i}"] for i in range(6)])
    s = sems

    def kdst(j):
        return j % 2

    with nc.Block() as block:
        @block.sync
        def _(sp):
            sp.dma_start(x_in[:], x_src[0]).then_inc(setup_sems["load"], 16)
            sp.dma_start(raw[:, 0, :, :].rearrange("p t d -> p (t d)"), a["ctx"][0]).then_inc(setup_sems["load"], 16)
            more = [(w["wvo"][:].rearrange("p h f -> p (h f)"), scratch["wvo"][layer]),
                    (w["router"][:], a[f"router{n}"].rearrange("(k p) e -> p k e", p=128))]
            if layer == 0:
                more += [(cosq[:], a["cosq"]), (sinq[:], a["sinq"])]
            for dst, src in more:
                sp.dma_start(dst, src).then_inc(setup_sems["load"], 16)
            sp.wait_ge(setup_sems["load"], 32 + 16 * len(more))
            if layer == 0:
                sp.dma_start(x_mid[G], x_in[:]).then_inc(setup_sems["load"], 16)
                sp.wait_ge(setup_sems["load"], 48 + 16 * len(more))

        @block.vector
        def _(dve):
            nc.vector.memset(kones[DC:DC + 1, :].bitcast(F32), 1.0)
    nc.all_engine_barrier(sems_to_clear=setup_range)

    with nc.Fori(0, G) as g:
        with nc.Block() as block:
            @block.sync
            def _(sp):
                def weights_of(i):
                    if i >= WSLOT:
                        sp.wait_ge(s["down_done"], i - WSLOT + 1)
                    sp.dma_start(wexp_in[:, i % WSLOT, :], a["experts"][i]).then_inc(s[f"weights_loaded_{i % WSLOT}"], 16)

                sp.dma_start(raw[:, 1, :, :].rearrange("p t d -> p (t d)"), a["ctx"][BG * g + 1]).then_inc(s["ctx_loaded_1"], 16)

                def head_weights(h):
                    source = scratch["w1" if layer == 0 else "wabs"][h]
                    sp.dma_start(w_in[:, h % HSLOT, :, :].rearrange("p k q -> p (k q)"), source).then_inc(s[f"head_loaded_{h % HSLOT}"], 16)

                def second_weights(h):
                    sp.dma_start(w2[:, h % HSLOT, :, :].rearrange("p k q -> p (k q)"), scratch["w2"][h]).then_inc(s[f"second_loaded_{h % HSLOT}"], 16)

                for h in range(HSLOT):
                    head_weights(h)
                if layer == 0:
                    for h in range(HSLOT):
                        second_weights(h)
                for kind, key, _ in steps:
                    if kind == ("qwide", "query")[layer] and key[0] + HSLOT < H:
                        sp.wait_ge(*R.filled(kind, key[0]))
                        head_weights(key[0] + HSLOT)
                    if kind == "query" and layer == 0 and key[0] + HSLOT < H:
                        sp.wait_ge(*R.filled("query", key[0]))
                        second_weights(key[0] + HSLOT)
                    if kind == "rope" and key[0] + 2 <= BG:
                        j = key[0] + 2
                        sp.wait_ge(s["rope_done"], key[0] + 1)
                        sem = s[f"ctx_loaded_{j}"] if j < BG else s["next_loaded"]
                        sp.dma_start(raw[:, j % 2, :, :].rearrange("p t d -> p (t d)"), a["ctx"][BG * g + j]).then_inc(sem, 16)
                    if kind == "maxT":
                        j, = key
                        sp.wait_ge(*R.drained("maxT", j))
                        sp.dma_start(qlow[DC:DC + 1, j, :].bitcast(F32), maxrow[:, j % 2, :].bitcast(F32)).then_inc(s["shift_loaded"], 16)
                    if kind == "attn":
                        sp.wait_ge(*R.filled("norm", BG - 1))
                        if layer == 0:
                            for i in range(WSLOT):
                                weights_of(i)
                        for dst, src in ffn_loads:
                            sp.dma_start(dst, src).then_inc(s["ffn_loaded"], 16)
                        sp.wait_ge(*R.drained("attn"))
                        sp.dma_start(x_in[:], x_src[g + 1]).then_inc(s["next_loaded"], 16)
                if layer == 0:
                    for i in range(WSLOT, E0 + 1):
                        weights_of(i)
                sp.wait_ge(s["out_ready"], 2)
                sp.dma_start(x_dst[g], x_cen[:]).then_inc(s["stored"], 16)
                sp.wait_ge(s["next_loaded"], 32)
                sp.wait_ge(s["stored"], 16)

            @block.tensor
            def _(pe):
                def split_product(dst, w_hi, w_lo, x_hi, x_lo, start, stop):
                    pe.matmul(dst, w_hi, x_hi, start=start, stop=False)
                    pe.matmul(dst, w_lo, x_hi, start=False, stop=False)
                    return pe.matmul(dst, w_hi, x_lo, start=False, stop=stop)

                for kind, key, reg in steps:
                    if reg is not None:
                        R.room(pe, kind, *key)
                        acc = region[reg]
                    if kind == "mean":
                        src = x_in if key[0] == 0 else x_res
                        if key[0]:
                            pe.wait_ge(*R.drained("attn"))
                        for k in range(KT):
                            mm = pe.matmul(acc[:, 0:NT], c["mean_w"][:], src[:, k, :], start=(k == 0), stop=(k == KT - 1))
                        mm.then_inc(*R.signal_filled(kind, *key))
                    elif kind == "var":
                        pe.wait_ge(s["squared"], key[0] + 1)
                        for k in range(KT):
                            mm = pe.matmul(acc[:, 0:NT], c["mean_w"][:], x_sq[:, k, :], start=(k == 0), stop=(k == KT - 1))
                        mm.then_inc(*R.signal_filled(kind, *key))
                    elif kind == "keyT":
                        j, b = key
                        pe.wait_ge(s["rope_done"], j + 1)
                        for i in range(4):
                            mm = pe.transpose(acc[0:DC, i * LP:(i + 1) * LP], kv[:, j % 3, 4 * b + i, :], c["ident"][0:LP, 0:LP])
                        mm.then_inc(*R.signal_filled(kind, *key))
                    elif kind == "qwide":
                        h, = key
                        if h == 0:
                            pe.wait_ge(s["x_low"], 1)
                        pe.wait_ge(s["w_low"], h + 1)
                        for half in range(2):
                            cols = slice(half * HALF, (half + 1) * HALF)
                            for k in range(KT):
                                mm = split_product(acc[0:HALF, half, 0:NT], w_high[:, h % HSLOT, k, cols], w_low[:, h % HSLOT, k, cols],
                                                   x_high[:, k, :], x_low[:, k, :], k == 0, k == KT - 1)
                        mm.then_inc(*R.signal_filled(kind, *key))
                    elif kind == "query":
                        h, = key
                        dst = acc[:, 0, 0:NT] if reg < 2 else acc[:, 0:NT]
                        if layer == 0:
                            pe.wait_ge(s["qrot"], 2 * (h + 1))
                            pe.wait_ge(s[f"second_loaded_{h % HSLOT}"], 16 * (h // HSLOT + 1))
                            for half in range(2):
                                mm = pe.matmul(dst, w2[:, h % HSLOT, half, :], qr[:, h % 2, half, :], start=(half == 0), stop=(half == 1))
                        else:
                            if h == 0:
                                pe.wait_ge(s["x_low"], 1)
                            pe.wait_ge(s["w_low"], h + 1)
                            for k in range(KT):
                                mm = split_product(dst, w_high[:, h % HSLOT, k, :], w_low[:, h % HSLOT, k, :],
                                                   x_high[:, k, :], x_low[:, k, :], k == 0, k == KT - 1)
                        mm.then_inc(*R.signal_filled(kind, *key))
                    elif kind == "smax":
                        j, t, b = key
                        if b == 0:
                            pe.wait_ge(*R.drained("query", head_rows(t)))
                            if t == 0:
                                for i in range(3):
                                    pe.wait_ge(*R.drained("keyT", j, i))
                        pe.matmul(acc[:, 0:LB], qhigh[:, j, t * 128:(t + 1) * 128], kparts[:, kdst(j), b * LB:(b + 1) * LB],
                                  start=True, stop=True).then_inc(*R.signal_filled(kind, *key))
                    elif kind == "maxT":
                        j, = key
                        pe.wait_ge(s["maxneg"], j + 1)
                        pe.matmul(acc[0:NMAX, 0:128], maxneg[:, j % 2, :], c["ident"][:], start=True, stop=True)\
                            .then_inc(*R.signal_filled(kind, *key))
                    elif kind == "score":
                        j, t = key
                        if t == 0:
                            pe.wait_ge(s["shift_loaded"], 16 * (j + 1))
                            pe.wait_ge(*R.drained("query", H - 1))
                        pe.wait_ge(s["keyone"], 3 * j + t // 4 + 1)
                        cols = slice(t * LP, (t + 1) * LP)
                        for half in range(2):
                            q = slice(half * HQ, (half + 1) * HQ)
                            pe.matmul(acc[0:LP, half, 0:HQ], kparts[:, kdst(j), cols], qhigh[:, j, q], start=True, stop=False)
                        for half in range(2):
                            q = slice(half * HQ, (half + 1) * HQ)
                            mm = pe.matmul(acc[0:LP, half, 0:HQ], kones[:, cols], qlow[:, j, q], start=False, stop=True)
                        mm.then_inc(*R.signal_filled(kind, *key))
                    elif kind == "mix":
                        j, t = key
                        if t == 0 and j:
                            pe.wait_ge(s["mixed"], j)
                        if t == 0 and not j:
                            last = H - 1 if layer == 0 else max(h for h in range(H) if h % 3 == 2)
                            pe.wait_ge(*R.drained("query", last))
                        pe.wait_ge(*R.drained("score", j, t))
                        for half in range(2):
                            mm = pe.matmul(mix_acc[64 * half:64 * half + DC, 0:HQ], kv[:, j % 3, t, :],
                                           prob[:, (j * LT + t) % NPROB, half * HQ:(half + 1) * HQ], start=(t == 0), stop=(t == LT - 1))
                        mm.then_inc(s["premix"], 1)
                    elif kind == "norm":
                        j, = key
                        pe.wait_ge(s["dve_sum"], vector_sums(j + 1))
                        for half in range(2):
                            mm = pe.matmul(acc[64 * half:64 * half + DC, 0:HQ], c["ones"][0:LP, :],
                                           sum_dve[:, half * HQ:(half + 1) * HQ], start=True, stop=True)
                        mm.then_inc(*R.signal_filled(kind, *key))
                    elif kind == "attn":
                        pe.wait_ge(s["ctx_ready"], BG)
                        for m in range(KT):
                            for i in range(H // 2):
                                mm = pe.matmul(acc[:, m, 0:NT].rearrange("p (j s) -> p j s", j=BG), w["wvo"][:, i, m * 128:(m + 1) * 128],
                                               ctx_n[:, :, i * S:(i + 1) * S], start=(i == 0), stop=(i == H // 2 - 1))
                        mm.then_inc(*R.signal_filled(kind, *key))
                    elif kind == "route":
                        pe.wait_ge(s["normed"], 2)
                        for i in range(RT):
                            for k in range(KT):
                                mm = pe.matmul(acc[0:TR, 0, i * NE:(i + 1) * NE], x_n[:, k, i * TR:(i + 1) * TR], w["router"][:, k, :],
                                               start=(k == 0), stop=(k == KT - 1))
                        mm.then_inc(*R.signal_filled(kind, *key))
                    elif kind == "gateup" and layer == 0:
                        i, = key
                        if i == 0:
                            pe.wait_ge(s["x_low"], 2)
                        pe.wait_ge(s["e_low"], i + 1)
                        for half in range(2):
                            for k in range(KT):
                                at = slice((half * KT + k) * I0, (half * KT + k + 1) * I0)
                                mm = split_product(acc[:, half, 0:NT], wexp_high[:, i % WSLOT, at], wexp_low[:, i % WSLOT, at],
                                                   x_high[:, k, :], x_low[:, k, :], k == 0, k == KT - 1)
                        mm.then_inc(*R.signal_filled(kind, *key))
                    elif kind == "weight":
                        i, = key
                        if i == 1:
                            pe.wait_ge(*R.drained("cwT"))
                        pe.matmul(acc[:, 0:NT], c["pick"][:, i - 1:i].broadcast_to([32 + E0, 128]), cwT[:], start=True, stop=True)\
                            .then_inc(*R.signal_filled(kind, *key))
                    elif kind == "cwT":
                        pe.wait_ge(s["routed"], 1)
                        for r in range(RT):
                            mm = pe.matmul(acc[0:E0, r * TR:(r + 1) * TR], cw[:, r, :], c["ident"][0:TR, 0:TR], start=True, stop=True)
                        mm.then_inc(*R.signal_filled(kind, *key))
                    elif kind == "down" and layer == 0:
                        i, = key
                        if i == 0:
                            pe.wait_ge(s["normed"], 2)
                        pe.wait_ge(s["hid_low"], i + 1)
                        for m in range(KT):
                            at = slice(2 * D + m * 128, 2 * D + (m + 1) * 128)
                            mm = split_product(region[(2, 5)[m]][:, 0:NT], wexp_high[:, i % WSLOT, at], wexp_low[:, i % WSLOT, at],
                                               hid_high[:, i % 2, :], hid_low[:, i % 2, :], i == 0, i == E0)
                        mm.then_inc(s["down_done"], 1)
                    elif kind == "lora":
                        pe.wait_ge(s["x_low"], 2)
                        pe.wait_ge(s["ffn_low"], 2)
                        for half, name in enumerate(("upA", "gateA")):
                            for k in range(KT):
                                mm = split_product(acc[:, half, 0:NT], w[name + "_high"][:, k, :], w[name][:, k, :],
                                                   x_high[:, k, :], x_low[:, k, :], k == 0, k == KT - 1)
                        mm.then_inc(*R.signal_filled(kind, *key))
                    elif kind == "tokw":
                        for slot in range(2):
                            for r in range(RT):
                                mm = pe.matmul(acc[:, slot, r * TR:(r + 1) * TR], tokw[:, slot, r:r + 1].broadcast_to([TR, 128]), c["ident"][0:TR, 0:TR],
                                               start=True, stop=True)
                        mm.then_inc(*R.signal_filled(kind, *key))
                    elif kind == "mask":
                        pe.wait_ge(s["routed"], 1)
                        for slot in range(2):
                            for r in range(RT):
                                mm = pe.matmul(acc[:, slot, r * TR:(r + 1) * TR], mask_rows[:, slot, r, :],
                                               c["ident"][0:TR, 0:TR], start=True, stop=True)
                        mm.then_inc(*R.signal_filled(kind, *key))
                    elif kind == "gateup":
                        m, slot = key
                        M = min(128, HID - m * 128)
                        cols = slice(m * 128, m * 128 + M)
                        if m == 0:
                            pe.wait_ge(s["ffn_low"], len(split_names))
                            pe.wait_ge(s["lora_low"], slot + 1)
                        elif slot == 0:
                            pe.wait_ge(*R.drained("gateup", m - 1, 1))
                        for half, (base, low) in enumerate((("up", "upB"), ("gate", "gateB"))):
                            dst = acc[0:M, half, 0:NT]
                            if slot == 0:
                                for k in range(KT):
                                    split_product(dst, w[base + "_high"][:, k, cols], w[base][:, k, cols], x_high[:, k, :], x_low[:, k, :], k == 0, False)
                            mm = split_product(dst, w[low + "_high"][:, cols], w[low][:, cols], lora_high[:, slot, half, :], lora_low[:, slot, half, :], slot == 1, True)
                        mm.then_inc(*R.signal_filled(kind, *key))
                    elif kind == "down":
                        m, = key
                        M = min(128, HID - m * 128)
                        if m == 0:
                            pe.wait_ge(s["normed"], 2)
                        pe.wait_ge(s["hid_ready"], 2 * (m + 1))
                        for slot in range(2):
                            pe.matmul(region[3 + 2 * slot][:, 0:NT], w["downA"][0:M, m, :], hid[0:M, m % 2, slot, :],
                                      start=(m == 0), stop=(m == MT - 1))
                        pe.wait_ge(s["acc_done"], m + 1)
                        for q in range(KT):
                            mm = pe.matmul(region[(2, 4)[q]][:, 0:NT], w["down"][0:M, m, q * 128:(q + 1) * 128], hsum[0:M, m % 2, :],
                                           start=(m == 0), stop=False)
                        mm.then_inc(s["down_done"], 1)
                    elif kind == "loradown":
                        pe.wait_ge(s["lora_z"], 2)
                        for q in range(KT):
                            for slot in range(2):
                                mm = pe.matmul(region[(2, 4)[q]][:, 0:NT], w["downB"][:, q * 128:(q + 1) * 128], lora_z[:, slot, :],
                                               start=False, stop=(slot == 1))
                        mm.then_inc(s["down_done"], 1)

            @block.scalar
            def _(act):
                for kind, key, reg in steps:
                    if reg is not None:
                        acc = region[reg]
                    if kind == "var":
                        act.wait_ge(*R.filled(kind, *key))
                        if key[0]:
                            act.wait_ge(s["rstd"], 1)
                        nc.scalar.activation(x_std[:], acc[:, 0:NT], ACT.Sqrt, bias=c["eps"][:, 0:1]).then_inc(*R.signal_drained(kind, *key))
                    elif kind == "wsplit":
                        h, = key
                        act.wait_ge(s[f"head_loaded_{h % HSLOT}"], 16 * (h // HSLOT + 1))
                        nc.scalar.activation(w_high[:, h % HSLOT, :, :], w_in[:, h % HSLOT, :, :], ACT.Copy).then_inc(s["w_high"], 1)
                    elif kind == "xsplit":
                        act.wait_ge(s["normed"], key[0] + 1)
                        nc.scalar.activation(x_high[:], x_n[:], ACT.Copy).then_inc(s["x_high"], 1)
                    elif kind == "esplit":
                        i, = key
                        act.wait_ge(s[f"weights_loaded_{i % WSLOT}"], 16 * (i // WSLOT + 1))
                        nc.scalar.activation(wexp_high[:, i % WSLOT, :], wexp_in[:, i % WSLOT, :], ACT.Copy).then_inc(s["e_high"], 1)
                    elif kind == "hidden":
                        i, = key
                        act.wait_ge(*R.drained("gateup", i))
                        if i >= 2:
                            act.wait_ge(s["down_done"], i - 1)
                        nc.scalar.activation(hid_high[:, i % 2, :], hid[:, i % 2, :], ACT.Copy).then_inc(s["hid_high"], 1)
                    elif kind == "cwT":
                        act.wait_ge(*R.filled(kind))
                        nc.scalar.activation(cwT[0:E0, :], acc[0:E0, 0:NT], ACT.Copy).then_inc(s["cw_high"], 1)
                    elif kind == "attn" and layer == 1:
                        act.wait_ge(s["ffn_loaded"], 16 * len(ffn_loads))
                        for name in split_names:
                            nc.scalar.activation(w[name + "_high"][:], w[name + "_in"][:], ACT.Copy).then_inc(s["ffn_high"], 1)
                    elif kind == "mask":
                        act.wait_ge(s["lora_in"], 3)
                        act.wait_ge(*R.drained("lora"))
                        for slot in range(2):
                            nc.scalar.activation(lora_high[:, slot, :, :], lora_in[:, slot, :, :], ACT.Copy).then_inc(s["lora_high"], 1)
                    elif kind == "keyT":
                        j, b = key
                        cols = slice(b * LB, (b + 1) * LB)
                        act.wait_ge(*R.filled(kind, *key))
                        nc.scalar.activation(kparts[0:DC, kdst(j), cols], acc[0:DC, 0:LB], ACT.Copy).then_inc(s["keyh"], 1)
                    elif kind == "kone":
                        j, b = key
                        cols = slice(b * LB, (b + 1) * LB)
                        act.wait_ge(s["keyh"], 3 * j + b + 1)
                        if j:
                            act.wait_ge(*R.filled("score", j - 1, 4 * b + 3))
                        nc.scalar.activation(kones[0:DC, cols], kparts[0:DC, kdst(j), cols].bitcast(F32), ACT.Copy).then_inc(s["keyone"], 1)
                    elif kind == "query":
                        h, = key
                        src = acc[:, 0, 0:NT] if reg < 2 else acc[:, 0:NT]
                        act.wait_ge(*R.filled(kind, *key))
                        nc.scalar.activation(qhigh[:, :, h * S:(h + 1) * S], src.rearrange("p (j s) -> p j s", j=BG), ACT.Copy)\
                            .then_inc(s["qhigh"], 1)
                    elif kind == "maxT":
                        j, = key
                        act.wait_ge(*R.filled(kind, *key))
                        if j >= 2:
                            act.wait_ge(s["shift_loaded"], 16 * (j - 1))
                        nc.scalar.activation(maxrow[:, j % 2, :], acc[0:NMAX, 0:128], ACT.Copy).then_inc(*R.signal_drained(kind, *key))
                    elif kind == "score":
                        j, t = key
                        n_ = j * LT + t
                        act.wait_ge(*R.filled(kind, *key))
                        if n_ >= NPROB:
                            act.wait_ge(s["premix"], n_ - NPROB + 1)
                            jo, to = divmod(n_ - NPROB, LT)
                            if to < pool_tiles(jo):
                                act.wait_ge(s["pool_sum"], pool_sums(jo) + max(1, to))
                            else:
                                act.wait_ge(s["dve_sum"], vector_sums(jo) + max(1, to - pool_tiles(jo)))
                        nc.scalar.activation(prob[:, n_ % NPROB, :].rearrange("p (a b) -> p a b", a=2), acc[0:LP, :, 0:HQ], ACT.Exp)\
                            .then_inc(*R.signal_drained(kind, *key))
                    elif kind == "context":
                        j, = key
                        act.wait_ge(s["premix"], LT * (j + 1))
                        if j >= 2:
                            act.wait_ge(s["ctx_ready"], j - 1)
                        nc.scalar.activation(ctx_raw[:, j % 2, :], mix_acc[:, 0:HQ], ACT.Copy).then_inc(s["mixed"], 1)
                    elif kind == "norm":
                        j, = key
                        act.wait_ge(*R.filled(kind, *key))
                        if j:
                            act.wait_ge(s["recip"], 2 * j)
                        nc.scalar.activation(total[:], acc[:, 0:HQ], ACT.Copy).then_inc(*R.signal_drained(kind, *key))
                    elif kind == "route" and layer == 0:
                        act.wait_ge(*R.filled(kind))
                        nc.scalar.activation(rt1[:], acc[0:TR, 0, 0:RT * NE].rearrange("p (a e) -> p a e", a=RT), ACT.Exp, scale=-1.0)\
                            .then_inc(*R.signal_drained(kind))
                    elif kind == "tokw":
                        act.wait_ge(s["tok_step"], 2)
                        nc.scalar.activation(tok[:], tok[:], ACT.Exp).then_inc(s["tok_exp"], 1)
                    elif kind == "gateup" and layer == 0:
                        i, = key
                        act.wait_ge(*R.filled(kind, *key))
                        if i >= 2:
                            act.wait_ge(*R.drained(kind, i - 2))
                        nc.scalar.activation(gact[:, i % 2, :], acc[:, 0, 0:NT], ACT.Silu).then_inc(s["gate_act"], 1)
                    elif kind == "gateup":
                        m, slot = key
                        M = min(128, HID - m * 128)
                        if slot == 0:
                            act.wait_ge(*R.filled(kind, *key))
                            gate_src = acc[0:M, 0, 0:NT]
                        else:
                            act.wait_ge(*R.drained(kind, *key))
                            gate_src = gate_up[0:M, 0, :]
                        if m:
                            act.wait_ge(s["hid_ready"], 2 * (m - 1) + slot + 1)
                        nc.scalar.activation(sact[0:M, slot, :], gate_src, ACT.Silu).then_inc(s["gate_act"], 1)

            @block.gpsimd
            def _(pool):
                for kind, key, reg in steps:
                    if kind == "wsplit":
                        h, = key
                        w_slot = w_low[:, h % HSLOT, :, :]
                        pool.wait_ge(s["w_high"], h + 1)
                        nc.gpsimd.tensor_tensor(w_slot, w_in[:, h % HSLOT, :, :], w_high[:, h % HSLOT, :, :].bitcast(F32), ALU.subtract).then_inc(s["w_low"], 1)
                    elif kind == "xsplit" and layer == 0 and key[0] == 1:
                        pool.wait_ge(s["x_high"], 2)
                        nc.gpsimd.tensor_tensor(x_low[:], x_n[:], x_high[:].bitcast(F32), ALU.subtract).then_inc(s["x_low"], 1)
                    elif kind == "esplit":
                        i, = key
                        w_slot = wexp_low[:, i % WSLOT, :]
                        pool.wait_ge(s["e_high"], i + 1)
                        nc.gpsimd.tensor_tensor(w_slot, wexp_in[:, i % WSLOT, :], wexp_high[:, i % WSLOT, :].bitcast(F32), ALU.subtract).then_inc(s["e_low"], 1)
                    elif kind == "attn" and layer == 1:
                        for i, name in enumerate(split_names):
                            pool.wait_ge(s["ffn_high"], i + 1)
                            nc.gpsimd.tensor_tensor(w[name][:], w[name + "_in"][:], w[name + "_high"][:].bitcast(F32), ALU.subtract)\
                                .then_inc(s["ffn_low"], 1)
                    elif kind == "rotate":
                        j, = key
                        if j:
                            pool.wait_ge(s["rope_done"], j)
                        if 1 <= j:
                            pool.wait_ge(s[f"ctx_loaded_{j}"], 16)
                        r = raw[:, j % 2, :, :]
                        hd = DC // 2
                        nc.gpsimd.tensor_tensor(rope_s[:, :, 0:hd], r[:, :, hd:DC], c["sink"][:, :, 0:hd], ALU.mult).then_inc(s["rope_sin"], 1)
                        nc.gpsimd.tensor_tensor(rope_s[:, :, hd:DC], r[:, :, 0:hd], c["sink"][:, :, hd:DC], ALU.mult).then_inc(s["rope_sin"], 1)
                    elif kind == "qwide":
                        h, = key
                        pool.wait_ge(s["qcos"], h + 1)
                        pool.wait_ge(*R.drained("qwide", h))
                        if h >= 2:
                            pool.wait_ge(*R.filled("query", h - 2))
                        for half in range(2):
                            nc.gpsimd.tensor_tensor(qr[:, h % 2, half, :], qa[:, h % 2, half, :], qb[:, h % 2, 1 - half, :], ALU.add)\
                                .then_inc(s["qrot"], 1)
                    elif kind == "mix":
                        j, t = key
                        if 1 <= t < pool_tiles(j):
                            pool.wait_ge(*R.drained("score", j, t))
                            n_ = j * LT + t
                            dst = sum_pool[:, j % 2, :]
                            if t == 1:
                                if j >= 2:
                                    pool.wait_ge(s["dve_sum"], vector_sums(j - 1))
                                first_in = prob[:, (n_ - 1) % NPROB, :]
                            else:
                                pool.wait_ge(s["pool_sum"], pool_sums(j) + t - 1)
                                first_in = dst
                            nc.gpsimd.tensor_tensor(dst, first_in, prob[:, n_ % NPROB, :], ALU.add).then_inc(s["pool_sum"], 1)
                    elif kind == "gateup" and layer == 1 and key[1] == 1:
                        m, _ = key
                        M = min(128, HID - m * 128)
                        pool.wait_ge(s["hid_ready"], 2 * (m + 1))
                        if m >= 2:
                            pool.wait_ge(s["down_done"], m - 1)
                        nc.gpsimd.tensor_tensor(hsum[0:M, m % 2, :], hid[0:M, m % 2, 0, :], hid[0:M, m % 2, 1, :], ALU.add)\
                            .then_inc(s["acc_done"], 1)

            @block.vector
            def _(dve):
                V = nc.vector
                forks = [0]

                def then(ins):
                    forks[0] += 1
                    ins.then_inc(s["route_step"], 1)
                    dve.wait_ge(s["route_step"], forks[0])

                def ranks(v, groups, width, tie, dst):
                    shape = [TR, groups, width, width]
                    gt = cmp1[:, 0:groups * width * width].rearrange("p (g a b) -> p g a b", g=groups, a=width)
                    eq = cmp2[:, 0:groups * width * width].rearrange("p (g a b) -> p g a b", g=groups, a=width)
                    other = v.unsqueeze(2).broadcast_to(shape)
                    own = v.unsqueeze(3).broadcast_to(shape)
                    V.tensor_tensor(gt, other, own, ALU.is_gt)
                    then(V.tensor_tensor(eq, other, own, ALU.is_equal))
                    flat_eq = cmp2[:, 0:groups * width * width].rearrange("p (g x) -> p g x", g=groups)
                    then(V.tensor_tensor(flat_eq, flat_eq, tie[:].unsqueeze(1).broadcast_to([TR, groups, width * width]), ALU.mult))
                    then(V.tensor_tensor(gt, gt, eq, ALU.add))
                    then(V.tensor_reduce(dst, gt, AX.X, ALU.add))

                for kind, key, reg in steps:
                    if reg is not None:
                        acc = region[reg]
                    if kind == "rope":
                        j, = key
                        r = raw[:, j % 2, :, :]
                        if j:
                            dve.wait_ge(s[f"ctx_loaded_{j}"], 16)
                            dve.wait_ge(s["rope_done"], j)
                        V.tensor_tensor(rope_c[:], r, c["cosk"][:], ALU.mult).then_inc(s["rope_cos"], 1)
                        dve.wait_ge(s["rope_cos"], j + 1)
                        dve.wait_ge(s["rope_sin"], 2 * (j + 1))
                        if j >= 3:
                            dve.wait_ge(s["premix"], LT * (j - 2))
                        V.tensor_tensor(kv[:, j % 3, :, :], rope_c[:], rope_s[:], ALU.add).then_inc(s["rope_done"], 1)
                    elif kind == "mean":
                        src = x_in if key[0] == 0 else x_res
                        dve.wait_ge(*R.filled(kind, *key))
                        V.tensor_tensor(x_cen[:], src[:], acc[:, 0:NT].unsqueeze(1).broadcast_to([128, KT, NT]), ALU.subtract)\
                            .then_inc(*R.signal_drained(kind, *key))
                        dve.wait_ge(*R.drained(kind, *key))
                        if key[0]:
                            dve.wait_ge(s["x_low"], 1)
                        V.tensor_tensor(x_sq[:], x_cen[:], x_cen[:], ALU.mult).then_inc(s["squared"], 1)
                    elif kind == "var":
                        dve.wait_ge(*R.drained(kind, *key))
                        V.reciprocal(x_rstd[:], x_std[:]).then_inc(s["rstd"], 1)
                        dve.wait_ge(s["rstd"], key[0] + 1)
                        if key[0]:
                            dve.wait_ge(*R.filled("query", H - 1))
                        V.tensor_tensor(x_n[:], x_cen[:], x_rstd[:].unsqueeze(1).broadcast_to([128, KT, NT]), ALU.mult).then_inc(s["normed"], 1)
                    elif kind == "keyT":
                        j, b = key
                        cols = slice(b * LB, (b + 1) * LB)
                        dve.wait_ge(s["keyh"], 3 * j + b + 1)
                        V.tensor_tensor(kparts[DC:2 * DC, kdst(j), cols], acc[0:DC, 0:LB], kparts[0:DC, kdst(j), cols].bitcast(F32), ALU.subtract)\
                            .then_inc(*R.signal_drained(kind, *key))
                    elif kind == "xsplit":
                        if layer == 1 or key[0] == 0:
                            dve.wait_ge(s["x_high"], key[0] + 1)
                            V.tensor_tensor(x_low[:], x_n[:], x_high[:].bitcast(F32), ALU.subtract).then_inc(s["x_low"], 1)
                    elif kind == "cwT":
                        dve.wait_ge(s["cw_high"], 1)
                        V.tensor_tensor(cwT[32:32 + E0, :], acc[0:E0, 0:NT], cwT[0:E0, :].bitcast(F32), ALU.subtract).then_inc(*R.signal_drained(kind))
                    elif kind == "hidden":
                        i, = key
                        dve.wait_ge(s["hid_high"], i + 1)
                        V.tensor_tensor(hid_low[:, i % 2, :], hid[:, i % 2, :], hid_high[:, i % 2, :].bitcast(F32), ALU.subtract).then_inc(s["hid_low"], 1)
                    elif kind == "qwide":
                        h, = key
                        src = acc[0:HALF, :, 0:NT]
                        dve.wait_ge(*R.filled(kind, *key))
                        if h >= 2:
                            dve.wait_ge(s["qrot"], 2 * (h - 1))
                        V.tensor_tensor(qa[:, h % 2, :, :], src, cosq[:], ALU.mult).then_inc(s["qcos"], 1)
                        V.tensor_tensor(qb[:, h % 2, :, :], src, sinq[:], ALU.mult).then_inc(*R.signal_drained(kind, *key))
                    elif kind == "query":
                        h, = key
                        cols = slice(h * S, (h + 1) * S)
                        src = acc[0:DC, 0, 0:NT] if reg < 2 else acc[0:DC, 0:NT]
                        dve.wait_ge(s["qhigh"], h + 1)
                        V.tensor_tensor(qlow[0:DC, :, cols], src.rearrange("p (j s) -> p j s", j=BG), qhigh[0:DC, :, cols].bitcast(F32), ALU.subtract)\
                            .then_inc(*R.signal_drained(kind, *key))
                    elif kind == "smax":
                        j, t, b = key
                        dve.wait_ge(*R.filled(kind, *key))
                        V.tensor_reduce(maxpart[:, j % 2, t, b:b + 1], acc[:, 0:LB], AX.X, ALU.max).then_inc(*R.signal_drained(kind, *key))
                    elif kind == "maxneg":
                        j, = key
                        if j >= 2:
                            dve.wait_ge(*R.filled("maxT", j - 2))
                        for b in range(3):
                            dve.wait_ge(*R.drained("smax", j, NMAX - 1, b))
                        V.tensor_reduce(maxneg[:, j % 2, :], maxpart[:, j % 2, :, :], AX.X, ALU.max, negate=True).then_inc(s["maxneg"], 1)
                    elif kind == "mix":
                        j, t = key
                        if t > pool_tiles(j):
                            n_ = j * LT + t
                            dve.wait_ge(*R.drained("score", j, t))
                            dst = sum_dve[:]
                            if t == pool_tiles(j) + 1:
                                if j:
                                    dve.wait_ge(*R.filled("norm", j - 1))
                                first_in = prob[:, (n_ - 1) % NPROB, :]
                            else:
                                dve.wait_ge(s["dve_sum"], vector_sums(j) + t - pool_tiles(j) - 1)
                                first_in = dst
                            V.tensor_tensor(dst, first_in, prob[:, n_ % NPROB, :], ALU.add).then_inc(s["dve_sum"], 1)
                    elif kind == "context":
                        j, = key
                        dve.wait_ge(s["dve_sum"], vector_sums(j + 1) - 1)
                        dve.wait_ge(s["pool_sum"], pool_sums(j) + pool_tiles(j) - 1)
                        V.tensor_tensor(sum_dve[:], sum_dve[:], sum_pool[:, j % 2, :], ALU.add).then_inc(s["dve_sum"], 1)
                    elif kind == "share":
                        j, part = key
                        if part == 0:
                            dve.wait_ge(*R.drained("norm", j))
                            if j:
                                dve.wait_ge(s["ctx_ready"], j)
                        if part < 2:
                            cols = slice(part * HQ // 2, (part + 1) * HQ // 2)
                            V.reciprocal(recip[:, cols], total[:, cols]).then_inc(s["recip"], 1)
                        else:
                            dve.wait_ge(s["recip"], 2 * (j + 1))
                            dve.wait_ge(s["mixed"], j + 1)
                            V.tensor_tensor(ctx_n[:, j, :], ctx_raw[:, j % 2, :], recip[:], ALU.mult).then_inc(s["ctx_ready"], 1)
                    elif kind == "attn":
                        dve.wait_ge(*R.filled(kind, *key))
                        V.tensor_tensor(x_res[:], acc[:, :, 0:NT], x_in[:], ALU.add).then_inc(*R.signal_drained(kind, *key))
                    elif kind == "route" and layer == 0:
                        then(V.memset(cwT[:].bitcast(F32), 0.0))
                        dve.wait_ge(*R.drained(kind))
                        then(V.tensor_scalar(rt2[:], rt1[:], 1.0, None, ALU.add))
                        then(V.reciprocal(score[:], rt2[:]))
                        then(V.tensor_tensor(rt1[:], score[:], c["bias0"][:].unsqueeze(1).broadcast_to([TR, RT, NE]), ALU.add))
                        quads = rt1[:].rearrange("p a (g b) -> p (a g) b", g=GRP0)
                        quad2 = rt2[:].rearrange("p a (g b) -> p (a g) b", g=GRP0)
                        quad3 = rt3[:].rearrange("p a (g b) -> p (a g) b", g=GRP0)
                        ranks(quads, RT * GRP0, E0 // GRP0, c["tie4"], quad2)
                        then(V.tensor_scalar(rt2[:], rt2[:], 2.0, None, ALU.is_lt))
                        then(V.tensor_tensor(rt2[:], rt2[:], rt1[:], ALU.mult))
                        then(V.tensor_reduce(rg1[:].rearrange("p a g -> p (a g)"), quad2, AX.X, ALU.add))
                        ranks(rg1[:], RT, GRP0, c["tie4"], rg2[:])
                        then(V.tensor_scalar(rg2[:], rg2[:], 2.0, None, ALU.is_lt))
                        pick = rg2[:].rearrange("p a g -> p (a g)").unsqueeze(2).broadcast_to([TR, RT * GRP0, E0 // GRP0])
                        then(V.tensor_tensor(quad3, quads, pick, ALU.mult))
                        then(V.tensor_scalar(rg2[:], rg2[:], 1.0, -NEG, ALU.subtract, ALU.mult))
                        then(V.tensor_tensor(quad3, quad3, pick, ALU.add))
                        ranks(rt3[:], RT, E0, c["tie16"], rt4[:])
                        then(V.tensor_scalar(rt4[:], rt4[:], float(TOP0), None, ALU.is_lt))
                        then(V.tensor_tensor(rt4[:], rt4[:], score[:], ALU.mult))
                        then(V.tensor_reduce(rs1[:], rt4[:], AX.X, ALU.add))
                        then(V.tensor_scalar(rs1[:], rs1[:], 1e-20, None, ALU.add))
                        then(V.reciprocal(rs2[:], rs1[:]))
                        then(V.tensor_tensor(rt4[:], rt4[:], rs2[:].unsqueeze(2).broadcast_to([TR, RT, NE]), ALU.mult))
                        V.tensor_scalar(cw[:], rt4[:], 2.5, None, ALU.mult).then_inc(s["routed"], 1)
                    elif kind == "route":
                        dve.wait_ge(*R.filled(kind))
                        V.tensor_copy(score[:], acc[0:TR, 0, 0:RT * NE].rearrange("p (a e) -> p a e", a=RT)).then_inc(*R.signal_drained(kind))
                        dve.wait_ge(*R.drained(kind))
                        ranks(score[:], RT, NE, c["tie8"], rt1[:])
                        for slot in range(2):
                            then(V.tensor_scalar(mask[:, slot, :, :], rt1[:], float(slot), None, ALU.is_equal))
                            then(V.tensor_tensor(tokm[:, slot, :, :], mask[:, slot, :, :], score[:], ALU.mult))
                        then(V.tensor_copy(mask_rows.rearrange("p a b (e r) -> p (a b e) r", r=RANK),
                                           mask[:].rearrange("p a b e -> p (a b e)").unsqueeze(2).broadcast_to([TR, 2 * RT * E1, RANK])))
                        V.tensor_reduce(tokw[:], tokm[:], AX.X, ALU.add).then_inc(s["routed"], 1)
                    elif kind == "tokw":
                        dve.wait_ge(*R.filled(kind))
                        v = acc[:, :, 0:NT].rearrange("p a (j s) -> p a j s", s=S)
                        t4 = tok[:].rearrange("p a (j s) -> p a j s", s=S)
                        per_batch = tokmax[:].rearrange("p (a j) -> p a j", a=2)
                        wide_max = per_batch.unsqueeze(3).broadcast_to([128, 2, BG, S])
                        V.tensor_reduce(per_batch, v, AX.X, ALU.max).then_inc(s["tok_step"], 1)
                        dve.wait_ge(s["tok_step"], 1)
                        V.tensor_tensor(t4, v, wide_max, ALU.subtract).then_inc(s["tok_step"], 1)
                        dve.wait_ge(s["tok_exp"], 1)
                        then(V.tensor_reduce(per_batch, t4, AX.X, ALU.add))
                        then(V.reciprocal(tokmax[:], tokmax[:]))
                        V.tensor_tensor(tokc[:].rearrange("p a (j s) -> p a j s", s=S), t4, wide_max, ALU.mult).then_inc(*R.signal_drained(kind))
                    elif kind == "mask":
                        dve.wait_ge(*R.filled(kind))
                        V.tensor_copy(maskT[:], acc[:, :, 0:NT]).then_inc(*R.signal_drained(kind))
                        dve.wait_ge(*R.drained(kind))
                        dve.wait_ge(*R.filled("lora"))
                        then(V.tensor_tensor(mask_diff[:], maskT[:, 1, :], maskT[:, 0, :], ALU.subtract))
                        for slot, chosen in enumerate((maskT[:, 0, :], mask_diff[:])):
                            for half in range(2):
                                V.scalar_tensor_tensor(out=lora_in[:, slot, half, :], in0=region[0][:, half, 0:NT], scalar=2.0,
                                                       in1=chosen, op0=ALU.mult, op1=ALU.mult)\
                                    .then_inc(*(R.signal_drained("lora") if half and slot else (s["lora_in"], 1)))
                        for slot in range(2):
                            dve.wait_ge(s["lora_high"], slot + 1)
                            V.tensor_tensor(lora_low[:, slot, :, :], lora_in[:, slot, :, :], lora_high[:, slot, :, :].bitcast(F32), ALU.subtract)\
                                .then_inc(s["lora_low"], 1)
                    elif kind == "gateup" and layer == 0:
                        i, = key
                        dve.wait_ge(s["gate_act"], i + 1)
                        if i == 0:
                            V.tensor_tensor(hid[:, 0, :], gact[:, 0, :], acc[:, 1, 0:NT], ALU.mult).then_inc(*R.signal_drained(kind, *key))
                    elif kind == "weight":
                        i, = key
                        up = region[i % 2][:, 1, 0:NT]
                        dve.wait_ge(*R.filled(kind, *key))
                        V.tensor_tensor(gact[:, i % 2, :], gact[:, i % 2, :], acc[:, 0:NT], ALU.mult).then_inc(*R.signal_drained(kind, *key))
                        dve.wait_ge(*R.drained(kind, *key))
                        if i >= 2:
                            dve.wait_ge(s["down_done"], i - 1)
                        V.tensor_tensor(hid[:, i % 2, :], gact[:, i % 2, :], up, ALU.mult).then_inc(*R.signal_drained("gateup", i))
                    elif kind == "gateup":
                        m, slot = key
                        M = min(128, HID - m * 128)
                        if slot == 0:
                            dve.wait_ge(s["gate_act"], 2 * m + 1)
                            V.tensor_tensor(sact[0:M, 0, :], sact[0:M, 0, :], acc[0:M, 1, 0:NT], ALU.mult)\
                                .then_inc(*R.signal_drained(kind, *key))
                            dve.wait_ge(*R.drained(kind, *key))
                        else:
                            dve.wait_ge(*R.filled(kind, *key))
                            if m:
                                dve.wait_ge(s["hid_ready"], 2 * m)
                            V.tensor_copy(gate_up[0:M, :, :], region[0][0:M, :, 0:NT]).then_inc(s["gate_up"], 1)
                            dve.wait_ge(s["gate_up"], 2 * m + 1)
                            V.tensor_tensor(gate_up[0:M, :, :], gate_up[0:M, :, :], acc[0:M, :, 0:NT], ALU.add)\
                                .then_inc(*R.signal_drained(kind, *key))
                            dve.wait_ge(s["gate_act"], 2 * m + 2)
                            V.tensor_tensor(sact[0:M, 1, :], sact[0:M, 1, :], gate_up[0:M, 1, :], ALU.mult).then_inc(s["gate_up"], 1)
                            dve.wait_ge(s["gate_up"], 2 * m + 2)
                        if m >= 2:
                            dve.wait_ge(s["down_done"], m - 1)
                        V.tensor_tensor(hid[0:M, m % 2, slot, :], sact[0:M, slot, :], tokc[0:M, slot, :], ALU.mult)\
                            .then_inc(s["hid_ready"], 1)
                    elif kind == "loradown":
                        dve.wait_ge(s["down_done"], MT)
                        for slot in range(2):
                            V.scalar_tensor_tensor(out=lora_z[:, slot, :], in0=region[3 + 2 * slot][:, 0:NT], scalar=2.0,
                                                   in1=maskT[:, slot, :], op0=ALU.mult, op1=ALU.mult).then_inc(s["lora_z"], 1)
                    elif kind == "out":
                        dve.wait_ge(s["down_done"], E0 + 1 if layer == 0 else MT + 1)
                        for q in range(KT):
                            V.tensor_tensor(x_cen[:, q, :], region[(2, (5, 4)[layer])[q]][:, 0:NT], x_res[:, q, :], ALU.add)\
                                .then_inc(s["out_ready"], 1)
        nc.all_engine_barrier(sems_to_clear=group_range)


def kernel(**inputs):
    import concourse.bacc as bacc
    from concourse.bass_utils import run_bass_kernel_spmd

    def arr(x):
        return np.ascontiguousarray(np.asarray(x))

    x = arr(inputs["x"]).reshape(G, NT, KT, 128).transpose(0, 3, 2, 1)
    d = {"x": np.concatenate([x, np.zeros_like(x[:1])])}
    ctx = arr(inputs["ctx_512"]).reshape(B, LP, LT * DC)
    d["ctx"] = np.concatenate([ctx, np.zeros_like(ctx[:1])])
    d["cosk"], d["sink"], d["cosq"], d["sinq"] = rope_tables()
    d["ident"] = np.eye(128, dtype=np.float32)
    d["tie4"], d["tie8"], d["tie16"] = before_masks(4), before_masks(8), before_masks(16)
    d["bias"] = arr(inputs["L0_ffn_expert_bias"]).reshape(1, E0)
    for n in range(2):
        p = f"L{n}_xattn_"
        d[f"wq{n}"] = arr(inputs[p + "Wq"])
        d[f"kcq{n}"] = arr(inputs[p + "w_kc_q"])
        d[f"kckv{n}"] = arr(inputs[p + "w_kc_kv"])
        d[f"wo{n}"] = arr(inputs[p + "Wo"]).T
        d[f"wqr{n}"] = arr(inputs[p + "W_qr"]).transpose(2, 0, 1)
        d[f"wkr{n}"] = arr(inputs[p + "W_kr"]).transpose(2, 0, 1)
    d["router0"] = arr(inputs["L0_ffn_gate_weight"]).T
    d["router1"] = arr(inputs["L1_ffn_gate_w"]).T

    def expert(gate, up, down):
        parts = [m.T.reshape(KT, 128, I0).transpose(1, 0, 2).reshape(128, KT * I0) for m in (gate, up)]
        return np.concatenate(parts + [down.T], axis=1)

    q = "L0_ffn_"
    gate, up, down = (arr(inputs[q + f"{m}_proj"]) for m in ("gate", "up", "down"))
    shared = expert(*(arr(inputs[q + f"shared_{m}"]) for m in ("gate", "up", "down")))
    d["experts"] = np.stack([shared] + [expert(gate[e], up[e], down[e]) for e in range(E0)])
    q = "L1_ffn_"
    d["f_up"], d["f_gate"] = arr(inputs[q + "w_up"]).T, arr(inputs[q + "w_gate"]).T
    d["f_down"] = arr(inputs[q + "w_down"]).T
    d["f_upA"], d["f_gateA"] = (arr(inputs[q + m]).reshape(E1 * RANK, D).T for m in ("up_A", "gate_A"))
    d["f_upB"], d["f_gateB"] = (arr(inputs[q + m]).transpose(0, 2, 1).reshape(E1 * RANK, HID) for m in ("up_B", "gate_B"))
    d["f_downA"] = arr(inputs[q + "down_A"]).reshape(E1 * RANK, HID).T
    d["f_downB"] = arr(inputs[q + "down_B"]).transpose(0, 2, 1).reshape(E1 * RANK, D)

    nc = bacc.Bacc("TRN2", target_bir_lowering=False, num_devices=1)
    arrays, aps = {}, {}
    for name, v in d.items():
        arrays["in_" + name] = np.ascontiguousarray(v)
        aps[name] = nc.dram_tensor("in_" + name, v.shape, mybir.dt.from_np(v.dtype), kind="ExternalInput").ap()
    out = nc.dram_tensor("out_x", [G, 128, KT, NT], F32, kind="ExternalOutput").ap()
    x_mid = nc.dram_tensor("x_mid", [G + 1, 128, KT, NT], F32).ap()
    scratch = {name: nc.dram_tensor(name + "_merged", shape, F32).ap() for name, shape in (
        ("w1", [H, 128, KT * DCQ]), ("w2", [H, HALF, 4 * DC]), ("wabs", [H, 128, KT * 2 * DC]), ("wvo", [2, 128, H // 2 * D]))}
    build_program(nc, aps, scratch, out, x_mid)
    r = run_bass_kernel_spmd(nc, [arrays], core_ids=[0])
    y = r.results[0]["out_x"]
    return np.ascontiguousarray(y.transpose(0, 3, 2, 1)).reshape(B, S, D)
```

```python
from contextlib import ExitStack

import concourse.bass as bass
import numpy as np
from concourse import mybir

ALU = mybir.AluOpType
ACT = mybir.ActivationFunctionType
AX = mybir.AxisListType
F32 = mybir.dt.float32
F32R = mybir.dt.float32r

B, S, L, D = 32, 56, 1500, 256
H, HK, DC, DCQ, DR = 16, 128, 64, 192, 64
BG = 8
G = B // BG
NT = BG * S
NQ = H * S
HQ = NQ // 2
LT, LP = 12, 125
LB = L // 3
KT = D // 128
HALF = DCQ // 2
NMAX = NQ // 128
NPROB = 4
POOL_TILES, POOL_LAST = 10, 5
E0, TOP0, GRP0 = 16, 4, 4
E1, RANK = 8, 16
I0 = 128
HID = 704
MT = -(-HID // 128)
SHARE_AT = (1, 9, 11)
SMAX_PACE = (0, 0, 3, 3, 3, 3, 3, 3, 3, 0, 0, 0)
RT = NT // 112
TR = NT // RT
NEG = -3.0e38
EPS = 1e-5
WSLOT = 4
EARLY_MAX = 1
HSLOTS = (4, 6)
SPLIT_AHEAD = 2


def head_rows(t):
    return (128 * t + 127) // S


def pool_tiles(j):
    return POOL_TILES if j < BG - 1 else POOL_LAST


def pool_sums(j):
    return j * (POOL_TILES - 1)


def vector_sums(j):
    return sum(LT - pool_tiles(i) for i in range(j))


def schedule(layer):
    steps = []
    spin = [0]

    def add(kind, *key, region=None):
        steps.append((kind, key, region))

    def turn():
        spin[0] += 1
        return 3 + (spin[0] - 1) % 3

    def keys(j):
        for c in range(3):
            add("keyT", j, c, region=turn())

    def maxima(j, tiles):
        for t in tiles:
            for c in range(3):
                add("smax", j, t, c, region=turn())

    add("rotate", 0)
    for h in range(SPLIT_AHEAD):
        add("wsplit", h)
    add("rope", 0)
    keys(0)
    done = 0
    ahead = 3 if layer == 0 else 2
    for h in range(H + ahead):
        if h == H - 3:
            add("rotate", 1)
        if h == H:
            add("rope", 1)
        if h + SPLIT_AHEAD < H:
            add("wsplit", h + SPLIT_AHEAD)
        if layer == 0:
            if h < H:
                add("qwide", h, region=h % 2)
            if 2 <= h < H + 2:
                add("query", h - 2, region=2)
        elif h < H:
            add("query", h, region=h % 3)
        while done < NMAX and head_rows(done) <= h - ahead:
            maxima(0, [done])
            done += 1
    maxima(0, range(done, NMAX))
    add("maxneg", 0)
    add("maxT", 0, region=turn())
    keys(1)
    maxima(1, range(EARLY_MAX))
    last = None
    for c in range(3):
        add("kone", 0, c)
    for j in range(BG):
        ahead = [(row, c) for row in range(EARLY_MAX if j == 0 else 0, NMAX) for c in range(3)] if j + 1 < BG else []
        for t in range(LT):
            if t == 0 and j + 2 < BG:
                add("rotate", j + 2)
            if t == 1 and j:
                add("kone", j, 2)
            if t in (5, 9) and j + 1 < BG:
                add("kone", j + 1, t // 4 - 1)
            add("score", j, t, region=t % 2)
            for _ in range(SMAX_PACE[t]):
                if ahead:
                    row, c = ahead.pop(0)
                    add("smax", j + 1, row, c, region=turn())
            if j + 1 < BG and t == 8:
                add("maxneg", j + 1)
            if last is not None:
                add("mix", *last)
                if last[1] == LT - 1:
                    add("context", last[0])
            last = (j, t)
            if 0 < j < BG - 1 and t == 0:
                keys(j + 1)
            if t == 1 and j:
                add("norm", j - 1, region=turn())
            if t in SHARE_AT and j:
                add("share", j - 1, SHARE_AT.index(t))
            if j + 1 < BG and t == 9:
                add("maxT", j + 1, region=turn())
            if t == 10 and j + 2 < BG:
                add("rope", j + 2)
        assert not ahead
    add("mix", *last)
    add("context", BG - 1)
    add("norm", BG - 1, region=turn())
    for part in (0, 2, 1, 3):
        add("share", BG - 1, part)
    add("attn", region=0)
    if layer == 0:
        for i in range(2):
            add("esplit", i)
    add("mean", 0, region=2)
    add("var", 0, region=5)
    for part in range(2):
        add("rstd", 0, part)
    add("xsplit", 0)
    add("route", region=1)
    if layer == 0:
        add("gateup", 0, region=0)
        add("hidden", 0)
        add("esplit", 2)
        add("gateup", 1, region=1)
        add("down", 0)
        add("gateup", 2, region=0)
        add("cwT", region=3)
        for i in range(1, E0 + 1):
            if i > 2:
                add("gateup", i, region=i % 2)
            add("weight", i, region=3 + i % 2)
            if i > 1:
                add("down", i - 1)
            if i + 2 <= E0:
                add("esplit", i + 2)
            add("hidden", i)
            if i == E0 - 3:
                add("mean", 1, region=4)
            if i == E0 - 2:
                add("var", 1, region=3)
            if i > E0 - 2:
                add("rstd", 1, i - E0 + 1)
        add("down", E0)
        add("out")
    else:
        add("lora", region=0)
        add("mask", region=1)
        add("tokw", region=1)
        for m in range(MT):
            for slot in range(2):
                add("gateup", m, slot, region=slot)
            if m:
                add("down", m - 1)
        add("mean", 1, region=0)
        add("down", MT - 1)
        add("var", 1, region=1)
        add("loradown")
        add("rstd", 1, 0)
        add("out")
        add("rstd", 1, 1)
    add("xsplit", 1)
    return steps


class Regions:

    def __init__(self, steps, filled, drained):
        self.full, self.empty, self.at, self.before = filled, drained, {}, {}
        used = [0] * len(filled)
        for kind, key, region in steps:
            if region is not None:
                self.before[kind, key] = (region, used[region])
                used[region] += 1
                self.at[kind, key] = (region, used[region])
        self.used = used

    def room(self, eng, kind, *key):
        r, n = self.before[kind, key]
        if n:
            eng.wait_ge(self.empty[r], n)

    def filled(self, kind, *key):
        r, n = self.at[kind, key]
        return self.full[r], n

    def drained(self, kind, *key):
        r, n = self.at[kind, key]
        return self.empty[r], n

    def signal_filled(self, kind, *key):
        return self.full[self.at[kind, key][0]], 1

    def signal_drained(self, kind, *key):
        return self.empty[self.at[kind, key][0]], 1


def rope_tables():
    def table(n, dim):
        inv = (1.0 / 10000.0 ** (np.arange(0, dim, 2, dtype=np.float32) / np.float32(dim))).astype(np.float32)
        f = np.arange(n, dtype=np.float32)[:, None] * inv[None, :]
        return np.repeat(np.sin(f), 2, axis=-1), np.repeat(np.cos(f), 2, axis=-1)
    sk, ck = table(L, DC)
    sk = np.concatenate([-sk[:, :DC // 2], sk[:, DC // 2:]], axis=1)
    sq, cq = table(S, DCQ)
    lay = lambda a: np.tile(a.T, (1, BG))
    cosq = np.stack([lay(cq[:, :HALF]), lay(cq[:, HALF:])], axis=1)
    sinq = np.stack([lay(sq[:, HALF:]), -lay(sq[:, :HALF])], axis=1)
    return (ck.reshape(LP, LT * DC).astype(np.float32), sk.reshape(LP, LT * DC).astype(np.float32),
            np.ascontiguousarray(cosq, np.float32), np.ascontiguousarray(sinq, np.float32))


def before_masks(n):
    return np.tril(np.ones((n, n), np.float32), -1).reshape(1, n * n)


def build_program(nc, a, scratch, out, x_mid):
    top = ExitStack()
    with top:
        def sb(name, shape, dt=F32, stack=top):
            return stack.enter_context(nc.sbuf_tensor(name, shape, dt))

        wide = [top.enter_context(nc.psum_tensor(f"wide{i}", [128, 2, 512], F32)) for i in range(2)]
        single = [top.enter_context(nc.psum_tensor(f"single{i}", [128, 512], F32)) for i in range(4)]
        region = wide + single
        mix_acc = region[2]

        ident = sb("ident", [128, 128])
        ones = sb("ones", [128, DC])
        mean_w = sb("mean_w", [128, 128])
        eps = sb("eps", [128, 1])
        cosk = sb("cosk", [LP, LT, DC])
        sink = sb("sink", [LP, LT, DC])
        tie4 = sb("tie4", [TR, 16])
        tie8 = sb("tie8", [TR, 64])
        tie16 = sb("tie16", [TR, 256])
        bias0 = sb("bias0", [TR, E0])
        pick = sb("pick", [32 + E0, E0], F32R)

        s_names = ["load", "setup_full", "setup_const", "setup_stored", "first_pe", "first_dve", "first_act"] + [f"setup_{kind}_{n}" for kind in ("w1", "w2", "wvo") for n in range(2)] + [f"setup_copied_{i}" for i in range(2)]
        setup_sems = {n: top.enter_context(nc.semaphore(n)) for n in s_names}
        group_names = (
            [f"filled_{i}" for i in range(6)] + [f"drained_{i}" for i in range(6)]
            + [f"ctx_loaded_{j}" for j in range(1, BG)] + [f"weights_loaded_{i}" for i in range(WSLOT)]
            + [f"head_loaded_{i}" for i in range(max(HSLOTS))] + [f"second_loaded_{i}" for i in range(HSLOTS[0])]
            + ["ffn_loaded", "next_loaded", "shift_loaded",
               "cen_half", "sq_half", "squared", "rstd", "normed", "x_high", "x_low",
               "rope_cos", "rope_sin", "rope_done", "keyh", "keyone", "w_high", "w_low", "qcos", "qrot", "qhigh",
               "maxneg", "premix", "mixed", "pool_sum", "dve_sum", "recip", "ctx_ready", "attn_half", "res_half",
               "route_step", "routed", "cw_high", "e_high", "e_low", "gate_act", "shared_hid", "hid_high", "hid_low", "down_done",
               "ffn_high", "ffn_low", "lora_in", "lora_high", "lora_low", "tok_step", "tok_exp", "gate_up", "gate_copied",
               "hid_ready", "acc_done", "lora_z", "out_ready"])
        setup_sems["tokens_moved"] = top.enter_context(nc.semaphore("tokens_moved"))
        sems = {n: top.enter_context(nc.semaphore(n)) for n in group_names}
        nums = [s.num for s in sems.values()]
        group_range = range(min(nums), max(nums) + 1)
        setup_nums = [setup_sems[n].num for n in s_names]
        setup_range = range(min(setup_nums), max(setup_nums) + 1)
        assert len(group_range) == len(nums) and len(setup_range) == len(setup_nums)

        with nc.Block() as block:
            load = setup_sems["load"]

            @block.sync
            def _(sp):
                for dst, name in ((cosk, "cosk"), (sink, "sink")):
                    sp.dma_start(dst[:].rearrange("p a b -> p (a b)"), a[name]).then_inc(load, 16)
                sp.dma_start(ident[:], a["ident"]).then_inc(load, 16)
                for dst, name in ((tie4, "tie4"), (tie8, "tie8"), (tie16, "tie16"), (bias0, "bias")):
                    src = a[name]
                    sp.dma_start(dst[:], src.broadcast_to([TR, src.shape[1]])).then_inc(load, 16)
                sp.wait_ge(load, 7 * 16)

            @block.vector
            def _(dve):
                nc.vector.memset(ones[:], 1.0)
                nc.vector.memset(mean_w[:], 1.0 / D)
                nc.vector.memset(eps[:], EPS)
                nc.vector.memset(pick[:].bitcast(F32), 0.0).then_inc(setup_sems["setup_const"], 1)
                dve.wait_ge(setup_sems["setup_const"], 1)
                dve.wait_ge(load, 7 * 16)
                for r in (0, 32):
                    nc.vector.tensor_copy(pick[r:r + E0, :], ident[r:r + E0, r:r + E0])
        nc.all_engine_barrier(sems_to_clear=setup_range)

        merge_weights(nc, a, scratch, region, setup_sems, setup_range, sb)
        for layer in range(2):
            with ExitStack() as work:
                run_layer(nc, layer, a, scratch, x_mid, out, sems, group_range, setup_sems, setup_range, sb, work,
                          region, mix_acc,
                          dict(ident=ident, ones=ones, mean_w=mean_w, eps=eps, cosk=cosk, sink=sink, tie4=tie4,
                               tie8=tie8, tie16=tie16, bias0=bias0, pick=pick))


def merge_weights(nc, a, scratch, region, sems, sems_range, sb):
    full, copied, stored = sems["setup_full"], [sems["setup_copied_0"], sems["setup_copied_1"]], sems["setup_stored"]
    banks = [region[0][:, 0, :], region[0][:, 1, :], region[1][:, 0, :], region[1][:, 1, :]] + [region[i][:, :] for i in range(2, 6)]

    stages = [(0, "w2", 2), (0, "wvo", 1), (0, "w1", 2), (1, "w2", 2), (1, "wvo", 1), (1, "w1t", 2), (1, "wabs", 2)]
    items = [(layer, kind, h, c) for layer, kind, parts in stages for h in range(H) for c in range(parts)]
    weights_of = {"w2": ("wqr", "wkr"), "wvo": ("kckv", "wo"), "w1": ("kcq", "wq"), "w1t": ("kcq", "wq")}

    def last_of(layer, kind):
        return max(i for i, item in enumerate(items) if item[:2] == (layer, kind)) + 1

    with ExitStack() as stack:
        def raw_weights(n, where):
            shapes = dict(wqr=[DR, H, DCQ], wkr=[DR, H, DC], kckv=[128, H, DC], wo=[128, H, D], kcq=[128, H, DCQ], wq=[128, H, D])
            return {name: sb(f"{name}_raw{n}", shape, stack=where) for name, shape in shapes.items()}

        raw = {1: raw_weights(1, stack)}
        m = {(0, "w1"): sb("w1_product", [128, KT, H, DCQ], stack=stack), (0, "w2"): sb("w2_product0", [HALF, 2, H, 2 * DC], stack=stack),
             (0, "wvo"): sb("wvo_product0", [128, H // 2, D], stack=stack), (1, "wvo"): sb("wvo_product1", [128, H // 2, D], stack=stack)}
        with ExitStack() as before:
            raw[0] = raw_weights(0, before)
        m[1, "w1t"] = sb("w1t_product", [HALF, 2, H, D], stack=stack)
        m[1, "w2"] = sb("w2_product1", [HALF, 2, H, 2 * DC], stack=stack)
        m[1, "wabs"] = sb("wabs_product", [128, KT, H, 2 * DC], stack=stack)

        def place(item):
            layer, kind, h, c = item
            if kind == "wvo":
                p = 64 * (h // (H // 2))
                return m[layer, kind][p:p + DC, h % (H // 2), :], (p, p + DC), D
            rows, width = {"w2": (HALF, 2 * DC), "w1": (128, DCQ), "w1t": (HALF, D), "wabs": (128, 2 * DC)}[kind]
            return m[layer, kind][:, c, h, :], (0, rows), width

        with nc.Block() as block:
            @block.sync
            def _(sp):
                for layer in range(2):
                    for kind in ("w2", "wvo", "w1"):
                        for name in weights_of[kind]:
                            sp.dma_start(raw[layer][name][:].rearrange("p h f -> p (h f)"), a[f"{name}{layer}"])\
                                .then_inc(sems[f"setup_{kind}_{layer}"], 16)
                stores = 0
                for layer, kind, _ in stages:
                    if kind != "w1t" and (layer, kind) != (1, "w2"):
                        for k in range(2):
                            sp.wait_ge(copied[k], (last_of(layer, kind) + 1 - k) // 2)
                        if kind == "wvo":
                            sp.dma_start(scratch["wvo"][layer], m[layer, kind][:].rearrange("p h f -> p (h f)")).then_inc(stored, 16)
                        else:
                            sp.dma_start(scratch[kind].rearrange("h p (k q) -> p k h q", k=2), m[layer, kind][:]).then_inc(stored, 16)
                        stores += 1
                sp.wait_ge(stored, 16 * stores)

            @block.tensor
            def _(pe):
                for i, (layer, kind, h, c) in enumerate(items):
                    bank = banks[i % 8]
                    if h == 0 and c == 0:
                        if kind in weights_of:
                            pe.wait_ge(sems[f"setup_{kind[:2] if kind == 'w1t' else kind}_{layer}"], 32)
                        else:
                            for k in range(2):
                                pe.wait_ge(copied[k], (i + 1 - k) // 2)
                    if i >= 8:
                        pe.wait_ge(copied[i % 2], (i - 8) // 2 + 1)
                    r = raw[layer]
                    if kind == "w2":
                        mm = pe.matmul(bank[0:HALF, 0:DC], r["wqr"][:, h, c * HALF:(c + 1) * HALF], r["wkr"][:, h, :], start=True, stop=True)
                    elif kind == "w1":
                        mm = pe.matmul(bank[:, 0:DCQ], r["wq"][:, h, c * 128:(c + 1) * 128], r["kcq"][:, h, :], start=True, stop=True)
                    elif kind == "w1t":
                        mm = pe.matmul(bank[0:HALF, 0:D], r["kcq"][:, h, c * HALF:(c + 1) * HALF], r["wq"][:, h, :], start=True, stop=True)
                    elif kind == "wvo":
                        p = 64 * (h // (H // 2))
                        mm = pe.matmul(bank[p:p + DC, 0:D], r["kckv"][:, h, :], r["wo"][:, h, :], start=True, stop=True)
                    else:
                        for k in range(2):
                            mm = pe.matmul(bank[:, 0:2 * DC], m[1, "w1t"][:, k, h, c * 128:(c + 1) * 128], m[1, "w2"][:, k, h, :],
                                           start=(k == 0), stop=(k == 1))
                    mm.then_inc(full, 1)

            def copies(eng, k, copy):
                for i, item in enumerate(items):
                    if i % 2 == k:
                        dst, (p, q), width = place(item)
                        src = banks[i % 8][p:q, 0:width]
                        if item[1] == "w2":
                            src = banks[i % 8][p:q, 0:DC].unsqueeze(1).broadcast_to([q - p, 2, DC])
                            dst = dst.rearrange("p (a b) -> p a b", a=2)
                        eng.wait_ge(full, i + 1)
                        copy(dst, src).then_inc(copied[k], 1)

            @block.scalar
            def _(act):
                copies(act, 0, lambda dst, src: nc.scalar.activation(dst, src, ACT.Copy))

            @block.vector
            def _(dve):
                copies(dve, 1, nc.vector.tensor_copy)
        nc.all_engine_barrier(sems_to_clear=sems_range)


def run_layer(nc, layer, a, scratch, x_mid, out, sems, group_range, setup_sems, setup_range, sb, stack, region, mix_acc, c):
    n = str(layer)

    def buf(name, shape, dt=F32):
        return sb(name + n, shape, dt, stack=stack)

    def split_in_place(name, shape, where=stack):
        with ExitStack() as first_use:
            values = sb(name + "_values" + n, shape, stack=first_use)
        return values, sb(name + n, shape, F32R, stack=where)

    NE = E0 if layer == 0 else E1
    HSLOT = HSLOTS[layer]
    w = {"wvo": buf("wvo", [128, H // 2, D]), "router": buf("router", [128, KT, NE])}
    raw = buf("raw", [LP, 2, LT, DC])
    rope_c = buf("rope_c", [LP, LT, DC])
    rope_s = buf("rope_s", [LP, LT, DC])
    kv = buf("kv", [LP, 3, LT, DC])
    kparts = buf("kparts", [128, 2, L], F32R)
    kones = buf("kones", [DC + 1, L], F32R)
    ctx_raw = buf("ctx_raw", [128, 2, HQ])
    recip = buf("recip", [128, HQ])
    total = buf("total", [128, HQ])
    table_probe = buf("table_probe", [128, 4])
    ctx_n = buf("ctx_n", [128, BG, HQ])
    maxpart = buf("maxpart", [128, 2, NMAX, 3])
    maxneg = buf("maxneg", [128, 2, NMAX])
    maxrow = buf("maxrow", [NMAX, 2, 128], F32R)
    x_in = buf("x_in", [128, KT, NT])
    x_cen = buf("x_cen", [128, KT, NT])
    x_std = buf("x_std", [128, NT])
    x_rstd = buf("x_rstd", [128, NT])
    x_n = buf("x_n", [128, KT, NT])
    x_sq = x_n
    x_res = buf("x_res", [128, KT, NT])
    x_high = buf("x_high", [128, KT, NT], F32R)
    x_low = buf("x_low", [128, KT, NT], F32R)
    if layer == 0:
        cosq = buf("cosq", [HALF, 2, NT])
        sinq = buf("sinq", [HALF, 2, NT])
        w_in, w_low = split_in_place("w_low", [128, HSLOT, KT, DCQ])
        w_high = buf("w_high", [128, HSLOT, KT, DCQ], F32R)
        w2 = buf("w2", [HALF, HSLOT, 2, 2 * DC])
    else:
        with ExitStack() as making_queries:
            w_in, w_low = split_in_place("w_low", [128, HSLOT, KT, 2 * DC], making_queries)
            w_high = sb("w_high" + n, [128, HSLOT, KT, 2 * DC], F32R, stack=making_queries)
    with ExitStack() as attention:
        prob = sb("prob" + n, [LP, NPROB, NQ], stack=attention)
        sum_pool = sb("sum_pool" + n, [LP, 2, NQ], stack=attention)
        sum_dve = sb("sum_dve" + n, [LP, NQ], stack=attention)
        qhigh = sb("qhigh" + n, [128, BG, NQ], F32R, stack=attention)
        qlow = sb("qlow" + n, [DC + 1, BG, NQ], F32R, stack=attention)
    if layer == 0:
        qa = prob[0:HALF, 0:2, :].rearrange("p h (a b) -> p h a b", a=2)
        qb = prob[0:HALF, 2:4, :].rearrange("p h (a b) -> p h a b", a=2)
        qr = sum_pool[0:HALF, :, :].rearrange("p h (a b) -> p h a b", a=2)
        gact = buf("gact", [128, 2, NT])
        hid = buf("hid", [128, 2, NT])
        hid_high = buf("hid_high", [128, 2, NT], F32R)
        hid_low = buf("hid_low", [128, 2, NT], F32R)
        shared_up = buf("shared_up", [128, NT])
        cwT = buf("cwT", [32 + E0, NT], F32R)
    else:
        sact = buf("sact", [128, 2, NT])
        hid = buf("hid", [128, 2, 2, NT])
        gate_up = buf("gate_up", [128, 2, NT])
        hsum = buf("hsum", [128, 2, NT])
        mask_rows = buf("mask_rows", [TR, 2, RT, 128])
        tokmax = buf("tokmax", [128, 2 * BG])
        tokw = buf("tokw", [TR, 2, RT])
        mask = buf("mask", [TR, 2, RT, E1])
        tokm = buf("tokm", [TR, 2, RT, E1])
    score = buf("score", [TR, RT, NE])
    rt1 = buf("rt1", [TR, RT, NE])
    rt2 = buf("rt2", [TR, RT, NE])
    rt3 = buf("rt3", [TR, RT, NE])
    rt4 = buf("rt4", [TR, RT, NE])
    rg1 = buf("rg1", [TR, RT, GRP0])
    rg2 = buf("rg2", [TR, RT, GRP0])
    rs1 = buf("rs1", [TR, RT])
    rs2 = buf("rs2", [TR, RT])
    cw = buf("cw", [TR, RT, NE])
    cmp1 = buf("cmp1", [TR, RT * NE * NE])
    cmp2 = buf("cmp2", [TR, RT * NE * NE])
    ffn_loads = []
    if layer == 0:
        wexp_in, wexp_low = split_in_place("wexp_low", [128, WSLOT, 3 * D])
        wexp_high = buf("wexp_high", [128, WSLOT, 3 * D], F32R)
    else:
        lora_high = buf("lora_high", [128, 2, 2, NT], F32R)
        lora_in, lora_low = split_in_place("lora_low", [128, 2, 2, NT])
        tok = buf("tok", [128, 2, NT])
        tokc = buf("tokc", [128, 2, NT])
        maskT = buf("maskT", [128, 2, NT])
        mask_diff = buf("mask_diff", [128, NT])
        lora_z = tok
        for name, shape in (("upA", [128, KT, 128]), ("gateA", [128, KT, 128]), ("up", [128, KT, HID]), ("gate", [128, KT, HID])):
            w[name + "_in"], w[name] = split_in_place("w_" + name, shape)
            w[name + "_high"] = buf(f"w_{name}_high", shape, F32R)
            ffn_loads.append((w[name + "_in"][:], a["f_" + name].rearrange("(k p) e -> p k e", p=128)))
        for name in ("upB", "gateB"):
            w[name + "_in"], w[name] = split_in_place("w_" + name, [128, HID])
            w[name + "_high"] = buf(f"w_{name}_high", [128, HID], F32R)
            ffn_loads.append((w[name + "_in"][:], a["f_" + name]))
        w["downB"] = buf("w_downB", [128, D])
        ffn_loads.append((w["downB"][:], a["f_downB"]))
        whole = HID // 128
        for name, width in (("down", D), ("downA", 128)):
            w[name] = buf("w_" + name, [128, MT, width])
            src = a["f_" + name]
            ffn_loads.append((w[name][:, 0:whole, :], src[0:whole * 128, :].rearrange("(m p) e -> p m e", p=128)))
            ffn_loads.append((w[name][0:HID - whole * 128, whole, :], src[whole * 128:HID, :]))
        split_names = ("upA", "gateA", "up", "gate", "upB", "gateB")

    x_src = a["x"] if layer == 0 else x_mid
    x_dst = x_mid if layer == 0 else out
    steps = schedule(layer)
    R = Regions(steps, [sems[f"filled_{i}"] for i in range(6)], [sems[f"drained_{i}"] for i in range(6)])
    s = sems

    def first_bank(reg):
        return region[reg][:, 0, 0:NT] if reg < 2 else region[reg][:, 0:NT]

    def kdst(j):
        return j % 2

    tokens_moved = setup_sems["tokens_moved"]
    first_pe, first_dve, first_act = (setup_sems[f"first_{e}"] for e in ("pe", "dve", "act"))
    with nc.Block() as block:
        @block.sync
        def _(sp):
            sp.dma_start(x_in[:], x_src[0]).then_inc(tokens_moved, 16)
            sp.dma_start(raw[:, 0, :, :].rearrange("p t d -> p (t d)"), a["ctx"][0]).then_inc(setup_sems["load"], 16)
            more = [(w["wvo"][:].rearrange("p h f -> p (h f)"), scratch["wvo"][layer]),
                    (w["router"][:], a[f"router{n}"].rearrange("(k p) e -> p k e", p=128))]
            if layer == 0:
                more += [(cosq[:], a["cosq"]), (sinq[:], a["sinq"])]
            for dst, src in more:
                sp.dma_start(dst, src).then_inc(setup_sems["load"], 16)
            if layer == 0:
                sp.wait_ge(tokens_moved, 16)
                sp.dma_start(x_mid[G], x_in[:]).then_inc(setup_sems["load"], 16)
            sp.wait_ge(setup_sems["load"], 16 * (1 + len(more) + (layer == 0)))

        @block.tensor
        def _(pe):
            pe.wait_ge(tokens_moved, 16)
            for k in range(KT):
                mm = pe.matmul(region[2][:, 0:NT], c["mean_w"][:], x_in[:, k, :], start=(k == 0), stop=(k == KT - 1))
            mm.then_inc(first_pe, 1)
            pe.wait_ge(first_dve, 2)
            for k in range(KT):
                mm = pe.matmul(region[5][:, 0:NT], c["mean_w"][:], x_sq[:, k, :], start=(k == 0), stop=(k == KT - 1))
            mm.then_inc(first_pe, 1)

        @block.scalar
        def _(act):
            act.wait_ge(first_pe, 2)
            nc.scalar.activation(x_std[:], region[5][:, 0:NT], ACT.Sqrt, bias=c["eps"][:, 0:1]).then_inc(first_act, 1)
            act.wait_ge(first_dve, 4)
            nc.scalar.activation(x_high[:], x_n[:], ACT.Copy).then_inc(first_act, 1)

        @block.vector
        def _(dve):
            nc.vector.memset(kones[DC:DC + 1, :].bitcast(F32), 1.0)
            dve.wait_ge(first_pe, 1)
            nc.vector.tensor_tensor(x_cen[:], x_in[:], region[2][:, 0:NT].unsqueeze(1).broadcast_to([128, KT, NT]), ALU.subtract).then_inc(first_dve, 1)
            dve.wait_ge(first_dve, 1)
            nc.vector.tensor_tensor(x_sq[:], x_cen[:], x_cen[:], ALU.mult).then_inc(first_dve, 1)
            dve.wait_ge(first_act, 1)
            nc.vector.reciprocal(x_rstd[:], x_std[:]).then_inc(first_dve, 1)
            dve.wait_ge(first_dve, 3)
            nc.vector.tensor_tensor(x_n[:], x_cen[:], x_rstd[:].unsqueeze(1).broadcast_to([128, KT, NT]), ALU.mult).then_inc(first_dve, 1)
            dve.wait_ge(first_act, 2)
            nc.vector.tensor_tensor(x_low[:], x_n[:], x_high[:].bitcast(F32), ALU.subtract)
    nc.all_engine_barrier(sems_to_clear=setup_range)

    with nc.Fori(0, G) as g:
        with nc.Block() as block:
            @block.sync
            def _(sp):
                def weights_of(i):
                    if i >= WSLOT:
                        sp.wait_ge(s["down_done"], i - WSLOT + 1)
                    sp.dma_start(wexp_in[:, i % WSLOT, :], a["experts"][i]).then_inc(s[f"weights_loaded_{i % WSLOT}"], 16)

                def head_weights(h):
                    source = scratch["w1" if layer == 0 else "wabs"][h]
                    sp.dma_start(w_in[:, h % HSLOT, :, :].rearrange("p k q -> p (k q)"), source).then_inc(s[f"head_loaded_{h % HSLOT}"], 16)

                def second_weights(h):
                    sp.dma_start(w2[:, h % HSLOT, :, :].rearrange("p k q -> p (k q)"), scratch["w2"][h]).then_inc(s[f"second_loaded_{h % HSLOT}"], 16)

                for h in range(HSLOT):
                    head_weights(h)
                sp.dma_start(raw[:, 1, :, :].rearrange("p t d -> p (t d)"), a["ctx"][BG * g + 1]).then_inc(s["ctx_loaded_1"], 16)

                if layer == 0:
                    for h in range(HSLOT):
                        second_weights(h)
                for kind, key, _ in steps:
                    if kind == ("qwide", "query")[layer] and key[0] + HSLOT < H:
                        sp.wait_ge(*R.filled(kind, key[0]))
                        head_weights(key[0] + HSLOT)
                    if kind == "query" and layer == 0 and key[0] + HSLOT < H:
                        sp.wait_ge(*R.filled("query", key[0]))
                        second_weights(key[0] + HSLOT)
                    if kind == "rope" and key[0] + 2 <= BG:
                        j = key[0] + 2
                        sp.wait_ge(s["rope_done"], key[0] + 1)
                        sem = s[f"ctx_loaded_{j}"] if j < BG else s["next_loaded"]
                        sp.dma_start(raw[:, j % 2, :, :].rearrange("p t d -> p (t d)"), a["ctx"][BG * g + j]).then_inc(sem, 16)
                    if kind == "maxT":
                        j, = key
                        sp.wait_ge(*R.drained("maxT", j))
                        sp.dma_start(qlow[DC:DC + 1, j, :].bitcast(F32), maxrow[:, j % 2, :].bitcast(F32)).then_inc(s["shift_loaded"], 16)
                    if kind == "attn":
                        sp.wait_ge(*R.filled("norm", BG - 1))
                        if layer == 0:
                            for i in range(WSLOT):
                                weights_of(i)
                        for dst, src in ffn_loads:
                            sp.dma_start(dst, src).then_inc(s["ffn_loaded"], 16)
                        sp.wait_ge(*R.drained("attn"))
                        sp.dma_start(x_in[:], x_src[g + 1]).then_inc(s["next_loaded"], 16)
                if layer == 0:
                    for i in range(WSLOT, E0 + 1):
                        weights_of(i)
                sp.wait_ge(s["out_ready"], 2)
                sp.dma_start(x_dst[g], x_res[:]).then_inc(tokens_moved, 16)

            @block.tensor
            def _(pe):
                def split_product(dst, w_hi, w_lo, x_hi, x_lo, start, stop):
                    pe.matmul(dst, w_hi, x_hi, start=start, stop=False)
                    pe.matmul(dst, w_lo, x_hi, start=False, stop=False)
                    return pe.matmul(dst, w_hi, x_lo, start=False, stop=stop)

                for kind, key, reg in steps:
                    if reg is not None:
                        R.room(pe, kind, *key)
                        acc = region[reg]
                    if kind == "mean":
                        src = (x_res, x_in)[key[0]]
                        if key[0]:
                            pe.wait_ge(s["next_loaded"], 32)
                            if layer == 1:
                                pe.wait_ge(s["gate_copied"], MT)
                        for k in range(KT):
                            if not key[0]:
                                pe.wait_ge(*((s["res_half"], 1) if k == 0 else R.drained("attn")))
                            mm = pe.matmul(first_bank(reg), c["mean_w"][:], src[:, k, :], start=(k == 0), stop=(k == KT - 1))
                        mm.then_inc(*R.signal_filled(kind, *key))
                    elif kind == "var":
                        for k in range(KT):
                            pe.wait_ge(s[("sq_half", "squared")[k]], key[0] + 1)
                            mm = pe.matmul(first_bank(reg), c["mean_w"][:], x_sq[:, k, :], start=(k == 0), stop=(k == KT - 1))
                        mm.then_inc(*R.signal_filled(kind, *key))
                    elif kind == "keyT":
                        j, b = key
                        pe.wait_ge(s["rope_done"], j + 1)
                        for i in range(4):
                            mm = pe.transpose(acc[0:DC, i * LP:(i + 1) * LP], kv[:, j % 3, 4 * b + i, :], c["ident"][0:LP, 0:LP])
                        mm.then_inc(*R.signal_filled(kind, *key))
                    elif kind == "qwide":
                        h, = key
                        pe.wait_ge(s["w_low"], h + 1)
                        for half in range(2):
                            cols = slice(half * HALF, (half + 1) * HALF)
                            for k in range(KT):
                                mm = split_product(acc[0:HALF, half, 0:NT], w_high[:, h % HSLOT, k, cols], w_low[:, h % HSLOT, k, cols],
                                                   x_high[:, k, :], x_low[:, k, :], k == 0, k == KT - 1)
                        mm.then_inc(*R.signal_filled(kind, *key))
                    elif kind == "query":
                        h, = key
                        dst = acc[:, 0, 0:NT] if reg < 2 else acc[:, 0:NT]
                        if layer == 0:
                            pe.wait_ge(s["qrot"], 2 * (h + 1))
                            pe.wait_ge(s[f"second_loaded_{h % HSLOT}"], 16 * (h // HSLOT + 1))
                            for half in range(2):
                                mm = pe.matmul(dst, w2[:, h % HSLOT, half, :], qr[:, h % 2, half, :], start=(half == 0), stop=(half == 1))
                        else:
                            pe.wait_ge(s["w_low"], h + 1)
                            for k in range(KT):
                                mm = split_product(dst, w_high[:, h % HSLOT, k, :], w_low[:, h % HSLOT, k, :],
                                                   x_high[:, k, :], x_low[:, k, :], k == 0, k == KT - 1)
                        mm.then_inc(*R.signal_filled(kind, *key))
                    elif kind == "smax":
                        j, t, b = key
                        if b == 0:
                            pe.wait_ge(*R.drained("query", head_rows(t)))
                            if t == 0:
                                for i in range(3):
                                    pe.wait_ge(*R.drained("keyT", j, i))
                        pe.matmul(acc[:, 0:LB], qhigh[:, j, t * 128:(t + 1) * 128], kparts[:, kdst(j), b * LB:(b + 1) * LB],
                                  start=True, stop=True).then_inc(*R.signal_filled(kind, *key))
                    elif kind == "maxT":
                        j, = key
                        pe.wait_ge(s["maxneg"], j + 1)
                        pe.matmul(acc[0:NMAX, 0:128], maxneg[:, j % 2, :], c["ident"][:], start=True, stop=True)\
                            .then_inc(*R.signal_filled(kind, *key))
                    elif kind == "score":
                        j, t = key
                        if t == 0:
                            pe.wait_ge(s["shift_loaded"], 16 * (j + 1))
                            pe.wait_ge(*R.drained("query", H - 1))
                        pe.wait_ge(s["keyone"], 3 * j + t // 4 + 1)
                        cols = slice(t * LP, (t + 1) * LP)
                        for half in range(2):
                            q = slice(half * HQ, (half + 1) * HQ)
                            pe.matmul(acc[0:LP, half, 0:HQ], kparts[:, kdst(j), cols], qhigh[:, j, q], start=True, stop=False)
                        for half in range(2):
                            q = slice(half * HQ, (half + 1) * HQ)
                            mm = pe.matmul(acc[0:LP, half, 0:HQ], kones[:, cols], qlow[:, j, q], start=False, stop=True)
                        mm.then_inc(*R.signal_filled(kind, *key))
                    elif kind == "mix":
                        j, t = key
                        if t == 0 and j:
                            pe.wait_ge(s["mixed"], j)
                        if t == 0 and not j:
                            last = H - 1 if layer == 0 else max(h for h in range(H) if h % 3 == 2)
                            pe.wait_ge(*R.drained("query", last))
                        pe.wait_ge(*R.drained("score", j, t))
                        for half in range(2):
                            mm = pe.matmul(mix_acc[64 * half:64 * half + DC, 0:HQ], kv[:, j % 3, t, :],
                                           prob[:, (j * LT + t) % NPROB, half * HQ:(half + 1) * HQ], start=(t == 0), stop=(t == LT - 1))
                        mm.then_inc(s["premix"], 1)
                    elif kind == "norm":
                        j, = key
                        pe.wait_ge(s["dve_sum"], vector_sums(j + 1))
                        for half in range(2):
                            mm = pe.matmul(acc[64 * half:64 * half + DC, 0:HQ], c["ones"][0:LP, :],
                                           sum_dve[:, half * HQ:(half + 1) * HQ], start=True, stop=True)
                        mm.then_inc(*R.signal_filled(kind, *key))
                    elif kind == "attn":
                        pe.wait_ge(s["ctx_ready"], BG)
                        for m in range(KT):
                            for i in range(H // 2):
                                if m == 0 and i == H // 4:
                                    pe.wait_ge(s["ctx_ready"], BG + 1)
                                mm = pe.matmul(acc[:, m, 0:NT].rearrange("p (j s) -> p j s", j=BG), w["wvo"][:, i, m * 128:(m + 1) * 128],
                                               ctx_n[:, :, i * S:(i + 1) * S], start=(i == 0), stop=(i == H // 2 - 1))
                            if m == 0:
                                mm.then_inc(s["attn_half"], 1)
                        mm.then_inc(*R.signal_filled(kind, *key))
                    elif kind == "route":
                        for i in range(RT):
                            pe.wait_ge(s["normed"], 1 + 2 * i // RT)
                            for k in range(KT):
                                mm = pe.matmul(acc[0:TR, 0, i * NE:(i + 1) * NE], x_n[:, k, i * TR:(i + 1) * TR], w["router"][:, k, :],
                                               start=(k == 0), stop=(k == KT - 1))
                        mm.then_inc(*R.signal_filled(kind, *key))
                    elif kind == "gateup" and layer == 0:
                        i, = key
                        if i == 0:
                            pe.wait_ge(s["x_low"], 1)
                        pe.wait_ge(s["e_low"], i + 1)
                        for half in range(2):
                            for k in range(KT):
                                at = slice((half * KT + k) * I0, (half * KT + k + 1) * I0)
                                mm = split_product(acc[:, half, 0:NT], wexp_high[:, i % WSLOT, at], wexp_low[:, i % WSLOT, at],
                                                   x_high[:, k, :], x_low[:, k, :], k == 0, k == KT - 1)
                        mm.then_inc(*R.signal_filled(kind, *key))
                    elif kind == "weight":
                        i, = key
                        if i == 1:
                            pe.wait_ge(*R.drained("cwT"))
                        pe.matmul(acc[:, 0:NT], c["pick"][:, i - 1:i].broadcast_to([32 + E0, 128]), cwT[:], start=True, stop=True)\
                            .then_inc(*R.signal_filled(kind, *key))
                    elif kind == "cwT":
                        pe.wait_ge(s["routed"], 1)
                        for r in range(RT):
                            mm = pe.matmul(acc[0:E0, r * TR:(r + 1) * TR], cw[:, r, :], c["ident"][0:TR, 0:TR], start=True, stop=True)
                        mm.then_inc(*R.signal_filled(kind, *key))
                    elif kind == "down" and layer == 0:
                        i, = key
                        if i == 0:
                            pe.wait_ge(s["normed"], 2)
                        pe.wait_ge(s["hid_low"], i + 1)
                        for m in range(KT):
                            at = slice(2 * D + m * 128, 2 * D + (m + 1) * 128)
                            mm = split_product(region[(2, 5)[m]][:, 0:NT], wexp_high[:, i % WSLOT, at], wexp_low[:, i % WSLOT, at],
                                               hid_high[:, i % 2, :], hid_low[:, i % 2, :], i == 0, i == E0)
                        mm.then_inc(s["down_done"], 1)
                    elif kind == "lora":
                        pe.wait_ge(s["x_low"], 1)
                        pe.wait_ge(s["ffn_low"], 2)
                        for half, name in enumerate(("upA", "gateA")):
                            for k in range(KT):
                                mm = split_product(acc[:, half, 0:NT], w[name + "_high"][:, k, :], w[name][:, k, :],
                                                   x_high[:, k, :], x_low[:, k, :], k == 0, k == KT - 1)
                        mm.then_inc(*R.signal_filled(kind, *key))
                    elif kind == "tokw":
                        for slot in range(2):
                            for r in range(RT):
                                mm = pe.matmul(acc[:, slot, r * TR:(r + 1) * TR], tokw[:, slot, r:r + 1].broadcast_to([TR, 128]), c["ident"][0:TR, 0:TR],
                                               start=True, stop=True)
                        mm.then_inc(*R.signal_filled(kind, *key))
                    elif kind == "mask":
                        pe.wait_ge(s["routed"], 1)
                        for slot in range(2):
                            for r in range(RT):
                                mm = pe.matmul(acc[:, slot, r * TR:(r + 1) * TR], mask_rows[:, slot, r, :],
                                               c["ident"][0:TR, 0:TR], start=True, stop=True)
                        mm.then_inc(*R.signal_filled(kind, *key))
                    elif kind == "gateup":
                        m, slot = key
                        M = min(128, HID - m * 128)
                        cols = slice(m * 128, m * 128 + M)
                        if m == 0 and slot == 0:
                            pe.wait_ge(s["ffn_low"], len(split_names))
                        elif slot == 0:
                            pe.wait_ge(s["gate_copied"], m)
                        for half, (base, low) in enumerate((("up", "upB"), ("gate", "gateB"))):
                            dst = acc[0:M, half, 0:NT]
                            if slot == 0:
                                for k in range(KT):
                                    split_product(dst, w[base + "_high"][:, k, cols], w[base][:, k, cols], x_high[:, k, :], x_low[:, k, :], k == 0, False)
                            if m == 0 and half == 0:
                                pe.wait_ge(s["lora_low"], slot + 1)
                            mm = split_product(dst, w[low + "_high"][:, cols], w[low][:, cols], lora_high[:, slot, half, :], lora_low[:, slot, half, :], slot == 1, True)
                        mm.then_inc(*R.signal_filled(kind, *key))
                    elif kind == "down":
                        m, = key
                        M = min(128, HID - m * 128)
                        if m == 0:
                            pe.wait_ge(s["normed"], 2)
                        pe.wait_ge(s["hid_ready"], 2 * (m + 1))
                        for slot in range(2):
                            pe.matmul(region[3 + 2 * slot][:, 0:NT], w["downA"][0:M, m, :], hid[0:M, m % 2, slot, :],
                                      start=(m == 0), stop=(m == MT - 1))
                        pe.wait_ge(s["acc_done"], m + 1)
                        for q in range(KT):
                            mm = pe.matmul(region[(2, 4)[q]][:, 0:NT], w["down"][0:M, m, q * 128:(q + 1) * 128], hsum[0:M, m % 2, :],
                                           start=(m == 0), stop=False)
                        mm.then_inc(s["down_done"], 1)
                    elif kind == "loradown":
                        pe.wait_ge(s["lora_z"], 2)
                        for q in range(KT):
                            for slot in range(2):
                                mm = pe.matmul(region[(2, 4)[q]][:, 0:NT], w["downB"][:, q * 128:(q + 1) * 128], lora_z[:, slot, :],
                                               start=False, stop=(slot == 1))
                        mm.then_inc(s["down_done"], 1)

            @block.scalar
            def _(act):
                for kind, key, reg in steps:
                    if reg is not None:
                        acc = region[reg]
                    if kind == "mean":
                        if not key[0]:
                            nc.scalar.activation(table_probe[:, 0:1], c["eps"][:], ACT.Sqrt)
                    elif kind == "var":
                        act.wait_ge(*R.filled(kind, *key))
                        if key[0]:
                            act.wait_ge(s["rstd"], 2)
                        nc.scalar.activation(x_std[:], first_bank(reg), ACT.Sqrt, bias=c["eps"][:, 0:1]).then_inc(*R.signal_drained(kind, *key))
                    elif kind == "wsplit":
                        h, = key
                        act.wait_ge(s[f"head_loaded_{h % HSLOT}"], 16 * (h // HSLOT + 1))
                        nc.scalar.activation(w_high[:, h % HSLOT, :, :], w_in[:, h % HSLOT, :, :], ACT.Copy).then_inc(s["w_high"], 1)
                    elif kind == "xsplit":
                        act.wait_ge(s["normed"], 2 * (key[0] + 1))
                        if key[0]:
                            act.wait_ge(*R.filled("gateup", *((E0,), (MT - 1, 0))[layer]))
                        nc.scalar.activation(x_high[:], x_n[:], ACT.Copy).then_inc(s["x_high"], 1)
                        nc.scalar.activation(table_probe[:, key[0] + 1:key[0] + 2], c["eps"][:], ACT.Exp)
                    elif kind == "esplit":
                        i, = key
                        act.wait_ge(s[f"weights_loaded_{i % WSLOT}"], 16 * (i // WSLOT + 1))
                        nc.scalar.activation(wexp_high[:, i % WSLOT, :], wexp_in[:, i % WSLOT, :], ACT.Copy).then_inc(s["e_high"], 1)
                    elif kind == "hidden":
                        i, = key
                        if i:
                            act.wait_ge(*R.drained("gateup", i))
                        else:
                            act.wait_ge(s["shared_hid"], 1)
                        if i >= 2:
                            act.wait_ge(s["down_done"], i - 1)
                        nc.scalar.activation(hid_high[:, i % 2, :], hid[:, i % 2, :], ACT.Copy).then_inc(s["hid_high"], 1)
                    elif kind == "cwT":
                        act.wait_ge(*R.filled(kind))
                        nc.scalar.activation(cwT[0:E0, :], acc[0:E0, 0:NT], ACT.Copy).then_inc(s["cw_high"], 1)
                    elif kind == "attn" and layer == 1:
                        act.wait_ge(s["ffn_loaded"], 16 * len(ffn_loads))
                        for name in split_names:
                            nc.scalar.activation(w[name + "_high"][:], w[name + "_in"][:], ACT.Copy).then_inc(s["ffn_high"], 1)
                    elif kind == "mask":
                        act.wait_ge(*R.filled(kind))
                        nc.scalar.activation(maskT[:], acc[:, :, 0:NT], ACT.Copy).then_inc(*R.signal_drained(kind))
                        act.wait_ge(s["lora_in"], 3)
                        act.wait_ge(*R.drained("lora"))
                        for slot in range(2):
                            nc.scalar.activation(lora_high[:, slot, :, :], lora_in[:, slot, :, :], ACT.Copy).then_inc(s["lora_high"], 1)
                    elif kind == "keyT":
                        j, b = key
                        cols = slice(b * LB, (b + 1) * LB)
                        act.wait_ge(*R.filled(kind, *key))
                        nc.scalar.activation(kparts[0:DC, kdst(j), cols], acc[0:DC, 0:LB], ACT.Copy).then_inc(s["keyh"], 1)
                    elif kind == "kone":
                        j, b = key
                        cols = slice(b * LB, (b + 1) * LB)
                        act.wait_ge(s["keyh"], 3 * j + b + 1)
                        if j:
                            act.wait_ge(*R.filled("score", j - 1, 4 * b + 3))
                        nc.scalar.activation(kones[0:DC, cols], kparts[0:DC, kdst(j), cols].bitcast(F32), ACT.Copy).then_inc(s["keyone"], 1)
                    elif kind == "query":
                        h, = key
                        src = acc[:, 0, 0:NT] if reg < 2 else acc[:, 0:NT]
                        act.wait_ge(*R.filled(kind, *key))
                        nc.scalar.activation(qhigh[:, :, h * S:(h + 1) * S], src.rearrange("p (j s) -> p j s", j=BG), ACT.Copy)\
                            .then_inc(s["qhigh"], 1)
                    elif kind == "maxT":
                        j, = key
                        act.wait_ge(*R.filled(kind, *key))
                        if j >= 2:
                            act.wait_ge(s["shift_loaded"], 16 * (j - 1))
                        nc.scalar.activation(maxrow[:, j % 2, :], acc[0:NMAX, 0:128], ACT.Copy).then_inc(*R.signal_drained(kind, *key))
                    elif kind == "score":
                        j, t = key
                        n_ = j * LT + t
                        act.wait_ge(*R.filled(kind, *key))
                        if n_ >= NPROB:
                            act.wait_ge(s["premix"], n_ - NPROB + 1)
                            jo, to = divmod(n_ - NPROB, LT)
                            if to < pool_tiles(jo):
                                act.wait_ge(s["pool_sum"], pool_sums(jo) + max(1, to))
                            else:
                                act.wait_ge(s["dve_sum"], vector_sums(jo) + max(1, to - pool_tiles(jo)))
                        nc.scalar.activation(prob[:, n_ % NPROB, :].rearrange("p (a b) -> p a b", a=2), acc[0:LP, :, 0:HQ], ACT.Exp)\
                            .then_inc(*R.signal_drained(kind, *key))
                    elif kind == "context":
                        j, = key
                        act.wait_ge(s["premix"], LT * (j + 1))
                        if j >= 2:
                            act.wait_ge(s["ctx_ready"], j - 1)
                        nc.scalar.activation(ctx_raw[:, j % 2, :], mix_acc[:, 0:HQ], ACT.Copy).then_inc(s["mixed"], 1)
                    elif kind == "norm" and key[0] < BG - 1:
                        j, = key
                        act.wait_ge(*R.filled(kind, *key))
                        if j:
                            act.wait_ge(s["recip"], 2 * j)
                        nc.scalar.activation(total[:], acc[:, 0:HQ], ACT.Copy).then_inc(*R.signal_drained(kind, *key))
                    elif kind == "route" and layer == 0:
                        act.wait_ge(*R.filled(kind))
                        nc.scalar.activation(rt1[:], acc[0:TR, 0, 0:RT * NE].rearrange("p (a e) -> p a e", a=RT), ACT.Exp, scale=-1.0)\
                            .then_inc(*R.signal_drained(kind))
                    elif kind == "tokw":
                        act.wait_ge(*R.drained(kind))
                        nc.scalar.activation(tok[:], tok[:], ACT.Exp).then_inc(s["tok_exp"], 1)
                    elif kind == "gateup" and layer == 0:
                        i, = key
                        act.wait_ge(*R.filled(kind, *key))
                        if i >= 2:
                            if i == 2:
                                act.wait_ge(s["shared_hid"], 1)
                            act.wait_ge(*R.drained(kind, i - 2))
                        nc.scalar.activation(gact[:, i % 2, :], acc[:, 0, 0:NT], ACT.Silu).then_inc(s["gate_act"], 1)
                        if i == 0:
                            nc.scalar.activation(shared_up[:], acc[:, 1, 0:NT], ACT.Copy).then_inc(*R.signal_drained(kind, *key))
                    elif kind == "gateup":
                        m, slot = key
                        M = min(128, HID - m * 128)
                        if slot == 0:
                            act.wait_ge(*R.filled(kind, *key))
                            gate_src = acc[0:M, 0, 0:NT]
                            if m:
                                act.wait_ge(s["hid_ready"], 2 * m)
                                act.wait_ge(s["gate_act"], 2 * m)
                        else:
                            act.wait_ge(*R.drained(kind, *key))
                            gate_src = gate_up[0:M, 0, :]
                        if m:
                            act.wait_ge(s["hid_ready"], 2 * (m - 1) + slot + 1)
                        nc.scalar.activation(sact[0:M, slot, :], gate_src, ACT.Silu).then_inc(s["gate_act"], 1)
                        if slot == 0:
                            nc.scalar.activation(gate_up[0:M, :, :], acc[0:M, :, 0:NT], ACT.Copy).then_inc(s["gate_copied"], 1)

            @block.gpsimd
            def _(pool):
                for kind, key, reg in steps:
                    if kind == "wsplit":
                        h, = key
                        w_slot = w_low[:, h % HSLOT, :, :]
                        pool.wait_ge(s["w_high"], h + 1)
                        nc.gpsimd.tensor_tensor(w_slot, w_in[:, h % HSLOT, :, :], w_high[:, h % HSLOT, :, :].bitcast(F32), ALU.subtract).then_inc(s["w_low"], 1)
                    elif kind == "esplit":
                        i, = key
                        w_slot = wexp_low[:, i % WSLOT, :]
                        pool.wait_ge(s["e_high"], i + 1)
                        nc.gpsimd.tensor_tensor(w_slot, wexp_in[:, i % WSLOT, :], wexp_high[:, i % WSLOT, :].bitcast(F32), ALU.subtract).then_inc(s["e_low"], 1)
                    elif kind == "gateup" and layer == 0 and key[0] == 0:
                        pool.wait_ge(s["gate_act"], 1)
                        pool.wait_ge(*R.drained(kind, 0))
                        nc.gpsimd.tensor_tensor(hid[:, 0, :], gact[:, 0, :], shared_up[:], ALU.mult).then_inc(s["shared_hid"], 1)
                    elif kind == "hidden" and key[0] == 0:
                        pool.wait_ge(s["hid_high"], 1)
                        nc.gpsimd.tensor_tensor(hid_low[:, 0, :], hid[:, 0, :], hid_high[:, 0, :].bitcast(F32), ALU.subtract).then_inc(s["hid_low"], 1)
                    elif kind == "attn" and layer == 1:
                        for i, name in enumerate(split_names):
                            pool.wait_ge(s["ffn_high"], i + 1)
                            nc.gpsimd.tensor_tensor(w[name][:], w[name + "_in"][:], w[name + "_high"][:].bitcast(F32), ALU.subtract)\
                                .then_inc(s["ffn_low"], 1)
                    elif kind == "rotate":
                        j, = key
                        if j:
                            pool.wait_ge(s["rope_done"], j)
                        if 1 <= j:
                            pool.wait_ge(s[f"ctx_loaded_{j}"], 16)
                        r = raw[:, j % 2, :, :]
                        hd = DC // 2
                        nc.gpsimd.tensor_tensor(rope_s[:, :, 0:hd], r[:, :, hd:DC], c["sink"][:, :, 0:hd], ALU.mult).then_inc(s["rope_sin"], 1)
                        nc.gpsimd.tensor_tensor(rope_s[:, :, hd:DC], r[:, :, 0:hd], c["sink"][:, :, hd:DC], ALU.mult).then_inc(s["rope_sin"], 1)
                    elif kind == "qwide":
                        h, = key
                        pool.wait_ge(s["qcos"], h + 1)
                        pool.wait_ge(*R.drained("qwide", h))
                        if h >= 2:
                            pool.wait_ge(*R.filled("query", h - 2))
                        for half in range(2):
                            nc.gpsimd.tensor_tensor(qr[:, h % 2, half, :], qa[:, h % 2, half, :], qb[:, h % 2, 1 - half, :], ALU.add)\
                                .then_inc(s["qrot"], 1)
                    elif kind == "mix":
                        j, t = key
                        if 1 <= t < pool_tiles(j):
                            pool.wait_ge(*R.drained("score", j, t))
                            n_ = j * LT + t
                            dst = sum_pool[:, j % 2, :]
                            if t == 1:
                                if j >= 2:
                                    pool.wait_ge(s["dve_sum"], vector_sums(j - 1))
                                first_in = prob[:, (n_ - 1) % NPROB, :]
                            else:
                                pool.wait_ge(s["pool_sum"], pool_sums(j) + t - 1)
                                first_in = dst
                            nc.gpsimd.tensor_tensor(dst, first_in, prob[:, n_ % NPROB, :], ALU.add).then_inc(s["pool_sum"], 1)
                    elif kind == "gateup" and layer == 1 and key[1] == 1:
                        m, _ = key
                        M = min(128, HID - m * 128)
                        pool.wait_ge(s["hid_ready"], 2 * (m + 1))
                        if m >= 2:
                            pool.wait_ge(s["down_done"], m - 1)
                        nc.gpsimd.tensor_tensor(hsum[0:M, m % 2, :], hid[0:M, m % 2, 0, :], hid[0:M, m % 2, 1, :], ALU.add)\
                            .then_inc(s["acc_done"], 1)

            @block.vector
            def _(dve):
                V = nc.vector
                forks = [0]

                def then(ins):
                    forks[0] += 1
                    ins.then_inc(s["route_step"], 1)
                    dve.wait_ge(s["route_step"], forks[0])

                def ranks(v, groups, width, tie, dst):
                    shape = [TR, groups, width, width]
                    gt = cmp1[:, 0:groups * width * width].rearrange("p (g a b) -> p g a b", g=groups, a=width)
                    eq = cmp2[:, 0:groups * width * width].rearrange("p (g a b) -> p g a b", g=groups, a=width)
                    other = v.unsqueeze(2).broadcast_to(shape)
                    own = v.unsqueeze(3).broadcast_to(shape)
                    V.tensor_tensor(gt, other, own, ALU.is_gt)
                    then(V.tensor_tensor(eq, other, own, ALU.is_equal))
                    flat_eq = cmp2[:, 0:groups * width * width].rearrange("p (g x) -> p g x", g=groups)
                    then(V.tensor_tensor(flat_eq, flat_eq, tie[:].unsqueeze(1).broadcast_to([TR, groups, width * width]), ALU.mult))
                    then(V.tensor_tensor(gt, gt, eq, ALU.add))
                    then(V.tensor_reduce(dst, gt, AX.X, ALU.add))

                for kind, key, reg in steps:
                    if reg is not None:
                        acc = region[reg]
                    if kind == "rope":
                        j, = key
                        r = raw[:, j % 2, :, :]
                        if j:
                            dve.wait_ge(s[f"ctx_loaded_{j}"], 16)
                            dve.wait_ge(s["rope_done"], j)
                        V.tensor_tensor(rope_c[:], r, c["cosk"][:], ALU.mult).then_inc(s["rope_cos"], 1)
                        dve.wait_ge(s["rope_cos"], j + 1)
                        dve.wait_ge(s["rope_sin"], 2 * (j + 1))
                        if j >= 3:
                            dve.wait_ge(s["premix"], LT * (j - 2))
                        V.tensor_tensor(kv[:, j % 3, :, :], rope_c[:], rope_s[:], ALU.add).then_inc(s["rope_done"], 1)
                    elif kind == "mean":
                        src = (x_res, x_in)[key[0]]
                        dve.wait_ge(*R.filled(kind, *key))
                        if key[0]:
                            dve.wait_ge(s["normed"], 2)
                            dve.wait_ge(s["x_low"], 1)
                        for k in range(KT):
                            last = k == KT - 1
                            V.tensor_tensor(x_cen[:, k, :], src[:, k, :], first_bank(reg), ALU.subtract)\
                                .then_inc(*(R.signal_drained(kind, *key) if last else (s["cen_half"], 1)))
                            dve.wait_ge(*(R.drained(kind, *key) if last else (s["cen_half"], key[0] + 1)))
                            V.tensor_tensor(x_sq[:, k, :], x_cen[:, k, :], x_cen[:, k, :], ALU.mult).then_inc(s[("sq_half", "squared")[k]], 1)
                    elif kind == "rstd":
                        which, part = key
                        cols = slice(part * NT // 2, (part + 1) * NT // 2)
                        if part == 0:
                            dve.wait_ge(*R.drained("var", which))
                        V.reciprocal(x_rstd[:, cols], x_std[:, cols]).then_inc(s["rstd"], 1)
                        dve.wait_ge(s["rstd"], 2 * which + part + 1)
                        if which == 0:
                            dve.wait_ge(*R.filled("query", H - 1))
                        V.tensor_tensor(x_n[:, :, cols], x_cen[:, :, cols], x_rstd[:, cols].unsqueeze(1).broadcast_to([128, KT, NT // 2]), ALU.mult)\
                            .then_inc(s["normed"], 1)
                    elif kind == "keyT":
                        j, b = key
                        cols = slice(b * LB, (b + 1) * LB)
                        dve.wait_ge(s["keyh"], 3 * j + b + 1)
                        V.tensor_tensor(kparts[DC:2 * DC, kdst(j), cols], acc[0:DC, 0:LB], kparts[0:DC, kdst(j), cols].bitcast(F32), ALU.subtract)\
                            .then_inc(*R.signal_drained(kind, *key))
                    elif kind == "xsplit":
                        dve.wait_ge(s["x_high"], key[0] + 1)
                        V.tensor_tensor(x_low[:], x_n[:], x_high[:].bitcast(F32), ALU.subtract).then_inc(s["x_low"], 1)
                    elif kind == "cwT":
                        dve.wait_ge(s["cw_high"], 1)
                        V.tensor_tensor(cwT[32:32 + E0, :], acc[0:E0, 0:NT], cwT[0:E0, :].bitcast(F32), ALU.subtract).then_inc(*R.signal_drained(kind))
                    elif kind == "hidden":
                        i, = key
                        if i == 0:
                            continue
                        dve.wait_ge(s["hid_high"], i + 1)
                        V.tensor_tensor(hid_low[:, i % 2, :], hid[:, i % 2, :], hid_high[:, i % 2, :].bitcast(F32), ALU.subtract).then_inc(s["hid_low"], 1)
                    elif kind == "qwide":
                        h, = key
                        src = acc[0:HALF, :, 0:NT]
                        dve.wait_ge(*R.filled(kind, *key))
                        if h >= 2:
                            dve.wait_ge(s["qrot"], 2 * (h - 1))
                        V.tensor_tensor(qa[:, h % 2, :, :], src, cosq[:], ALU.mult).then_inc(s["qcos"], 1)
                        V.tensor_tensor(qb[:, h % 2, :, :], src, sinq[:], ALU.mult).then_inc(*R.signal_drained(kind, *key))
                    elif kind == "query":
                        h, = key
                        cols = slice(h * S, (h + 1) * S)
                        src = acc[0:DC, 0, 0:NT] if reg < 2 else acc[0:DC, 0:NT]
                        dve.wait_ge(s["qhigh"], h + 1)
                        V.tensor_tensor(qlow[0:DC, :, cols], src.rearrange("p (j s) -> p j s", j=BG), qhigh[0:DC, :, cols].bitcast(F32), ALU.subtract)\
                            .then_inc(*R.signal_drained(kind, *key))
                    elif kind == "smax":
                        j, t, b = key
                        dve.wait_ge(*R.filled(kind, *key))
                        V.tensor_reduce(maxpart[:, j % 2, t, b:b + 1], acc[:, 0:LB], AX.X, ALU.max).then_inc(*R.signal_drained(kind, *key))
                    elif kind == "maxneg":
                        j, = key
                        if j >= 2:
                            dve.wait_ge(*R.filled("maxT", j - 2))
                        for b in range(3):
                            dve.wait_ge(*R.drained("smax", j, NMAX - 1, b))
                        V.tensor_reduce(maxneg[:, j % 2, :], maxpart[:, j % 2, :, :], AX.X, ALU.max, negate=True).then_inc(s["maxneg"], 1)
                    elif kind == "mix":
                        j, t = key
                        if t > pool_tiles(j):
                            n_ = j * LT + t
                            dve.wait_ge(*R.drained("score", j, t))
                            dst = sum_dve[:]
                            if t == pool_tiles(j) + 1:
                                if j:
                                    dve.wait_ge(*R.filled("norm", j - 1))
                                first_in = prob[:, (n_ - 1) % NPROB, :]
                            else:
                                dve.wait_ge(s["dve_sum"], vector_sums(j) + t - pool_tiles(j) - 1)
                                first_in = dst
                            V.tensor_tensor(dst, first_in, prob[:, n_ % NPROB, :], ALU.add).then_inc(s["dve_sum"], 1)
                    elif kind == "context":
                        j, = key
                        dve.wait_ge(s["dve_sum"], vector_sums(j + 1) - 1)
                        dve.wait_ge(s["pool_sum"], pool_sums(j) + pool_tiles(j) - 1)
                        V.tensor_tensor(sum_dve[:], sum_dve[:], sum_pool[:, j % 2, :], ALU.add).then_inc(s["dve_sum"], 1)
                    elif kind == "share":
                        j, part = key
                        if part == 0:
                            dve.wait_ge(*(R.drained if j < BG - 1 else R.filled)("norm", j))
                            if j:
                                dve.wait_ge(s["ctx_ready"], j)
                        if j == BG - 1 and part >= 2:
                            cols = slice((part - 2) * HQ // 2, (part - 1) * HQ // 2)
                            dve.wait_ge(*((s["recip"], 2 * j + 1) if part == 2 else R.drained("norm", j)))
                            dve.wait_ge(s["mixed"], BG)
                            V.tensor_tensor(ctx_n[:, j, cols], ctx_raw[:, j % 2, cols], recip[:, cols], ALU.mult).then_inc(s["ctx_ready"], 1)
                        elif part < 2:
                            cols = slice(part * HQ // 2, (part + 1) * HQ // 2)
                            sums = total if j < BG - 1 else region[R.at["norm", (j,)][0]]
                            V.reciprocal(recip[:, cols], sums[:, cols])\
                                .then_inc(*(R.signal_drained("norm", j) if j == BG - 1 and part else (s["recip"], 1)))
                        else:
                            dve.wait_ge(s["recip"], 2 * (j + 1))
                            dve.wait_ge(s["mixed"], j + 1)
                            V.tensor_tensor(ctx_n[:, j, :], ctx_raw[:, j % 2, :], recip[:], ALU.mult).then_inc(s["ctx_ready"], 1)
                    elif kind == "attn":
                        dve.wait_ge(s["attn_half"], 1)
                        dve.wait_ge(tokens_moved, 16 * (g + 1))
                        V.tensor_tensor(x_res[:, 0, :], acc[:, 0, 0:NT], x_in[:, 0, :], ALU.add).then_inc(s["res_half"], 1)
                        dve.wait_ge(*R.filled(kind, *key))
                        V.tensor_tensor(x_res[:, 1, :], acc[:, 1, 0:NT], x_in[:, 1, :], ALU.add).then_inc(*R.signal_drained(kind, *key))
                    elif kind == "route" and layer == 0:
                        then(V.memset(cwT[:].bitcast(F32), 0.0))
                        dve.wait_ge(*R.drained(kind))
                        then(V.tensor_scalar(rt2[:], rt1[:], 1.0, None, ALU.add))
                        then(V.reciprocal(score[:], rt2[:]))
                        then(V.tensor_tensor(rt1[:], score[:], c["bias0"][:].unsqueeze(1).broadcast_to([TR, RT, NE]), ALU.add))
                        quads = rt1[:].rearrange("p a (g b) -> p (a g) b", g=GRP0)
                        quad2 = rt2[:].rearrange("p a (g b) -> p (a g) b", g=GRP0)
                        quad3 = rt3[:].rearrange("p a (g b) -> p (a g) b", g=GRP0)
                        ranks(quads, RT * GRP0, E0 // GRP0, c["tie4"], quad2)
                        then(V.tensor_scalar(rt2[:], rt2[:], 2.0, None, ALU.is_lt))
                        then(V.tensor_tensor(rt2[:], rt2[:], rt1[:], ALU.mult))
                        then(V.tensor_reduce(rg1[:].rearrange("p a g -> p (a g)"), quad2, AX.X, ALU.add))
                        ranks(rg1[:], RT, GRP0, c["tie4"], rg2[:])
                        then(V.tensor_scalar(rg2[:], rg2[:], 2.0, None, ALU.is_lt))
                        pick = rg2[:].rearrange("p a g -> p (a g)").unsqueeze(2).broadcast_to([TR, RT * GRP0, E0 // GRP0])
                        then(V.tensor_tensor(quad3, quads, pick, ALU.mult))
                        then(V.tensor_scalar(rg2[:], rg2[:], 1.0, -NEG, ALU.subtract, ALU.mult))
                        then(V.tensor_tensor(quad3, quad3, pick, ALU.add))
                        ranks(rt3[:], RT, E0, c["tie16"], rt4[:])
                        then(V.tensor_scalar(rt4[:], rt4[:], float(TOP0), None, ALU.is_lt))
                        then(V.tensor_tensor(rt4[:], rt4[:], score[:], ALU.mult))
                        then(V.tensor_reduce(rs1[:], rt4[:], AX.X, ALU.add))
                        then(V.tensor_scalar(rs1[:], rs1[:], 1e-20, None, ALU.add))
                        then(V.reciprocal(rs2[:], rs1[:]))
                        then(V.tensor_tensor(rt4[:], rt4[:], rs2[:].unsqueeze(2).broadcast_to([TR, RT, NE]), ALU.mult))
                        V.tensor_scalar(cw[:], rt4[:], 2.5, None, ALU.mult).then_inc(s["routed"], 1)
                    elif kind == "route":
                        dve.wait_ge(*R.filled(kind))
                        V.tensor_copy(score[:], acc[0:TR, 0, 0:RT * NE].rearrange("p (a e) -> p a e", a=RT)).then_inc(*R.signal_drained(kind))
                        dve.wait_ge(*R.drained(kind))
                        ranks(score[:], RT, NE, c["tie8"], rt1[:])
                        for slot in range(2):
                            then(V.tensor_scalar(mask[:, slot, :, :], rt1[:], float(slot), None, ALU.is_equal))
                            then(V.tensor_tensor(tokm[:, slot, :, :], mask[:, slot, :, :], score[:], ALU.mult))
                        then(V.tensor_copy(mask_rows.rearrange("p a b (e r) -> p (a b e) r", r=RANK),
                                           mask[:].rearrange("p a b e -> p (a b e)").unsqueeze(2).broadcast_to([TR, 2 * RT * E1, RANK])))
                        V.tensor_reduce(tokw[:], tokm[:], AX.X, ALU.add).then_inc(s["routed"], 1)
                    elif kind == "tokw":
                        dve.wait_ge(*R.filled(kind))
                        v = acc[:, :, 0:NT].rearrange("p a (j s) -> p a j s", s=S)
                        t4 = tok[:].rearrange("p a (j s) -> p a j s", s=S)
                        per_batch = tokmax[:].rearrange("p (a j) -> p a j", a=2)
                        wide_max = per_batch.unsqueeze(3).broadcast_to([128, 2, BG, S])
                        V.tensor_reduce(per_batch, v, AX.X, ALU.max).then_inc(s["tok_step"], 1)
                        dve.wait_ge(s["tok_step"], 1)
                        V.tensor_tensor(t4, v, wide_max, ALU.subtract).then_inc(*R.signal_drained(kind))
                        dve.wait_ge(s["tok_exp"], 1)
                        then(V.tensor_reduce(per_batch, t4, AX.X, ALU.add))
                        then(V.reciprocal(tokmax[:], tokmax[:]))
                        then(V.tensor_tensor(tokc[:].rearrange("p a (j s) -> p a j s", s=S), t4, wide_max, ALU.mult))
                    elif kind == "mask":
                        dve.wait_ge(*R.drained(kind))
                        dve.wait_ge(*R.filled("lora"))
                        then(V.tensor_tensor(mask_diff[:], maskT[:, 1, :], maskT[:, 0, :], ALU.subtract))
                        for slot, chosen in enumerate((maskT[:, 0, :], mask_diff[:])):
                            for half in range(2):
                                V.scalar_tensor_tensor(out=lora_in[:, slot, half, :], in0=region[0][:, half, 0:NT], scalar=2.0,
                                                       in1=chosen, op0=ALU.mult, op1=ALU.mult)\
                                    .then_inc(*(R.signal_drained("lora") if half and slot else (s["lora_in"], 1)))
                        for slot in range(2):
                            dve.wait_ge(s["lora_high"], slot + 1)
                            V.tensor_tensor(lora_low[:, slot, :, :], lora_in[:, slot, :, :], lora_high[:, slot, :, :].bitcast(F32), ALU.subtract)\
                                .then_inc(s["lora_low"], 1)
                    elif kind == "gateup" and layer == 0:
                        i, = key
                        dve.wait_ge(s["gate_act"], i + 1)
                    elif kind == "weight":
                        i, = key
                        up = region[i % 2][:, 1, 0:NT]
                        dve.wait_ge(*R.filled(kind, *key))
                        V.tensor_tensor(gact[:, i % 2, :], gact[:, i % 2, :], acc[:, 0:NT], ALU.mult).then_inc(*R.signal_drained(kind, *key))
                        dve.wait_ge(*R.drained(kind, *key))
                        if i >= 2:
                            dve.wait_ge(s["down_done"], i - 1)
                        V.tensor_tensor(hid[:, i % 2, :], gact[:, i % 2, :], up, ALU.mult).then_inc(*R.signal_drained("gateup", i))
                    elif kind == "gateup":
                        m, slot = key
                        M = min(128, HID - m * 128)
                        if slot == 0:
                            dve.wait_ge(s["gate_act"], 2 * m + 1)
                            dve.wait_ge(s["gate_copied"], m + 1)
                            V.tensor_tensor(sact[0:M, 0, :], sact[0:M, 0, :], acc[0:M, 1, 0:NT], ALU.mult)\
                                .then_inc(*R.signal_drained(kind, *key))
                            dve.wait_ge(*R.drained(kind, *key))
                        else:
                            dve.wait_ge(*R.filled(kind, *key))
                            V.tensor_tensor(gate_up[0:M, :, :], gate_up[0:M, :, :], acc[0:M, :, 0:NT], ALU.add)\
                                .then_inc(*R.signal_drained(kind, *key))
                            dve.wait_ge(s["gate_act"], 2 * m + 2)
                            V.tensor_tensor(sact[0:M, 1, :], sact[0:M, 1, :], gate_up[0:M, 1, :], ALU.mult).then_inc(s["gate_up"], 1)
                            dve.wait_ge(s["gate_up"], m + 1)
                        if m >= 2:
                            dve.wait_ge(s["down_done"], m - 1)
                        V.tensor_tensor(hid[0:M, m % 2, slot, :], sact[0:M, slot, :], tokc[0:M, slot, :], ALU.mult)\
                            .then_inc(s["hid_ready"], 1)
                    elif kind == "loradown":
                        dve.wait_ge(s["down_done"], MT)
                        for slot in range(2):
                            V.scalar_tensor_tensor(out=lora_z[:, slot, :], in0=region[3 + 2 * slot][:, 0:NT], scalar=2.0,
                                                   in1=maskT[:, slot, :], op0=ALU.mult, op1=ALU.mult).then_inc(s["lora_z"], 1)
                    elif kind == "out":
                        dve.wait_ge(s["down_done"], E0 + 1 if layer == 0 else MT + 1)
                        for q in range(KT):
                            V.tensor_tensor(x_res[:, q, :], region[(2, (5, 4)[layer])[q]][:, 0:NT], x_res[:, q, :], ALU.add)\
                                .then_inc(s["out_ready"], 1)
        nc.all_engine_barrier(sems_to_clear=group_range)

    with nc.Block() as block:
        @block.sync
        def _(sp):
            sp.wait_ge(tokens_moved, 16 * (G + 1))
    nc.all_engine_barrier(sems_to_clear=range(tokens_moved.num, tokens_moved.num + 1))


def kernel(**inputs):
    import concourse.bacc as bacc
    from concourse.bass_utils import run_bass_kernel_spmd

    def arr(x):
        return np.ascontiguousarray(np.asarray(x))

    x = arr(inputs["x"]).reshape(G, NT, KT, 128).transpose(0, 3, 2, 1)
    d = {"x": np.concatenate([x, np.zeros_like(x[:1])])}
    ctx = arr(inputs["ctx_512"]).reshape(B, LP, LT * DC)
    d["ctx"] = np.concatenate([ctx, np.zeros_like(ctx[:1])])
    d["cosk"], d["sink"], d["cosq"], d["sinq"] = rope_tables()
    d["ident"] = np.eye(128, dtype=np.float32)
    d["tie4"], d["tie8"], d["tie16"] = before_masks(4), before_masks(8), before_masks(16)
    d["bias"] = arr(inputs["L0_ffn_expert_bias"]).reshape(1, E0)
    for n in range(2):
        p = f"L{n}_xattn_"
        flat = lambda v: v.reshape(v.shape[0], -1)
        d[f"wq{n}"] = flat(arr(inputs[p + "Wq"]).reshape(H, HK, D).transpose(1, 0, 2))
        d[f"kcq{n}"] = flat(arr(inputs[p + "w_kc_q"]).transpose(1, 0, 2))
        d[f"kckv{n}"] = flat(arr(inputs[p + "w_kc_kv"]).transpose(1, 0, 2))
        d[f"wo{n}"] = flat(arr(inputs[p + "Wo"]).T.reshape(H, HK, D).transpose(1, 0, 2))
        d[f"wqr{n}"] = flat(arr(inputs[p + "W_qr"]).transpose(2, 0, 1))
        d[f"wkr{n}"] = flat(arr(inputs[p + "W_kr"]).transpose(2, 0, 1))
    d["router0"] = arr(inputs["L0_ffn_gate_weight"]).T
    d["router1"] = arr(inputs["L1_ffn_gate_w"]).T

    def expert(gate, up, down):
        parts = [m.T.reshape(KT, 128, I0).transpose(1, 0, 2).reshape(128, KT * I0) for m in (gate, up)]
        return np.concatenate(parts + [down.T], axis=1)

    q = "L0_ffn_"
    gate, up, down = (arr(inputs[q + f"{m}_proj"]) for m in ("gate", "up", "down"))
    shared = expert(*(arr(inputs[q + f"shared_{m}"]) for m in ("gate", "up", "down")))
    d["experts"] = np.stack([shared] + [expert(gate[e], up[e], down[e]) for e in range(E0)])
    q = "L1_ffn_"
    d["f_up"], d["f_gate"] = arr(inputs[q + "w_up"]).T, arr(inputs[q + "w_gate"]).T
    d["f_down"] = arr(inputs[q + "w_down"]).T
    d["f_upA"], d["f_gateA"] = (arr(inputs[q + m]).reshape(E1 * RANK, D).T for m in ("up_A", "gate_A"))
    d["f_upB"], d["f_gateB"] = (arr(inputs[q + m]).transpose(0, 2, 1).reshape(E1 * RANK, HID) for m in ("up_B", "gate_B"))
    d["f_downA"] = arr(inputs[q + "down_A"]).reshape(E1 * RANK, HID).T
    d["f_downB"] = arr(inputs[q + "down_B"]).transpose(0, 2, 1).reshape(E1 * RANK, D)

    nc = bacc.Bacc("TRN2", target_bir_lowering=False, num_devices=1)
    arrays, aps = {}, {}
    for name, v in d.items():
        arrays["in_" + name] = np.ascontiguousarray(v)
        aps[name] = nc.dram_tensor("in_" + name, v.shape, mybir.dt.from_np(v.dtype), kind="ExternalInput").ap()
    out = nc.dram_tensor("out_x", [G, 128, KT, NT], F32, kind="ExternalOutput").ap()
    x_mid = nc.dram_tensor("x_mid", [G + 1, 128, KT, NT], F32).ap()
    scratch = {name: nc.dram_tensor(name + "_merged", shape, F32).ap() for name, shape in (
        ("w1", [H, 128, KT * DCQ]), ("w2", [H, HALF, 4 * DC]), ("wabs", [H, 128, KT * 2 * DC]), ("wvo", [2, 128, H // 2 * D]))}
    build_program(nc, aps, scratch, out, x_mid)
    r = run_bass_kernel_spmd(nc, [arrays], core_ids=[0])
    y = r.results[0]["out_x"]
    return np.ascontiguousarray(y.transpose(0, 3, 2, 1)).reshape(B, S, D)
```
